# Optimizing a Trainium2 kernel written in Bass

```python
import numpy as np
import jax
import jax.numpy as jnp

def _softmax(x, axis=-1):
    return jax.nn.softmax(x, axis=axis)

def _gelu(x):
    return jax.nn.gelu(x, approximate=True)

def _silu(x):
    return jax.nn.silu(x)

def _sigmoid(x):
    return jax.nn.sigmoid(x)

def _layernorm(x, axis=-1, eps=1e-05):
    m = jnp.mean(x, axis=axis, keepdims=True)
    v = jnp.var(x, axis=axis, keepdims=True)
    return (x - m) / jnp.sqrt(v + eps)

def _scatter_add(tgt, idx, src, axis=0):
    return tgt.at[idx].add(src)

def _segment_sum(src, seg, n):
    return jax.ops.segment_sum(src, seg, n)
kernel_name = 'mk_seq_postln_d2_jaxref_r8_51b4f3'

def setup_inputs(seed: int=0):
    np.random.seed(seed)
    _w = jnp.asarray

    def _L0_attn_setup():
        import jax, jax.numpy as jnp
        import numpy as np
        D_MODEL = 256
        N_HEADS = 16
        HEAD_DIM = D_MODEL // N_HEADS

        def _alibi_slopes(n_heads: int) -> jnp.ndarray:
            start = 2.0 ** (-8.0 / n_heads)
            return jnp.asarray([start * start ** i for i in range(n_heads)], dtype=jnp.float32)
        key = jax.random.key(seed)
        ks = jax.random.split(key, 9)
        B, S, D = (2, 256, D_MODEL)
        scale = 1.0 / np.sqrt(D)
        return {'x': jax.random.normal(ks[0], (B, S, D), dtype=jnp.float32), 'wq': jax.random.normal(ks[1], (D, D), dtype=jnp.float32) * scale, 'bq': jnp.zeros((D,), dtype=jnp.float32), 'wk': jax.random.normal(ks[2], (D, D), dtype=jnp.float32) * scale, 'bk': jnp.zeros((D,), dtype=jnp.float32), 'wv': jax.random.normal(ks[3], (D, D), dtype=jnp.float32) * scale, 'bv': jnp.zeros((D,), dtype=jnp.float32), 'wo': jax.random.normal(ks[4], (D, D), dtype=jnp.float32) * scale, 'bo': jnp.zeros((D,), dtype=jnp.float32)}
    _L0_attn_in = _L0_attn_setup()

    def _L0_ffn_setup():
        import jax, jax.numpy as jnp
        import numpy as np
        B, S, D, F, E, K = (2, 256, 256, 512, 8, 1)

        def _silu_mul(gu):
            g, u = jnp.split(gu, 2, axis=-1)
            return jax.nn.silu(g) * u

        def _moe_forward(hidden_states, router_w, w_gate_up, w_down, shared_gate_up, shared_down, top_k=K):
            b, s, d = hidden_states.shape
            x = hidden_states.reshape(-1, d)
            router_logits = x @ router_w.T
            topk_vals, topk_ids = jax.lax.top_k(router_logits, top_k)
            gate = jax.nn.sigmoid(topk_vals.astype(jnp.float32)).astype(x.dtype)
            xs = (x[:, None, :] * gate[:, :, None]).reshape(-1, d)
            ids_flat = topk_ids.reshape(-1)
            n_experts = w_gate_up.shape[0]

            def body(acc, inp):
                wg, wd, e = inp
                h = _silu_mul(xs @ wg)
                o = h @ wd
                mask = (ids_flat == e)[:, None]
                return (acc + jnp.where(mask, o, jnp.zeros((), o.dtype)), None)
            acc0 = jnp.zeros_like(xs)
            routed, _ = jax.lax.scan(body, acc0, (w_gate_up, w_down, jnp.arange(n_experts)))
            routed = routed.reshape(-1, top_k, d).sum(1)
            shared = _silu_mul(x @ shared_gate_up) @ shared_down
            return (routed + shared).reshape(b, s, d)
        key = jax.random.key(seed)
        ks = jax.random.split(key, 6)
        scale = 0.02
        return {'hidden_states': jax.random.normal(ks[0], (B, S, D), jnp.float32), 'router_w': jax.random.normal(ks[1], (E, D), jnp.float32) * scale, 'w_gate_up': jax.random.normal(ks[2], (E, D, 2 * F), jnp.float32) * scale, 'w_down': jax.random.normal(ks[3], (E, F, D), jnp.float32) * scale, 'shared_gate_up': jax.random.normal(ks[4], (D, 2 * F), jnp.float32) * scale, 'shared_down': jax.random.normal(ks[5], (F, D), jnp.float32) * scale}
    _L0_ffn_in = _L0_ffn_setup()

    def _L1_attn_setup():
        import jax, jax.numpy as jnp
        import numpy as np
        H = 16
        NORM = 16.0
        SCALE = 128.0 ** (-0.5)
        EPS = 1e-05

        def _gla_core(x, Wq, Wk, Wkg1, Wkg2, bkg2, Wv, Wg, bg, Wo):
            B, L, D = x.shape
            q = x @ Wq.T
            k = x @ Wk.T * SCALE
            kg = x @ Wkg1.T @ Wkg2.T + bkg2
            v = x @ Wv.T
            gproj = x @ Wg.T + bg
            dk = q.shape[-1] // H
            dv = D // H
            heads = lambda t, dh: t.reshape(B, L, H, dh).transpose(0, 2, 1, 3)
            qh = heads(q, dk)
            kh = heads(k, dk)
            vh = heads(v, dv)
            gk = jax.nn.log_sigmoid(heads(kg, dk)) / NORM
            tfirst = lambda t: t.transpose(2, 0, 1, 3)

            def step(S, inp):
                qt, kt, vt, gt = inp
                S = S * jnp.exp(gt)[..., None] + kt[..., None] * vt[..., None, :]
                ot = jnp.einsum('bhk,bhkv->bhv', qt, S)
                return (S, ot)
            S0 = jnp.zeros((B, H, dk, dv), x.dtype)
            _, os = jax.lax.scan(step, S0, (tfirst(qh), tfirst(kh), tfirst(vh), tfirst(gk)))
            o = os.transpose(1, 2, 0, 3)
            mu = o.mean(-1, keepdims=True)
            var = ((o - mu) ** 2).mean(-1, keepdims=True)
            o = (o - mu) * jax.lax.rsqrt(var + EPS)
            o = o.transpose(0, 2, 1, 3).reshape(B, L, D)
            return jax.nn.silu(gproj) * o @ Wo.T
        key = jax.random.key(seed)
        ks = jax.random.split(key, 10)
        B, L, D = (2, 256, 256)
        g = lambda k, shape, s: jax.random.normal(k, shape, jnp.float32) * s
        return {'x': g(ks[0], (B, L, D), 1.0), 'Wq': g(ks[1], (128, D), 0.02), 'Wk': g(ks[2], (128, D), 0.02), 'Wkg1': g(ks[3], (16, D), 0.02), 'Wkg2': g(ks[4], (128, 16), 0.05), 'bkg2': jnp.zeros((128,), jnp.float32), 'Wv': g(ks[5], (D, D), 0.02), 'Wg': g(ks[6], (D, D), 0.02), 'bg': jnp.zeros((D,), jnp.float32), 'Wo': g(ks[7], (D, D), 0.02)}
    _L1_attn_in = _L1_attn_setup()

    def _L1_ffn_setup():
        import jax, jax.numpy as jnp
        import numpy as np
        B, S, D = (2, 256, 256)
        H, HD = (16, 128)
        E, K, I = (16, 6, 176)
        SI = 352
        EPS = 1e-06

        def rmsnorm(x, w):
            v = jnp.mean(jnp.square(x), axis=-1, keepdims=True)
            return x * jax.lax.rsqrt(v + EPS) * w
        key = jax.random.key(seed)
        ks = jax.random.split(key, 14)
        s = 0.02
        return {'hidden_states': jax.random.normal(ks[0], (B, S, D), jnp.float32), 'ln1_w': jnp.ones((D,), jnp.float32), 'ln2_w': jnp.ones((D,), jnp.float32), 'wq': jax.random.normal(ks[1], (D, H * HD), jnp.float32) * s, 'wk': jax.random.normal(ks[2], (D, H * HD), jnp.float32) * s, 'wv': jax.random.normal(ks[3], (D, H * HD), jnp.float32) * s, 'wo': jax.random.normal(ks[4], (H * HD, D), jnp.float32) * s, 'gate_w': jax.random.normal(ks[5], (E, D), jnp.float32) * s, 'eg_w': jax.random.normal(ks[6], (E, I, D), jnp.float32) * s, 'eu_w': jax.random.normal(ks[7], (E, I, D), jnp.float32) * s, 'ed_w': jax.random.normal(ks[8], (E, D, I), jnp.float32) * s, 'sg_w': jax.random.normal(ks[9], (SI, D), jnp.float32) * s, 'su_w': jax.random.normal(ks[10], (SI, D), jnp.float32) * s, 'sd_w': jax.random.normal(ks[11], (D, SI), jnp.float32) * s}
    _L1_ffn_in = _L1_ffn_setup()
    _d = {'L0_attn_x': _L0_attn_in['x'], 'L0_attn_wq': _L0_attn_in['wq'], 'L0_attn_bq': _L0_attn_in['bq'], 'L0_attn_wk': _L0_attn_in['wk'], 'L0_attn_bk': _L0_attn_in['bk'], 'L0_attn_wv': _L0_attn_in['wv'], 'L0_attn_bv': _L0_attn_in['bv'], 'L0_attn_wo': _L0_attn_in['wo'], 'L0_attn_bo': _L0_attn_in['bo'], 'L0_ffn_router_w': _L0_ffn_in['router_w'], 'L0_ffn_w_gate_up': _L0_ffn_in['w_gate_up'], 'L0_ffn_w_down': _L0_ffn_in['w_down'], 'L0_ffn_shared_gate_up': _L0_ffn_in['shared_gate_up'], 'L0_ffn_shared_down': _L0_ffn_in['shared_down'], 'L1_attn_Wq': _L1_attn_in['Wq'], 'L1_attn_Wk': _L1_attn_in['Wk'], 'L1_attn_Wkg1': _L1_attn_in['Wkg1'], 'L1_attn_Wkg2': _L1_attn_in['Wkg2'], 'L1_attn_bkg2': _L1_attn_in['bkg2'], 'L1_attn_Wv': _L1_attn_in['Wv'], 'L1_attn_Wg': _L1_attn_in['Wg'], 'L1_attn_bg': _L1_attn_in['bg'], 'L1_attn_Wo': _L1_attn_in['Wo'], 'L1_ffn_ln1_w': _L1_ffn_in['ln1_w'], 'L1_ffn_ln2_w': _L1_ffn_in['ln2_w'], 'L1_ffn_wq': _L1_ffn_in['wq'], 'L1_ffn_wk': _L1_ffn_in['wk'], 'L1_ffn_wv': _L1_ffn_in['wv'], 'L1_ffn_wo': _L1_ffn_in['wo'], 'L1_ffn_gate_w': _L1_ffn_in['gate_w'], 'L1_ffn_eg_w': _L1_ffn_in['eg_w'], 'L1_ffn_eu_w': _L1_ffn_in['eu_w'], 'L1_ffn_ed_w': _L1_ffn_in['ed_w'], 'L1_ffn_sg_w': _L1_ffn_in['sg_w'], 'L1_ffn_su_w': _L1_ffn_in['su_w'], 'L1_ffn_sd_w': _L1_ffn_in['sd_w']}
    _x0 = _d['L0_attn_x']
    _d['L0_attn_x'] = jax.random.normal(jax.random.fold_in(jax.random.key(seed), 1), (2, 512, 256), dtype=_x0.dtype)
    del _x0
    return _d

def reference(L0_attn_x, L0_attn_wq, L0_attn_bq, L0_attn_wk, L0_attn_bk, L0_attn_wv, L0_attn_bv, L0_attn_wo, L0_attn_bo, L0_ffn_router_w, L0_ffn_w_gate_up, L0_ffn_w_down, L0_ffn_shared_gate_up, L0_ffn_shared_down, L1_attn_Wq, L1_attn_Wk, L1_attn_Wkg1, L1_attn_Wkg2, L1_attn_bkg2, L1_attn_Wv, L1_attn_Wg, L1_attn_bg, L1_attn_Wo, L1_ffn_ln1_w, L1_ffn_ln2_w, L1_ffn_wq, L1_ffn_wk, L1_ffn_wv, L1_ffn_wo, L1_ffn_gate_w, L1_ffn_eg_w, L1_ffn_eu_w, L1_ffn_ed_w, L1_ffn_sg_w, L1_ffn_su_w, L1_ffn_sd_w):

    def _L0_attn_ref(x, wq, bq, wk, bk, wv, bv, wo, bo):
        import jax, jax.numpy as jnp
        import numpy as np
        D_MODEL = 256
        N_HEADS = 16
        HEAD_DIM = D_MODEL // N_HEADS

        def _alibi_slopes(n_heads: int) -> jnp.ndarray:
            start = 2.0 ** (-8.0 / n_heads)
            return jnp.asarray([start * start ** i for i in range(n_heads)], dtype=jnp.float32)
        B, S, D = x.shape
        H, hd = (N_HEADS, HEAD_DIM)

        def heads(y):
            return y.reshape(B, S, H, hd).transpose(0, 2, 1, 3)
        q = heads(x @ wq + bq)
        k = heads(x @ wk + bk)
        v = heads(x @ wv + bv)
        scores = jnp.einsum('bhqd,bhkd->bhqk', q, k) / jnp.sqrt(jnp.float32(hd))
        pos = jnp.arange(S)
        rel = pos[None, :] - pos[:, None]
        slopes = _alibi_slopes(H)
        bias = slopes[:, None, None] * rel.astype(jnp.float32)
        causal = jnp.where(rel > 0, -jnp.inf, 0.0).astype(jnp.float32)
        scores = scores + (bias + causal)[None]
        attn = jax.nn.softmax(scores, axis=-1)
        out = jnp.einsum('bhqk,bhkd->bhqd', attn, v)
        out = out.transpose(0, 2, 1, 3).reshape(B, S, D)
        return out @ wo + bo

    def _L0_ffn_ref(hidden_states, router_w, w_gate_up, w_down, shared_gate_up, shared_down):
        import jax, jax.numpy as jnp
        import numpy as np
        B, S, D, F, E, K = (2, 256, 256, 512, 8, 1)

        def _silu_mul(gu):
            g, u = jnp.split(gu, 2, axis=-1)
            return jax.nn.silu(g) * u

        def _moe_forward(hidden_states, router_w, w_gate_up, w_down, shared_gate_up, shared_down, top_k=K):
            b, s, d = hidden_states.shape
            x = hidden_states.reshape(-1, d)
            router_logits = x @ router_w.T
            topk_vals, topk_ids = jax.lax.top_k(router_logits, top_k)
            gate = jax.nn.sigmoid(topk_vals.astype(jnp.float32)).astype(x.dtype)
            xs = (x[:, None, :] * gate[:, :, None]).reshape(-1, d)
            ids_flat = topk_ids.reshape(-1)
            n_experts = w_gate_up.shape[0]

            def body(acc, inp):
                wg, wd, e = inp
                h = _silu_mul(xs @ wg)
                o = h @ wd
                mask = (ids_flat == e)[:, None]
                return (acc + jnp.where(mask, o, jnp.zeros((), o.dtype)), None)
            acc0 = jnp.zeros_like(xs)
            routed, _ = jax.lax.scan(body, acc0, (w_gate_up, w_down, jnp.arange(n_experts)))
            routed = routed.reshape(-1, top_k, d).sum(1)
            shared = _silu_mul(x @ shared_gate_up) @ shared_down
            return (routed + shared).reshape(b, s, d)
        return _moe_forward(hidden_states, router_w, w_gate_up, w_down, shared_gate_up, shared_down)

    def _L1_attn_ref(x, Wq, Wk, Wkg1, Wkg2, bkg2, Wv, Wg, bg, Wo):
        import jax, jax.numpy as jnp
        import numpy as np
        H = 16
        NORM = 16.0
        SCALE = 128.0 ** (-0.5)
        EPS = 1e-05

        def _gla_core(x, Wq, Wk, Wkg1, Wkg2, bkg2, Wv, Wg, bg, Wo):
            B, L, D = x.shape
            q = x @ Wq.T
            k = x @ Wk.T * SCALE
            kg = x @ Wkg1.T @ Wkg2.T + bkg2
            v = x @ Wv.T
            gproj = x @ Wg.T + bg
            dk = q.shape[-1] // H
            dv = D // H
            heads = lambda t, dh: t.reshape(B, L, H, dh).transpose(0, 2, 1, 3)
            qh = heads(q, dk)
            kh = heads(k, dk)
            vh = heads(v, dv)
            gk = jax.nn.log_sigmoid(heads(kg, dk)) / NORM
            tfirst = lambda t: t.transpose(2, 0, 1, 3)

            def step(S, inp):
                qt, kt, vt, gt = inp
                S = S * jnp.exp(gt)[..., None] + kt[..., None] * vt[..., None, :]
                ot = jnp.einsum('bhk,bhkv->bhv', qt, S)
                return (S, ot)
            S0 = jnp.zeros((B, H, dk, dv), x.dtype)
            _, os = jax.lax.scan(step, S0, (tfirst(qh), tfirst(kh), tfirst(vh), tfirst(gk)))
            o = os.transpose(1, 2, 0, 3)
            mu = o.mean(-1, keepdims=True)
            var = ((o - mu) ** 2).mean(-1, keepdims=True)
            o = (o - mu) * jax.lax.rsqrt(var + EPS)
            o = o.transpose(0, 2, 1, 3).reshape(B, L, D)
            return jax.nn.silu(gproj) * o @ Wo.T
        return _gla_core(x, Wq, Wk, Wkg1, Wkg2, bkg2, Wv, Wg, bg, Wo)

    def _L1_ffn_ref(hidden_states, ln1_w, ln2_w, wq, wk, wv, wo, gate_w, eg_w, eu_w, ed_w, sg_w, su_w, sd_w):
        import jax, jax.numpy as jnp
        import numpy as np
        B, S, D = (2, 256, 256)
        H, HD = (16, 128)
        E, K, I = (16, 6, 176)
        SI = 352
        EPS = 1e-06

        def rmsnorm(x, w):
            v = jnp.mean(jnp.square(x), axis=-1, keepdims=True)
            return x * jax.lax.rsqrt(v + EPS) * w
        b, s, d = hidden_states.shape
        x = hidden_states
        h = rmsnorm(x, ln1_w)
        q = (h @ wq).reshape(b, s, H, HD)
        k = (h @ wk).reshape(b, s, H, HD)
        v = (h @ wv).reshape(b, s, H, HD)
        scores = jnp.einsum('bqhd,bkhd->bhqk', q, k) / np.sqrt(HD).astype(np.float32)
        causal = jnp.tril(jnp.ones((s, s), bool))
        scores = jnp.where(causal, scores, jnp.float32(-1000000000.0))
        attn = jax.nn.softmax(scores, axis=-1)
        ao = jnp.einsum('bhqk,bkhd->bqhd', attn, v).reshape(b, s, H * HD) @ wo
        x = x + ao
        h = rmsnorm(x, ln2_w)
        t = h.reshape(-1, d)
        T = t.shape[0]
        logits = t @ gate_w.T
        probs = jax.nn.softmax(logits, axis=-1)
        topv, topi = jax.lax.top_k(probs, K)
        topv = topv / jnp.sum(topv, axis=-1, keepdims=True)
        cw = jnp.zeros((T, E), t.dtype).at[jnp.arange(T)[:, None], topi].add(topv)
        g = jnp.einsum('td,eid->eti', t, eg_w)
        u = jnp.einsum('td,eid->eti', t, eu_w)
        hh = jax.nn.silu(g) * u
        routed = jnp.einsum('eti,edi,te->td', hh, ed_w, cw)
        shared = jax.nn.silu(t @ sg_w.T) * (t @ su_w.T) @ sd_w.T
        out = x + (routed + shared).reshape(b, s, d)
        return out
    x = L0_attn_x
    x = _layernorm(x + _L0_attn_ref(x, L0_attn_wq, L0_attn_bq, L0_attn_wk, L0_attn_bk, L0_attn_wv, L0_attn_bv, L0_attn_wo, L0_attn_bo), axis=-1)
    x = _layernorm(x + _L0_ffn_ref(x, L0_ffn_router_w, L0_ffn_w_gate_up, L0_ffn_w_down, L0_ffn_shared_gate_up, L0_ffn_shared_down), axis=-1)
    x = _layernorm(x + _L1_attn_ref(x, L1_attn_Wq, L1_attn_Wk, L1_attn_Wkg1, L1_attn_Wkg2, L1_attn_bkg2, L1_attn_Wv, L1_attn_Wg, L1_attn_bg, L1_attn_Wo), axis=-1)
    x = _layernorm(x + _L1_ffn_ref(x, L1_ffn_ln1_w, L1_ffn_ln2_w, L1_ffn_wq, L1_ffn_wk, L1_ffn_wv, L1_ffn_wo, L1_ffn_gate_w, L1_ffn_eg_w, L1_ffn_eu_w, L1_ffn_ed_w, L1_ffn_sg_w, L1_ffn_su_w, L1_ffn_sd_w), axis=-1)
    return x

_drawn_inputs = setup_inputs


def setup_inputs(seed=0):
    import zlib

    import numpy as np

    out = dict(_drawn_inputs(seed))
    spreads = {'L0_attn_bq': (0.0, 0.349),
     'L0_attn_bk': (0.0, 2.0),
     'L0_attn_bv': (0.0, 0.1),
     'L0_attn_bo': (0.0, 0.1),
     'L1_attn_bkg2': (0.0, 0.8),
     'L1_attn_bg': (0.0, 0.467),
     'L1_ffn_ln1_w': (1.0, 0.6),
     'L1_ffn_ln2_w': (1.0, 0.6)}
    factors = {'L0_ffn_router_w': 6.542,
     'L0_ffn_w_gate_up': 6.083,
     'L0_ffn_w_down': 6.086,
     'L1_attn_Wkg1': 8.0,
     'L1_attn_Wkg2': 8.0,
     'L1_ffn_wq': 8.0,
     'L1_ffn_wk': 8.0,
     'L1_ffn_gate_w': 8.0,
     'L1_ffn_eg_w': 8.0,
     'L1_ffn_eu_w': 8.0,
     'L1_ffn_ed_w': 8.0,
     'L1_ffn_sg_w': 5.426,
     'L1_ffn_su_w': 5.342,
     'L1_ffn_sd_w': 5.304,
     'L0_ffn_shared_gate_up': 2.765,
     'L0_ffn_shared_down': 2.8}
    for name, (base, spread) in spreads.items():
        noise = np.random.default_rng([zlib.crc32(name.encode()), seed]).standard_normal(out[name].shape)
        drawn = base * np.exp(spread * noise) if base else spread * noise
        out[name] = jnp.asarray(drawn.astype(out[name].dtype))
    for name, factor in factors.items():
        out[name] = (out[name] * factor).astype(out[name].dtype)
    return out
```

```python
from contextlib import ExitStack

import concourse.bass as bass
from concourse import mybir

F32 = mybir.dt.float32
BF16 = mybir.dt.bfloat16
I32 = mybir.dt.int32
U32 = mybir.dt.uint32
ALU = mybir.AluOpType
ACT = mybir.ActivationFunctionType
AX_X = mybir.AxisListType.X

P = 128
B, S, D = 2, 512, 256
T = B * S
TT = T // P
KD = D // P
QT = S // P
H = 16
HD0 = D // H
LN_EPS = 1e-5
E0, F0 = 8, 512
W0_SLOT = KD * 2 * F0 + F0 // P * D
N_TILES0 = T // P + E0 - 1
RC_WORDS = 384
CH = 64
NCH = T // CH
KSCALE = 128.0 ** -0.5
QSCALE1 = 128.0 ** -0.5
RMS_EPS = 1e-6
E1, K1, F1, FS1 = 16, 6, 176, 352
W1_SLOT = KD * 2 * F1 + 2 * D
W1_SHARED = E1 * W1_SLOT
W1_END = W1_SHARED + KD * 2 * FS1 + 3 * D
ARENA = 43008


def wait(eng, sem, value):
    if isinstance(value, int) and value <= 0:
        return
    eng.wait_ge(sem, value)


class Chain:

    def __init__(self, eng, sem, at=0):
        self.eng, self.sem, self.n = eng, sem, at

    def step(self, ins):
        ins.then_inc(self.sem, 1)
        self.n = self.n + 1
        return self.n

    def wait(self, n=None):
        self.eng.wait_ge(self.sem, self.n if n is None else n)


def program(nc, io, out):
    with ExitStack() as ctx:
        sems = {}

        def sem(name):
            if name not in sems:
                sems[name] = ctx.enter_context(nc.semaphore(name))
            return sems[name]

        def sb(name, shape, dt=F32):
            return ctx.enter_context(nc.sbuf_tensor(name, shape, dt))

        PS = ctx.enter_context(nc.psum_tensor("PS", [P, 8, 512], F32))

        X = sb("X", [P, TT, D])
        XT = sb("XT", [P, KD, T])
        R = sb("R", [P, TT, D])
        ident = sb("ident", [P, P])
        identb = sb("identb", [P, P], BF16)
        maskb = sb("maskb", [P, P], BF16)
        bn = sb("bn", [P, TT, 6])
        mv = sb("mv", [P, TT, 2])
        sd = sb("sd", [P, TT])
        rstd = sb("rstd", [P, TT])
        var = sb("var", [P, TT])
        eps5 = sb("eps5", [P, 1])
        negmax = sb("negmax", [P, 8])
        rowsum = sb("rowsum", [P, 8])
        rinv = sb("rinv", [P, 8])
        biasrow = sb("biasrow", [P, 2, D])
        bqk0 = sb("bqk0", [P, 2, KD])

        A = sb("A", [P, ARENA])

        def cut(at, words, dt=F32):
            v = A[:, at:at + words]
            return v if dt == F32 else v.bitcast(dt)

        W_A = [cut(18432 + 512 * n, 512).rearrange("p (k n) -> p k n", k=KD) for n in range(4)]
        QK6 = [cut(21504 + 8192 * w, 8192, BF16) for w in range(2)]
        V0 = cut(37888, TT * D).rearrange("p (t n) -> p t n", t=TT)
        PB = cut(39936, 4 * 512).rearrange("p (i n) -> p i n", i=4)
        PTS = cut(41984, 2 * 512).rearrange("p (i n) -> p i n", i=2)
        q32 = cut(39936, 1024).rearrange("p (i n) -> p i n", i=2)
        rest = cut(40960, 512)
        parts = cut(41472, 1536, BF16).rearrange("p (i q n) -> p i q n", i=2, q=3)
        AO = R
        scratch = nc.dram_tensor("qk_parts", (2, 3, D, T), BF16, kind="Internal").ap()

        def W_B(slot):
            at = W0_SLOT * slot
            return (cut(at, KD * 2 * F0).rearrange("p (k n) -> p k n", k=KD),
                    cut(at + KD * 2 * F0, F0 // P * D).rearrange("p (j n) -> p j n", j=F0 // P))

        XS0 = R
        XI = cut(37888, 2 * D).rearrange("p (i n) -> p i n", i=2)
        XIT = cut(38400, 2 * D).rearrange("p (i k t) -> p i k t", i=2, k=KD)
        YO = cut(38912, 2 * D).rearrange("p (i n) -> p i n", i=2)
        SG = cut(39936, 2 * F0).rearrange("p (i n) -> p i n", i=2)
        HB = cut(40960, 2 * F0).rearrange("p (i n) -> p i n", i=2)
        HBT = cut(41984, 2 * F0).rearrange("p (i n) -> p i n", i=2)
        YS = cut(0, TT * D).rearrange("p (t n) -> p t n", t=TT)
        YR = cut(TT * D, TT * D).rearrange("p (t n) -> p t n", t=TT)
        rw0 = sb("rw0", [P, KD, E0])
        rc = sb("rc", [P, RC_WORDS])
        iota_e = rc[:, 0:16]
        tile_sizes = rc[:, 16:24]
        iota_j = rc[:, 24:24 + N_TILES0]
        before = rc[:, 128:256]
        ones = rc[:, 256:384]
        lg = sb("lg", [P, TT, E0])
        mx = sb("mx", [P, TT, 8])
        ix = sb("ix", [P, TT, 8], U32)
        ixf = sb("ixf", [P, TT])
        oh = sb("oh", [P, TT, E0])
        en = sb("en", [P, TT])
        gate = sb("gate", [P, TT])
        cmp0 = sb("cmp0", [P, E0, 8])
        nt = sb("nt", [P, E0])
        incl = sb("incl", [P, E0])
        first_row = sb("first_row", [P, E0])
        base = sb("base", [P, TT, E0])
        slotf = sb("slotf", [P, TT])
        slot = sb("slot", [P, TT], U32)
        cmpj = sb("cmpj", [1, N_TILES0, E0])
        texf = sb("texf", [1, TT + N_TILES0])
        tile_at = sb("tile_at", [1, TT + N_TILES0], I32)
        zeros = sb("zeros", [P, D])
        at_c = 27648
        wq1, wk1 = (cut(at_c + 256 * n, 256).rearrange("p (k n) -> p k n", k=KD) for n in range(2))
        wkg1 = cut(at_c + 512, 32).rearrange("p (k n) -> p k n", k=KD)
        wkg2 = cut(at_c + 544, P)[0:16, :]
        wvg = cut(at_c + 672, 1024).rearrange("p (k n) -> p k n", k=KD)
        wo1 = cut(at_c + 1696, 512).rearrange("p (k n) -> p k n", k=KD)
        run = cut(at_c + 2208, T)
        own_head = cut(at_c + 3232, H)
        own_block = cut(at_c + 3248, D)
        causal = cut(at_c + 3504, CH)
        bkg = cut(at_c + 3568, 1)
        ga, gb, gc_, gd, ge = (cut(21632 + T * n, T) for n in range(5))
        QX = [ga, gb]
        ATS = [gd, ge]
        kg1 = cut(31728, T)[0:16, :]
        e1, e2, e3, e4 = (cut(32752 + T * n, T) for n in range(4))
        V1 = cut(36848, TT * D).rearrange("p (t n) -> p t n", t=TT)
        GP = cut(38896, TT * D).rearrange("p (t n) -> p t n", t=TT)
        KH = cut(40944, TT * P).rearrange("p (t n) -> p t n", t=TT)
        ST = [cut(41968 + D * n, D) for n in range(2)]
        UP = cut(42480, D)
        YT = cut(21632, KD * T).rearrange("p (k t) -> p k t", k=KD)
        dec = sb("dec", [P, NCH])
        gsum = sb("gsum", [P, TT * H])
        gvar = sb("gvar", [P, TT * H])
        WD = [cut(21632 + 768 * n, 768).rearrange("p (w k n) -> p w k n", w=3, k=KD) for n in range(2)]
        QKT = [cut(23168 + 2048 * n, 2048).rearrange("p (w t) -> p w t", w=2) for n in range(2)]
        VH = [cut(27264 + 1024 * n, 1024).rearrange("p (t d) -> p t d", t=TT) for n in range(2)]
        AOT = cut(29312, 2048).rearrange("p (g t) -> p g t", g=2)
        WOP = cut(31360, 512).rearrange("p (g n) -> p g n", g=2)
        PB1 = cut(31872, 2048).rearrange("p (i n) -> p i n", i=4)
        PTS1 = cut(33920, 1024).rearrange("p (i n) -> p i n", i=2)
        HN = cut(34944, TT * D).rearrange("p (t n) -> p t n", t=TT)
        sq = cut(36992, D)
        ssq = sb("ssq", [P, TT])
        eps6 = sb("eps6", [P, 1])
        SG1 = cut(21632, 2 * FS1).rearrange("p (i n) -> p i n", i=2)
        HB1 = cut(22336, 2 * FS1).rearrange("p (i n) -> p i n", i=2)
        HBT1 = cut(23040, 2 * 384).rearrange("p (i n) -> p i n", i=2)
        rw1 = cut(37248, KD * E1).rearrange("p (k e) -> p k e", k=KD)
        lg1 = cut(37280, TT * E1).rearrange("p (t e) -> p t e", t=TT)
        cw = cut(37408, TT * E1).rearrange("p (t e) -> p t e", t=TT)
        OH1 = cut(38176, TT * K1 * E1).rearrange("p (t k e) -> p t k e", t=TT, k=K1)
        zsum = sb("zsum", [P, TT])
        ixf1 = sb("ixf1", [P, TT, 8])
        xs_rows = nc.dram_tensor("xs_rows", ((TT + N_TILES0) * P, D), F32, kind="Internal").ap()
        y_rows = nc.dram_tensor("y_rows", ((TT + N_TILES0) * P, D), F32, kind="Internal").ap()

        block = ctx.enter_context(nc.Block())

        Q_SLOT = [0, 0, 1, 1, 0, 2]
        K_SLOT = [0, 1, 0, 1, 2, 0]

        def dve_norm(dve, own, phase):
            own.wait()
            for t in range(TT):
                own.step(nc.vector.bn_stats(bn[:, t, :], R[:, t, :]))
            own.wait()
            for t in range(TT):
                ins = nc.vector.bn_aggr(mv[:, t, :], bn[:, t, :])
                own.step(ins)
            own.wait()
            nc.vector.tensor_copy(var[:, :], mv[:, :, 1]).then_inc(sem("var_ready"), 1)
            dve.wait_ge(sem("sd_ready"), phase)
            own.step(nc.vector.reciprocal(rstd[:, :], sd[:, :]))
            own.wait()
            for t in range(TT):
                nc.vector.tensor_scalar(X[:, t, :], R[:, t, :], mv[:, t, 0:1], rstd[:, t:t + 1],
                                        ALU.subtract, ALU.mult).then_inc(sem("x_ready"), 1)

        def act_sqrt(act, phase):
            if phase == 1:
                act.wait_ge(sem("eps_set"), 2)
            act.wait_ge(sem("var_ready"), phase)
            nc.scalar.activation(sd[:, :], var[:, :], ACT.Sqrt, bias=eps5[:, :]).then_inc(sem("sd_ready"), 1)

        N_IT = TT + N_TILES0

        def stream(eng, step, n_items=N_IT, peel=4):
            for n in range(peel):
                step(n, n % 2, n // 2)
            pairs = (n_items - peel - 2) // 2
            with eng.Fori(peel // 2, peel // 2 + pairs) as j:
                for p in range(2):
                    step(2 * j + p, p, j)
            for n in range(peel + 2 * pairs, n_items):
                step(n, n % 2, n // 2)

        def sp_b(sp):
            sp.wait_ge(sem("x_ready"), TT)
            sp.dma_start(xs_rows[0:T, :].rearrange("(t p) n -> p t n", p=P), X[:, :, :]).then_inc(sem("own_rows"), 16)
            sp.wait_ge(sem("own_rows"), 16)

            def load(n, p):
                at = n * P if isinstance(n, int) else sp.snap(n * P)
                wait(sp, sem("b_xturned"), n - 1)
                sp.dma_start(XI[:, p, :], xs_rows[bass.ds(at, P), :]).then_inc(sem(f"xi_in{p}"), 16)

            def store(n, p):
                at = n * P if isinstance(n, int) else sp.snap(n * P)
                sp.wait_ge(sem("b_y"), n + 1)
                sp.dma_start(y_rows[bass.ds(at, P), :], YO[:, p, :]).then_inc(sem(f"y_stored{p}"), 16)

            def step(n, p, half):
                if isinstance(n, int) and n + 2 == TT:
                    sp.wait_ge(sem("rows_scattered"), 16 * TT)
                if not (isinstance(n, int) and n + 2 >= N_IT):
                    load(n + 2, p)
                if not (isinstance(n, int) and n < 2):
                    store(n - 2, p)

            load(0, 0)
            load(1, 1)
            stream(sp, step, peel=TT)
            store(N_IT - 2, N_IT % 2)
            store(N_IT - 1, 1 - N_IT % 2)
            sp.wait_ge(sem("y_stored0"), 16 * (N_IT // 2 + 1))
            sp.wait_ge(sem("y_stored1"), 16 * (N_IT // 2))
            sp.wait_ge(sem("b_down"), N_IT)
            sp.dma_start(YS, y_rows[0:T, :].rearrange("(t p) n -> p t n", p=P)).then_inc(sem("ys_in"), 16)
            sp_c(sp)

        def pool_b(pool):
            pool.wait_ge(sem("slots"), 1)
            pool.wait_ge(sem("gated"), 1)
            for t in range(TT):
                nc.gpsimd.indirect_dma_start(
                    out=xs_rows[:, :], out_offset=bass.IndirectOffsetOnAxis(ap=slot[:, t:t + 1], axis=0),
                    in_=XS0[:, t, :], in_offset=None).then_inc(sem("rows_scattered"), 16)
            pool.wait_ge(sem("y_stored0"), 16 * (N_IT // 2 + 1))
            pool.wait_ge(sem("y_stored1"), 16 * (N_IT // 2))
            pool.wait_ge(sem("b_down"), N_IT)
            for t in range(TT):
                nc.gpsimd.indirect_dma_start(
                    out=YR[:, t, :], out_offset=None, in_=y_rows[:, :],
                    in_offset=bass.IndirectOffsetOnAxis(ap=slot[:, t:t + 1], axis=0))\
                    .then_inc(sem("yr_in"), 16)
            pool_c(pool)

        def pe_b(pe):
            pe_transpose_tokens(pe, X, "x_ready", lambda t: t + 1, "x1_turned")
            pe.wait_ge(sem("route_in"), 32)
            pe.wait_ge(sem("xT1"), 2)
            for t in range(TT):
                for k in range(KD):
                    ins = nc.tensor.matmul(PS[:, 4, t * E0:(t + 1) * E0], XT[:, k, t * P:(t + 1) * P], rw0[:, k, :],
                                           start=k == 0, stop=k == KD - 1)
            ins.then_inc(sem("logits"), 1)
            pe.wait_ge(sem("onehot"), 1)
            for t in range(TT):
                for s in range(t + 1):
                    nc.tensor.matmul(PS[:, 5, t * E0:(t + 1) * E0], (before if s == t else ones), oh[:, s, :],
                                     start=s == 0, stop=s == t)
            for s in range(TT):
                ins = nc.tensor.matmul(PS[:, 5, TT * E0:(TT + 1) * E0], ones, oh[:, s, :],
                                       start=s == 0, stop=s == TT - 1)
            ins.then_inc(sem("ranks"), 1)

            def turn_x(n, p, half):
                pe.wait_ge(sem(f"xi_in{p}"), 16 * half + 16)
                wait(pe, sem("b_xit"), n)
                for k in range(KD):
                    ins = nc.tensor.transpose(PS[:, 6, k * P:(k + 1) * P],
                                              XI[:, p, k * P:(k + 1) * P], ident[:, :])
                ins.then_inc(sem("b_xturned"), 1)

            def gate_up(n, p, half):
                pe.wait_ge(sem("b_xit"), n + 1)
                at = pe.value_load(tile_at[0:1, bass.ds(n, 1)], min_val=0, max_val=W0_SLOT * E0)
                for g in range(2):
                    wait(pe, sem("b_silu" if g == 0 else "b_h"), n - 1)
                    for k in range(KD):
                        ins = nc.tensor.matmul(PS[:, 2 * g + p, :], XIT[:, p, k, :],
                                               A[:, bass.ds(at + (k * 2 + g) * F0, F0)],
                                               start=k == 0, stop=k == KD - 1)
                    ins.then_inc(sem("b_gate" if g == 0 else "b_up"), 1)

            def turn_h(n, p, half):
                pe.wait_ge(sem("b_h"), n + 1)
                wait(pe, sem("b_ht"), n - 1)
                for j in range(F0 // P):
                    ins = nc.tensor.transpose(PS[:, 4 + p, j * P:(j + 1) * P], HB[:, p, j * P:(j + 1) * P], ident[:, :])
                ins.then_inc(sem("b_hturned"), 1)

            def down(n, p, half):
                pe.wait_ge(sem("b_ht"), n + 1)
                wait(pe, sem("b_y"), n)
                at = pe.value_load(tile_at[0:1, bass.ds(n, 1)], min_val=0, max_val=W0_SLOT * E0)
                for j in range(F0 // P):
                    ins = nc.tensor.matmul(PS[:, 7, 0:D], HBT[:, p, j * P:(j + 1) * P],
                                           A[:, bass.ds(at + KD * 2 * F0 + j * D, D)],
                                           start=j == 0, stop=j == F0 // P - 1)
                ins.then_inc(sem("b_down"), 1)

            pe.wait_ge(sem("tile_table"), 1)
            pe.wait_ge(sem("w_shared0"), 32)
            pe.wait_ge(sem("w_routed0"), 32 * E0)
            turn_x(0, 0, 0)

            def step(n, p, half):
                gate_up(n, p, half)
                if not (isinstance(n, int) and n < 2):
                    down(n - 2, p, half - 1)
                if not (isinstance(n, int) and n < 1):
                    turn_h(n - 1, 1 - p, half - (1 - p))
                if not (isinstance(n, int) and n == N_IT - 1):
                    turn_x(n + 1, 1 - p, half + p)

            stream(pe, step)
            n = N_IT - 1
            down(n - 1, 1 - n % 2, (n - 1) // 2)
            turn_h(n, n % 2, n // 2)
            down(n, n % 2, n // 2)
            pe_c(pe)

        def act_xT(act, turned, copied):
            for c in range(B):
                act.wait_ge(sem(turned), c + 1)
                nc.scalar.activation(XT[:, :, c * S:(c + 1) * S], PS[:, 2 * c:2 * c + 2, :], ACT.Copy)\
                    .then_inc(sem(copied), 1)

        def act_b(act):
            act.wait_ge(sem("a_proj"), TT)
            act_xT(act, "x1_turned", "xT1")
            act.wait_ge(sem("top1"), 1)
            nc.scalar.activation(en[:, :], mx[:, :, 0], ACT.Exp, scale=-1.0).then_inc(sem("exp_neg"), 1)

            def copy_ht(n, p, half):
                act.wait_ge(sem("b_hturned"), n + 1)
                wait(act, sem("b_down"), n - 1)
                nc.scalar.activation(HBT[:, p, :], PS[:, 4 + p, :], ACT.Copy).then_inc(sem("b_ht"), 1)

            def step(n, p, half):
                act.wait_ge(sem("b_gate"), n + 1)
                wait(act, sem("b_h"), n - 1)
                nc.scalar.activation(SG[:, p, :], PS[:, p, :], ACT.Silu).then_inc(sem("b_silu"), 1)
                if not (isinstance(n, int) and n < 1):
                    copy_ht(n - 1, 1 - p, half)

            stream(act, step)
            copy_ht(N_IT - 1, (N_IT - 1) % 2, 0)
            act_sqrt(act, 2)
            act_c(act)

        def dve_b(dve, own):
            dve.wait_ge(sem("logits"), 1)
            own.step(nc.vector.tensor_copy(lg[:, :, :], PS[:, 4, 0:TT * E0].rearrange("p (t e) -> p t e", e=E0)))
            own.wait()
            for t in range(TT):
                own.step(nc.vector.max(mx[:, t, :], lg[:, t, :]))
            own.wait()
            for t in range(TT):
                own.step(nc.vector.max_index(ix[:, t, :], mx[:, t, :], lg[:, t, :]))
            own.wait()
            nc.vector.tensor_copy(ixf[:, :], ix[:, :, 0]).then_inc(sem("top1"), 1)
            dve.wait_ge(sem("top1"), 1)
            dve.wait_ge(sem("route_in"), 32)
            nc.vector.tensor_tensor(oh[:, :, :], ixf[:, :].unsqueeze(2).to_broadcast([P, TT, E0]),
                                    iota_e[:, 0:E0].unsqueeze(1).to_broadcast([P, TT, E0]), ALU.is_equal)\
                .then_inc(sem("onehot"), 1)
            dve.wait_ge(sem("exp_neg"), 1)
            own.step(nc.vector.tensor_scalar(en[:, :], en[:, :], 1.0, None, ALU.add))
            own.wait()
            own.step(nc.vector.reciprocal(gate[:, :], en[:, :]))
            own.wait()
            nc.vector.tensor_tensor(XS0[:, :, :], X[:, :, :], gate[:, :].unsqueeze(2).to_broadcast([P, TT, D]),
                                    ALU.mult).then_inc(sem("gated"), 1)
            dve.wait_ge(sem("ranks"), 1)
            own.step(nc.vector.tensor_tensor(
                cmp0[:, :, :], PS[:, 5, TT * E0:(TT + 1) * E0].unsqueeze(2).to_broadcast([P, E0, 8]),
                tile_sizes.unsqueeze(1).to_broadcast([P, E0, 8]), ALU.is_gt))
            own.wait()
            own.step(nc.vector.tensor_reduce(nt[:, :], cmp0[:, :, :], AX_X, ALU.add))
            own.wait()
            own.step(nc.vector.tensor_tensor_scan(incl[:, :], ones[:, 0:E0], nt[:, :], 0.0, ALU.mult, ALU.add))
            own.wait()
            own.step(nc.vector.tensor_tensor(first_row[:, :], incl[:, :], nt[:, :], ALU.subtract))
            own.step(nc.vector.tensor_tensor(
                cmpj[:, :, :], incl[0:1, :].unsqueeze(1).to_broadcast([1, N_TILES0, E0]),
                iota_j[0:1, :].unsqueeze(2).to_broadcast([1, N_TILES0, E0]), ALU.is_le))
            own.step(nc.vector.memset(texf[:, 0:TT], 0.0))
            own.wait()
            own.step(nc.vector.tensor_scalar(first_row[:, :], first_row[:, :], float(P), float(T), ALU.mult, ALU.add))
            own.step(nc.vector.tensor_reduce(texf[:, TT:], cmpj[:, :, :], AX_X, ALU.add))
            own.wait()
            own.step(nc.vector.tensor_tensor(
                base[:, :, :], PS[:, 5, 0:TT * E0].rearrange("p (t e) -> p t e", e=E0),
                first_row[:, :].unsqueeze(1).to_broadcast([P, TT, E0]), ALU.add))
            own.step(nc.vector.tensor_scalar(texf[:, TT:], texf[:, TT:], float(E0 - 1), 1.0, ALU.min, ALU.add))
            own.wait()
            own.step(nc.vector.tensor_tensor(base[:, :, :], base[:, :, :], oh[:, :, :], ALU.mult))
            nc.vector.tensor_scalar(tile_at[:, :], texf[:, :], float(W0_SLOT), None, ALU.mult)\
                .then_inc(sem("tile_table"), 1)
            own.wait()
            own.step(nc.vector.tensor_reduce(slotf[:, :], base[:, :, :], AX_X, ALU.add))
            own.wait()
            nc.vector.tensor_copy(slot[:, :], slotf[:, :]).then_inc(sem("slots"), 1)

            def copy_xit(n, p, half):
                dve.wait_ge(sem("b_xturned"), n + 1)
                wait(dve, sem("b_up"), n - 1)
                nc.vector.tensor_copy(XIT[:, p, :, :], PS[:, 6, 0:D].rearrange("p (k t) -> p k t", k=KD))\
                    .then_inc(sem("b_xit"), 1)

            def copy_y(n, p, half):
                dve.wait_ge(sem("b_down"), n + 1)
                wait(dve, sem(f"y_stored{p}"), 16 * half)
                nc.vector.tensor_copy(YO[:, p, :], PS[:, 7, 0:D]).then_inc(sem("b_y"), 1)

            copy_xit(0, 0, 0)

            def step(n, p, half):
                dve.wait_ge(sem("b_silu"), n + 1)
                dve.wait_ge(sem("b_up"), n + 1)
                wait(dve, sem("b_hturned"), n - 1)
                nc.vector.tensor_tensor(HB[:, p, :], SG[:, p, :], PS[:, 2 + p, :], ALU.mult).then_inc(sem("b_h"), 1)
                if not (isinstance(n, int) and n == N_IT - 1):
                    copy_xit(n + 1, 1 - p, half + p)
                if not (isinstance(n, int) and n < 2):
                    copy_y(n - 2, p, half - 1)

            stream(dve, step)
            n = N_IT - 1
            copy_y(n - 1, (n - 1) % 2, (n - 1) // 2)
            copy_y(n, n % 2, n // 2)
            dve.wait_ge(sem("ys_in"), 16)
            own.step(nc.vector.tensor_tensor(R[:, :, :], X[:, :, :], YS, ALU.add))
            own.wait()
            dve.wait_ge(sem("yr_in"), 16 * TT)
            own.step(nc.vector.tensor_tensor(R[:, :, :], R[:, :, :], YR, ALU.add))
            dve_norm(dve, own, 2)
            dve_c(dve, own)

        def sp_c(sp):
            loads = [(wq1, io["L1_attn_WqT"].rearrange("(k p) n -> p k n", p=P)),
                     (wk1, io["L1_attn_WkT"].rearrange("(k p) n -> p k n", p=P)),
                     (wkg1, io["L1_attn_Wkg1T"].rearrange("(k p) n -> p k n", p=P)),
                     (wkg2, io["L1_attn_Wkg2T"]),
                     (wvg, io["L1_attn_WvgT"].rearrange("(k p) n -> p k n", p=P)),
                     (wo1, io["L1_attn_WoT"].rearrange("(k p) n -> p k n", p=P)),
                     (run, io["run"].rearrange("(o n) -> o n", o=1).to_broadcast([P, T])),
                     (cut(at_c + 3232, H + D + CH), io["gla_consts"]),
                     (bkg, io["L1_attn_bkg2"].rearrange("(p o) -> p o", o=1)),
                     (biasrow[:, 0, :], io["L1_attn_bg"].rearrange("(o n) -> o n", o=1).to_broadcast([P, D]))]
            for dst, src in loads:
                sp.dma_start(dst, src).then_inc(sem("c_in"), 16)
            sp_d(sp)

        C_LOADS = 16 * 10

        def pool_c(pool):
            pool.wait_ge(sem("c_in"), C_LOADS)
            for c in range(NCH):
                if c == 0:
                    pool.wait_ge(sem("c_qt"), 1)
                if c >= 2:
                    pool.wait_ge(sem("c_at"), c - 1)
                nc.gpsimd.tensor_tensor(QX[c % 2].rearrange("p (h t) -> p h t", h=H),
                                        e1[:, c * CH:(c + 1) * CH].unsqueeze(1).to_broadcast([P, H, CH]),
                                        own_head.unsqueeze(2).to_broadcast([P, H, CH]), ALU.mult)\
                    .then_inc(sem("c_qx"), 1)

        def pe_c(pe):
            pe_transpose_tokens(pe, X, "x_ready", lambda t: TT + t + 1, "x2_turned")
            pe.wait_ge(sem("c_in"), C_LOADS)
            pe.wait_ge(sem("xT2"), 2)
            for c in range(B):
                for k in range(KD):
                    ins = nc.tensor.matmul(PS[0:16, 6 + c, :], wkg1[:, k, :], XT[:, k, c * S:(c + 1) * S],
                                           start=k == 0, stop=k == KD - 1)
                ins.then_inc(sem("c_kg1"), 1)
            for w, wt in ((0, wq1), (1, wk1)):
                for c in range(B):
                    for k in range(KD):
                        ins = nc.tensor.matmul(PS[:, 2 * w + c, :], wt[:, k, :], XT[:, k, c * S:(c + 1) * S],
                                               start=k == 0, stop=k == KD - 1)
            ins.then_inc(sem("c_qk"), 1)
            for c in range(B):
                pe.wait_ge(sem("c_kg1s"), c + 1)
                nc.tensor.matmul(PS[:, 4 + c, :], wkg2, kg1[:, c * S:(c + 1) * S], start=True, stop=True)\
                    .then_inc(sem("c_kg"), 1)
            for t in range(TT):
                if t >= 2:
                    pe.wait_ge(sem("c_v"), t - 1)
                    pe.wait_ge(sem("c_vgb"), t - 1)
                for k in range(KD):
                    ins = nc.tensor.matmul(PS[:, 6 + t % 2, :], XT[:, k, t * P:(t + 1) * P], wvg[:, k, :],
                                           start=k == 0, stop=k == KD - 1)
                ins.then_inc(sem("c_vg"), 1)
            pe.wait_ge(sem("c_kh"), 1)
            for t in range(TT):
                ins = nc.tensor.transpose(PS[:, 4 + t // 4, t % 4 * P:(t % 4 + 1) * P], e4[:, t * P:(t + 1) * P],
                                          ident[:, :])
                if t % 4 == 3:
                    ins.then_inc(sem("c_khturned"), 1)
            pe.wait_ge(sem("c_khs"), 2)
            pe.wait_ge(sem("c_v"), TT)
            pe.wait_ge(sem("c_vgb"), TT)

            pe.wait_ge(sem("c_qk_used"), 1)

            def chunk_scores(c):
                pb = c % 2 * CH
                pe.wait_ge(sem("c_qx"), c + 1)
                if c >= 2:
                    pe.wait_ge(sem("c_masked"), c - 1)
                for half in range(2):
                    ins = nc.tensor.matmul(PS[pb:pb + CH, 2 * (c % 2) + half, :], e2[:, c * CH:(c + 1) * CH],
                                           QX[c % 2][:, half * 512:(half + 1) * 512], start=True, stop=True)
                ins.then_inc(sem("c_at"), 1)

            chunk_scores(0)
            for c in range(NCH):
                pb, t, first = c % 2 * CH, c // 2, c % (NCH // B) == 0
                if c + 1 < NCH:
                    chunk_scores(c + 1)
                if c >= 2:
                    pe.wait_ge(sem("c_state"), c - 1)
                nc.tensor.matmul(PS[:, 6 + c % 2, 0:D], KH[pb:pb + CH, t, :], V1[pb:pb + CH, t, :],
                                 start=True, stop=True).then_inc(sem("c_update"), 1)
                if c >= 2:
                    pe.wait_ge(sem("c_copied"), c - 1)
                if not first:
                    pe.wait_ge(sem("c_state"), c)
                    nc.tensor.matmul(PS[pb:pb + CH, 4 + c % 2, 0:D], e3[:, c * CH:(c + 1) * CH], ST[(c - 1) % 2],
                                     start=True, stop=False, skip_group_check=True)
                pe.wait_ge(sem("c_masked"), c + 1)
                for h in range(H):
                    ins = nc.tensor.matmul(PS[pb:pb + CH, 4 + c % 2, h * 16:(h + 1) * 16],
                                           ATS[t % 2][pb:pb + CH, h * CH:(h + 1) * CH],
                                           V1[pb:pb + CH, t, h * 16:(h + 1) * 16],
                                           start=first, stop=True, skip_group_check=True)
                ins.then_inc(sem("c_o"), 1)
            pe_transpose_tokens(pe, R, "c_gated", lambda t: 1, "c_yturned")
            pe.wait_ge(sem("c_yT"), 2)
            for t in range(TT):
                for k in range(KD):
                    ins = nc.tensor.matmul(PS[:, 4 + t // 2, t % 2 * D:(t % 2 + 1) * D], YT[:, k, t * P:(t + 1) * P],
                                           wo1[:, k, :], start=k == 0, stop=k == KD - 1)
                ins.then_inc(sem("c_proj"), 1)
            pe_d(pe)

        def act_c(act):
            act_xT(act, "x2_turned", "xT2")
            for c in range(B):
                act.wait_ge(sem("c_kg1"), c + 1)
                nc.scalar.activation(kg1[:, c * S:(c + 1) * S], PS[0:16, 6 + c, :], ACT.Copy)\
                    .then_inc(sem("c_kg1s"), 1)
            act.wait_ge(sem("c_kg"), 2)
            act.wait_ge(sem("c_in"), C_LOADS)
            z = PS[:, 4:6, :].rearrange("p c t -> p (c t)")
            own = Chain(act, sem("act_own"))
            own.step(nc.scalar.activation(ga, z, ACT.Abs, bias=bkg))
            own.wait()
            own.step(nc.scalar.activation(gb, ga, ACT.Exp, scale=-1.0))
            own.wait()
            nc.scalar.activation(ga, gb, ACT.Ln, bias=1.0).then_inc(sem("c_ln"), 1)
            for t in range(TT):
                act.wait_ge(sem("c_vgb"), t + 1)
                nc.scalar.activation(V1[:, t, :], PS[:, 6 + t % 2, 0:D], ACT.Copy).then_inc(sem("c_v"), 1)
            act.wait_ge(sem("c_d"), 1)
            nc.scalar.activation(e1, gd, ACT.Exp, scale=1.0 / 16).then_inc(sem("c_e"), 1)
            nc.scalar.activation(e2, gd, ACT.Exp, scale=-1.0 / 16).then_inc(sem("c_e"), 1)
            nc.scalar.activation(e3, gc_, ACT.Exp, scale=1.0 / 16).then_inc(sem("c_e"), 1)
            nc.scalar.activation(e4, ge, ACT.Exp, scale=1.0 / 16).then_inc(sem("c_e"), 1)
            nc.scalar.activation(dec[:, :], gc_.rearrange("p (c t) -> p c t", c=NCH)[:, :, CH - 1], ACT.Exp,
                                 scale=1.0 / 16).then_inc(sem("c_e"), 1)
            for u in range(2):
                act.wait_ge(sem("c_khturned"), u + 1)
                nc.scalar.activation(KH[:, 4 * u:4 * u + 4, :], PS[:, 4 + u, :].rearrange("p (t n) -> p t n", t=4),
                                     ACT.Copy).then_inc(sem("c_khs"), 1)
            own.step(nc.scalar.activation(GP, GP, ACT.Silu))
            silu_done = own.n
            for c in range(NCH):
                pb, t = c % 2 * CH, c // 2
                act.wait_ge(sem("c_o"), c + 1)
                nc.scalar.activation(R[pb:pb + CH, t, :], PS[pb:pb + CH, 4 + c % 2, 0:D], ACT.Copy)\
                    .then_inc(sem("c_copied"), 1)
            act.wait_ge(sem("c_centred"), 1)
            act.wait_ge(sem("act_own"), silu_done)
            nc.scalar.activation(V1, R[:, :, :], ACT.Square).then_inc(sem("c_squared"), 1)
            act.wait_ge(sem("c_gvar"), 1)
            nc.scalar.activation(gvar[:, :], gvar[:, :], ACT.Sqrt, bias=eps5[:, :]).then_inc(sem("c_gsd"), 1)
            for c in range(B):
                act.wait_ge(sem("c_yturned"), c + 1)
                nc.scalar.activation(YT[:, :, c * S:(c + 1) * S], PS[:, 2 * c:2 * c + 2, :], ACT.Copy)\
                    .then_inc(sem("c_yT"), 1)
            act_sqrt(act, 3)
            act_d(act)

        def dve_c(dve, own):
            dve.wait_ge(sem("c_kg"), 2)
            dve.wait_ge(sem("c_in"), C_LOADS)
            z = PS[:, 4:6, :].rearrange("p c t -> p (c t)")
            dve.wait_ge(sem("c_ln"), 1)
            own.step(nc.vector.tensor_scalar(gb, z, bkg, 0.0, ALU.add, ALU.min))
            own.wait()
            own.step(nc.vector.tensor_tensor(gb, gb, ga, ALU.subtract))
            own.wait()
            own.step(nc.vector.tensor_tensor_scan(gc_, run, gb, 0.0, ALU.mult, ALU.add))
            own.wait()
            g3 = gc_.rearrange("p (c t) -> p c t", c=NCH)
            own.step(nc.vector.tensor_tensor(gd.rearrange("p (c t) -> p c t", c=NCH), g3,
                                             g3[:, :, CH // 2 - 1:CH // 2].to_broadcast([P, NCH, CH]), ALU.subtract))
            nc.vector.tensor_tensor(ge.rearrange("p (c t) -> p c t", c=NCH),
                                    g3[:, :, CH - 1:CH].to_broadcast([P, NCH, CH]), g3, ALU.subtract)\
                .then_inc(sem("c_d"), 1)
            for t in range(TT):
                dve.wait_ge(sem("c_vg"), t + 1)
                nc.vector.tensor_tensor(GP[:, t, :], PS[:, 6 + t % 2, D:2 * D], biasrow[:, 0, :], ALU.add)\
                    .then_inc(sem("c_vgb"), 1)
            q = PS[:, 0:2, :].rearrange("p c t -> p (c t)")
            kk = PS[:, 2:4, :].rearrange("p c t -> p (c t)")
            dve.wait_ge(sem("c_qk"), 1)
            dve.wait_ge(sem("c_e"), 5)
            nc.vector.tensor_tensor(e1, q, e1, ALU.mult).then_inc(sem("c_qt"), 1)
            nc.vector.scalar_tensor_tensor(e4, kk, KSCALE, e4, ALU.mult, ALU.mult).then_inc(sem("c_kh"), 1)
            own.step(nc.vector.scalar_tensor_tensor(e2, kk, KSCALE, e2, ALU.mult, ALU.mult))
            own.wait()
            nc.vector.tensor_tensor(e3, q, e3, ALU.mult).then_inc(sem("c_qk_used"), 1)
            for c in range(NCH):
                pb, t, first = c % 2 * CH, c // 2, c % (NCH // B) == 0
                dve.wait_ge(sem("c_at"), c + 1)
                if c >= 4:
                    dve.wait_ge(sem("c_o"), c - 3)
                nc.vector.tensor_tensor(ATS[t % 2][pb:pb + CH, :].rearrange("p (h t) -> p h t", h=H),
                                        PS[pb:pb + CH, 2 * (c % 2):2 * (c % 2) + 2, :]
                                        .rearrange("p a (h t) -> p (a h) t", t=CH),
                                        causal[pb:pb + CH, :].unsqueeze(1).to_broadcast([CH, H, CH]),
                                        ALU.mult).then_inc(sem("c_masked"), 1)
                dve.wait_ge(sem("c_update"), c + 1)
                if c >= 2:
                    dve.wait_ge(sem("c_o"), c)
                if c >= 1:
                    dve.wait_ge(sem("c_state"), c)
                if first:
                    nc.vector.tensor_tensor(ST[c % 2], PS[:, 6 + c % 2, 0:D], own_block, ALU.mult)\
                        .then_inc(sem("c_state"), 1)
                else:
                    own.step(nc.vector.tensor_tensor(UP, PS[:, 6 + c % 2, 0:D], own_block, ALU.mult))
                    own.wait()
                    nc.vector.scalar_tensor_tensor(ST[c % 2], ST[(c - 1) % 2], dec[:, c:c + 1], UP,
                                                   ALU.mult, ALU.add).then_inc(sem("c_state"), 1)
            dve.wait_ge(sem("c_copied"), NCH)
            o4 = R[:, :, :].rearrange("p t (h d) -> p (t h) d", h=H)

            def by_head(v):
                return v.unsqueeze(2).to_broadcast([P, TT * H, D // H])

            own.step(nc.vector.tensor_reduce(gsum[:, :], o4, AX_X, ALU.add))
            own.wait()
            own.step(nc.vector.tensor_scalar(gsum[:, :], gsum[:, :], 1.0 / (D // H), None, ALU.mult))
            own.wait()
            nc.vector.tensor_tensor(o4, o4, by_head(gsum[:, :]), ALU.subtract).then_inc(sem("c_centred"), 1)
            dve.wait_ge(sem("c_squared"), 1)
            own.step(nc.vector.tensor_reduce(gvar[:, :], V1.rearrange("p t (h d) -> p (t h) d", h=H), AX_X, ALU.add))
            own.wait()
            nc.vector.tensor_scalar(gvar[:, :], gvar[:, :], 1.0 / (D // H), None, ALU.mult).then_inc(sem("c_gvar"), 1)
            dve.wait_ge(sem("c_gsd"), 1)
            own.step(nc.vector.reciprocal(gsum[:, :], gvar[:, :]))
            own.wait()
            own.step(nc.vector.tensor_tensor(o4, o4, by_head(gsum[:, :]), ALU.mult))
            own.wait()
            nc.vector.tensor_tensor(R[:, :, :], R[:, :, :], GP, ALU.mult).then_inc(sem("c_gated"), 1)
            for u in range(4):
                dve.wait_ge(sem("c_proj"), 2 * u + 2)
                own.step(nc.vector.tensor_tensor(
                    R[:, 2 * u:2 * u + 2, :], PS[:, 4 + u, :].rearrange("p (t n) -> p t n", t=2),
                    X[:, 2 * u:2 * u + 2, :], ALU.add))
            dve_norm(dve, own, 3)
            dve_d(dve, own)

        def sp_d(sp):
            sp.wait_ge(sem("x_ready"), 2 * TT)
            sp.dma_start(A[:, 0:W1_SHARED].rearrange("p (e n) -> p e n", e=E1), io["w_experts1"])\
                .then_inc(sem("w_experts1"), 16)
            sp.dma_start(A[:, W1_SHARED:W1_SHARED + KD * 2 * FS1], io["w_shared_gu1"]).then_inc(sem("w_experts1"), 16)
            sp.dma_start(A[:, W1_SHARED + KD * 2 * FS1:W1_END], io["w_shared_dn1"]).then_inc(sem("w_experts1"), 16)
            sp.wait_ge(sem("c_proj"), TT)

            def load_head(g, p):
                if not isinstance(g, int):
                    g = sp.snap(g)
                wait(sp, sem("d_pieced"), 8 * g - 8)
                sp.dma_start(WD[p].rearrange("p w k n -> p (w k n)"),
                             io["w_qkv1"][bass.ds(g, 1), :, :].rearrange("g p n -> p (g n)"))\
                    .then_inc(sem(f"wd_in{p}"), 16)

            def load_wo(pair):
                if not isinstance(pair, int):
                    pair = sp.snap(pair)
                wait(sp, sem("d_wo"), 8 * pair)
                sp.dma_start(WOP.rearrange("p g n -> p (g n)"),
                             io["w_o1"][bass.ds(pair, 1), :, :].rearrange("g p n -> p (g n)"))\
                    .then_inc(sem("wo_in"), 16)

            load_head(0, 0)
            load_head(1, 1)
            for src, dst in (("L1_ffn_ln1_w", 0), ("L1_ffn_ln2_w", 1)):
                sp.dma_start(biasrow[:, dst, :], io[src].rearrange("(o n) -> o n", o=1).to_broadcast([P, D]))\
                    .then_inc(sem("ln_w_in"), 16)
            load_head(2, 0)
            load_head(3, 1)
            load_wo(0)
            with sp.Fori(1, H // 2 - 1) as pair:
                load_head(2 * pair + 2, 0)
                load_head(2 * pair + 3, 1)
                load_wo(pair)
            load_wo(H // 2 - 1)
            sp.dma_start(rw1, io["gate_w1"].rearrange("(k p) e -> p k e", p=P)).then_inc(sem("rw1_in"), 16)
            sp.wait_ge(sem("x_ready"), 4 * TT)
            sp.dma_start(out.rearrange("(t p) n -> p t n", p=P), X[:, :, :]).then_inc(sem("out_done"), 16)
            sp.wait_ge(sem("out_done"), 16)

        def pe_d(pe):
            pe_transpose_tokens(pe, HN, "hn_ready", lambda t: t + 1, "hn_turned")

            def project(g, n, p):
                if n == 0:
                    pe.wait_ge(sem(f"wd_in{p}"), (g - p) * 8 + 16)
                wait(pe, sem("d_piece"), 8 * g + n)
                if n < 4:
                    w, c = n // 2, n % 2
                    for k in range(KD):
                        ins = nc.tensor.matmul(PS[:, 6, :], WD[p][:, w, k, :], XT[:, k, c * S:(c + 1) * S],
                                               start=k == 0, stop=k == KD - 1)
                else:
                    for t in (2 * n - 8, 2 * n - 7):
                        for k in range(KD):
                            ins = nc.tensor.matmul(PS[:, 6, t % 2 * P:(t % 2 + 1) * P], XT[:, k, t * P:(t + 1) * P],
                                                   WD[p][:, 2, k, :], start=k == 0, stop=k == KD - 1)
                ins.then_inc(sem("d_pieced"), 1)

            def scores(N, g, n, p):
                b, i = n // 4, n % 4
                if n % 4 == 0:
                    pe.wait_ge(sem("d_piece"), 8 * g + 4)
                wait(pe, sem("d_exp"), N - 1)
                w = (i + 1) * P
                nc.tensor.matmul(PS[:, n % 2, 0:w], QKT[p][:, 0, b * S + i * P:b * S + w],
                                 QKT[p][:, 1, b * S:b * S + w], start=True, stop=False)
                nc.tensor.matmul(PS[:, n % 2, i * P:w], identb[:, :], maskb[:, :], start=False, stop=True)\
                    .then_inc(sem("d_scores"), 1)

            def turn(N, n):
                pe.wait_ge(sem("d_norm"), N + 1)
                wait(pe, sem("d_pt"), N - 1)
                for j in range(n % 4 + 1):
                    ins = nc.tensor.transpose(PS[:, 2 + n % 2, j * P:(j + 1) * P], PB1[:, n % 4, j * P:(j + 1) * P],
                                              ident[:, :])
                ins.then_inc(sem("d_turned"), 1)

            def values(N, g, n, p):
                b, i = n // 4, n % 4
                pe.wait_ge(sem("d_pt"), N + 1)
                if i == 0:
                    pe.wait_ge(sem("d_piece"), 8 * g + 8)
                    wait(pe, sem("d_aot"), 2 * g + b - 1)
                for j in range(i + 1):
                    ins = nc.tensor.matmul(PS[:, 4 + b, i * P:(i + 1) * P], VH[p][:, 4 * b + j, :],
                                           PTS1[:, n % 2, j * P:(j + 1) * P], start=j == 0, stop=j == i)
                ins.then_inc(sem("d_values"), 1)

            def project_out(pair, t):
                if t == 0:
                    pe.wait_ge(sem("wo_in"), 16 * pair + 16)
                if t % 4 == 0:
                    pe.wait_ge(sem("d_aot"), 4 * pair + 3 + t // 4)
                pe.wait_ge(sem("d_acc"), 8 * pair + t + 8)
                for g in range(2):
                    ins = nc.tensor.matmul(PS[:, 7, 0:D], AOT[:, g, t * P:(t + 1) * P], WOP[:, g, :],
                                           start=g == 0, stop=g == 1)
                ins.then_inc(sem("d_wo"), 1)

            pe.wait_ge(sem("xT3"), 2)
            for n in range(8):
                project(0, n, 0)
            scores(0, 0, 0, 0)

            def pair_steps(pair, first=False, last=False):
                for m in range(16):
                    N, p, n = 16 * pair + m, m // 8, m % 8
                    g = 2 * pair + p
                    if not (last and m == 15):
                        scores(N + 1, g + (n == 7), (n + 1) % 8, (m + 1) // 8 % 2)
                    if not (last and p == 1):
                        project(g + 1, n, 1 - p)
                    turn(N, n)
                    if m > 0:
                        values(N - 1, g - (n == 0), (n - 1) % 8, (m - 1) // 8)
                    elif not first:
                        values(N - 1, g - 1, 7, 1)
                    if m < 8 and not first:
                        project_out(pair - 1, m)

            pair_steps(0, first=True)
            with pe.Fori(1, H // 2 - 1) as pair:
                pair_steps(pair)
            pair_steps(H // 2 - 1, last=True)
            values(8 * H - 1, H - 1, 7, 1)
            for t in range(TT):
                project_out(H // 2 - 1, t)
            pe_e(pe)

        def act_rms(act, src, phase):
            for t in range(TT):
                if t > 0:
                    act.wait_ge(sem("squares"), TT * (phase - 1) + t)
                nc.scalar.activation(sq, src[:, t, :], ACT.Square, accum_out=ssq[:, t:t + 1])\
                    .then_inc(sem("squares"), 1)
            act.wait_ge(sem("squares"), TT * phase)
            nc.scalar.activation(sd[:, :], ssq[:, :], ACT.Sqrt, bias=eps6[:, :], scale=1.0 / D)\
                .then_inc(sem("rms_ready"), 1)

        def dve_rms(dve, own, src, phase):
            dve.wait_ge(sem("rms_ready"), phase)
            own.step(nc.vector.reciprocal(rstd[:, :], sd[:, :]))
            own.wait()
            dve.wait_ge(sem("ln_w_in"), 32)
            for t in range(TT):
                nc.vector.scalar_tensor_tensor(HN[:, t, :], src[:, t, :], rstd[:, t:t + 1], biasrow[:, phase - 1, :],
                                               ALU.mult, ALU.mult).then_inc(sem("hn_ready"), 1)

        def act_d(act):
            act.wait_ge(sem("x_ready"), 3 * TT)
            act.wait_ge(sem("eps_set"), 2)
            act_rms(act, X, 1)
            act_xT(act, "hn_turned", "xT3")

            def copy_piece(g, n, p):
                act.wait_ge(sem("d_pieced"), 8 * g + n + 1)
                wait(act, sem("d_values"), 8 * g - 8)
                if n < 4:
                    w, c = n // 2, n % 2
                    ins = nc.scalar.activation(QKT[p][:, w, c * S:(c + 1) * S], PS[:, 6, :], ACT.Copy,
                                               scale=QSCALE1 if w == 0 else 1.0)
                else:
                    ins = nc.scalar.activation(VH[p][:, 2 * n - 8:2 * n - 6, :],
                                               PS[:, 6, 0:2 * P].rearrange("p (t d) -> p t d", t=2), ACT.Copy)
                ins.then_inc(sem("d_piece"), 1)

            def exps(N, n):
                act.wait_ge(sem("d_max"), N + 1)
                wait(act, sem("d_turned"), N - 3)
                i = n % 4
                nc.scalar.activation(PB1[:, i, 0:(i + 1) * P], PS[:, n % 2, 0:(i + 1) * P], ACT.Exp,
                                     bias=negmax[:, n:n + 1], accum_out=rowsum[:, n:n + 1]).then_inc(sem("d_exp"), 1)

            def copy_out(pair, unit):
                p, b = unit // 2, unit % 2
                act.wait_ge(sem("d_values"), 16 * pair + 4 * unit + 4)
                wait(act, sem("d_wo"), 8 * (pair - 1) + 4 * b + 4)
                nc.scalar.activation(AOT[:, p, b * S:(b + 1) * S], PS[:, 4 + b, :], ACT.Copy).then_inc(sem("d_aot"), 1)

            for n in range(8):
                copy_piece(0, n, 0)
            exps(0, 0)

            def pair_steps(pair, first=False, last=False):
                for m in range(16):
                    N, p, n = 16 * pair + m, m // 8, m % 8
                    if not (last and m == 15):
                        exps(N + 1, (n + 1) % 8)
                    if not (last and p == 1):
                        copy_piece(2 * pair + p + 1, n, 1 - p)
                    if m % 4 == 0:
                        if m > 0:
                            copy_out(pair, m // 4 - 1)
                        elif not first:
                            copy_out(pair - 1, 3)

            pair_steps(0, first=True)
            with act.Fori(1, H // 2 - 1) as pair:
                pair_steps(pair)
            pair_steps(H // 2 - 1, last=True)
            copy_out(H // 2 - 1, 3)
            act_e(act)

        def dve_d(dve, own):
            dve_rms(dve, own, X, 1)
            for t in range(TT):
                nc.vector.tensor_copy(R[:, t, :], X[:, t, :]).then_inc(sem("d_acc"), 1)

            def maxes(N, n):
                dve.wait_ge(sem("d_scores"), N + 1)
                wait(dve, sem("d_exp"), N - 7)
                i = n % 4
                nc.vector.tensor_reduce(negmax[:, n:n + 1], PS[:, n % 2, 0:(i + 1) * P], AX_X, ALU.max,
                                        negate=True).then_inc(sem("d_max"), 1)

            def normalise(N, n):
                i = n % 4
                dve.wait_ge(sem("d_exp"), N + 1)
                nc.vector.reciprocal(rinv[:, n:n + 1], rowsum[:, n:n + 1]).then_inc(sem("d_rinv"), 1)
                dve.wait_ge(sem("d_rinv"), N + 1)
                nc.vector.tensor_scalar(PB1[:, i, 0:(i + 1) * P], PB1[:, i, 0:(i + 1) * P], rinv[:, n:n + 1], None,
                                        ALU.mult).then_inc(sem("d_norm"), 1)

            def copy_pt(N, n):
                dve.wait_ge(sem("d_turned"), N + 1)
                wait(dve, sem("d_values"), N - 1)
                w = (n % 4 + 1) * P
                nc.vector.tensor_copy(PTS1[:, n % 2, 0:w], PS[:, 2 + n % 2, 0:w]).then_inc(sem("d_pt"), 1)

            def accumulate(pair, t):
                dve.wait_ge(sem("d_wo"), 8 * pair + t + 1)
                dve.wait_ge(sem("d_acc"), 8 * pair + t + 1)
                nc.vector.tensor_tensor(R[:, t, :], R[:, t, :], PS[:, 7, 0:D], ALU.add).then_inc(sem("d_acc"), 1)

            maxes(0, 0)

            def pair_steps(pair, first=False, last=False):
                for m in range(16):
                    N, n = 16 * pair + m, m % 8
                    normalise(N, n)
                    if not (last and m == 15):
                        maxes(N + 1, (n + 1) % 8)
                    copy_pt(N, n)
                    if 0 < m <= 8 and not first:
                        accumulate(pair - 1, m - 1)

            pair_steps(0, first=True)
            with dve.Fori(1, H // 2 - 1) as pair:
                pair_steps(pair)
            pair_steps(H // 2 - 1, last=True)
            for t in range(TT):
                accumulate(H // 2 - 1, t)
            dve_e(dve, own)

        def act_e(act):
            act.wait_ge(sem("d_acc"), 4 * H + TT)
            act_rms(act, R, 2)
            act_xT(act, "h2_turned", "xT4")
            for t in range(TT):
                act.wait_ge(sem("e_max"), 1)
                nc.scalar.activation(cw[:, t, :], lg1[:, t, :], ACT.Exp, bias=negmax[:, t:t + 1],
                                     accum_out=zsum[:, t:t + 1]).then_inc(sem("e_exp"), 1)

            def silu(N, p, f):
                act.wait_ge(sem("e_gu"), N + 1)
                wait(act, sem("e_h"), N - 1)
                nc.scalar.activation(SG1[:, p, 0:f], PS[:, p, 0:f], ACT.Silu).then_inc(sem("e_silu"), 1)

            def copy_ht(N, p, rows, n):
                act.wait_ge(sem("e_hturned"), N + 1)
                wait(act, sem("e_down"), N - 1)
                nc.scalar.activation(HBT1[0:rows, p, 0:n], PS[0:rows, 4 + p, 0:n], ACT.Copy).then_inc(sem("e_ht"), 1)

            def shared(t):
                silu(t, t % 2, FS1)
                if t > 0:
                    shared_ht(t - 1)

            def shared_ht(t):
                p = t % 2
                act.wait_ge(sem("e_hturned"), t + 1)
                wait(act, sem("e_down"), t - 1)
                nc.scalar.activation(HBT1[:, p, 0:256], PS[:, 4 + p, 0:256], ACT.Copy)
                nc.scalar.activation(HBT1[0:96, p, 256:384], PS[0:96, 4 + p, 256:384], ACT.Copy)\
                    .then_inc(sem("e_ht"), 1)

            for t in range(TT):
                shared(t)

            def expert(e, first=False):
                for t in range(TT):
                    N = TT * (e + 1) + t
                    silu(N, t % 2, F1)
                    if first and t == 0:
                        shared_ht(TT - 1)
                    else:
                        copy_ht(N - 1, (t - 1) % 2, F1 // 2, 2 * P)

            expert(0, first=True)
            with act.Fori(1, E1) as e:
                expert(e)
            copy_ht(TT * (E1 + 1) - 1, 1, F1 // 2, 2 * P)
            act_sqrt(act, 4)

        def pe_e(pe):
            pe_transpose_tokens(pe, HN, "hn_ready", lambda t: TT + t + 1, "h2_turned")
            pe.wait_ge(sem("rw1_in"), 16)
            pe.wait_ge(sem("xT4"), 2)
            for t in range(TT):
                for k in range(KD):
                    ins = nc.tensor.matmul(PS[:, 7, t * E1:(t + 1) * E1], XT[:, k, t * P:(t + 1) * P], rw1[:, k, :],
                                           start=k == 0, stop=k == KD - 1)
            ins.then_inc(sem("e_logits"), 1)
            pe.wait_ge(sem("w_experts1"), 48)

            def down(N, t, chunks, at, p):
                pe.wait_ge(sem("e_ht"), N + 1)
                wait(pe, sem("e_acc"), N)
                for j, (rows, c) in enumerate(chunks):
                    ins = nc.tensor.matmul(PS[:, 6, 0:D], HBT1[0:rows, p, c:c + P], A[0:rows, bass.ds(at + j * D, D)],
                                           start=j == 0, stop=j == len(chunks) - 1)
                ins.then_inc(sem("e_down"), 1)

            def turn_h(N, chunks, width, p):
                pe.wait_ge(sem("e_h"), N + 1)
                wait(pe, sem("e_ht"), N - 1)
                for j, (rows, c) in enumerate(chunks):
                    ins = nc.tensor.transpose(PS[0:rows, 4 + p, c:c + P], HB1[:, p, j * width:j * width + rows],
                                              ident[:, :])
                ins.then_inc(sem("e_hturned"), 1)

            SH = [(P, 0), (P, P), (96, 2 * P)]
            EX = [(F1 // 2, 0), (F1 // 2, P)]

            def shared_gate_up(t):
                for g in range(2):
                    wait(pe, sem("e_silu" if g == 0 else "e_h"), t - 1)
                    for k in range(KD):
                        ins = nc.tensor.matmul(PS[:, 2 * g + t % 2, 0:FS1], XT[:, k, t * P:(t + 1) * P],
                                               A[:, bass.ds(W1_SHARED + (2 * k + g) * FS1, FS1)],
                                               start=k == 0, stop=k == KD - 1)
                ins.then_inc(sem("e_gu"), 1)

            sh_dn = W1_SHARED + KD * 2 * FS1
            for t in range(TT):
                shared_gate_up(t)
                if t >= 2:
                    down(t - 2, t - 2, SH, sh_dn, t % 2)
                if t >= 1:
                    turn_h(t - 1, SH, P, (t - 1) % 2)

            def gate_up(N, t, at):
                wait(pe, sem("e_h"), N - 1)
                for k in range(KD):
                    ins = nc.tensor.matmul(PS[:, t % 2, 0:2 * F1], XT[:, k, t * P:(t + 1) * P],
                                           A[:, bass.ds(at + k * 2 * F1, 2 * F1)], start=k == 0, stop=k == KD - 1)
                ins.then_inc(sem("e_gu"), 1)

            def expert(e, first=False):
                at = e * W1_SLOT
                if not isinstance(e, int):
                    at = pe.snap(at)
                for t in range(TT):
                    N = TT * (e + 1) + t
                    gate_up(N, t, at)
                    if first and t < 2:
                        down(N - 2, TT - 2 + t, SH, sh_dn, t % 2)
                    else:
                        down(N - 2, t, EX, at + KD * 2 * F1 - (W1_SLOT if t < 2 else 0), t % 2)
                    if first and t < 1:
                        turn_h(N - 1, SH, P, 1)
                    else:
                        turn_h(N - 1, EX, F1 // 2, (t - 1) % 2)

            expert(0, first=True)
            with pe.Fori(1, E1) as e:
                expert(e)
            N = TT * (E1 + 1)
            last_dn = (E1 - 1) * W1_SLOT + KD * 2 * F1
            down(N - 2, 0, EX, last_dn, 0)
            turn_h(N - 1, EX, F1 // 2, 1)
            down(N - 1, 1, EX, last_dn, 1)

        def dve_e(dve, own):
            dve_rms(dve, own, R, 2)
            dve.wait_ge(sem("e_logits"), 1)
            own.step(nc.vector.tensor_copy(lg1, PS[:, 7, 0:TT * E1].rearrange("p (t e) -> p t e", e=E1)))
            own.wait()
            nc.vector.tensor_reduce(negmax[:, :], lg1, AX_X, ALU.max, negate=True).then_inc(sem("e_max"), 1)
            dve.wait_ge(sem("e_exp"), TT)
            own.step(nc.vector.reciprocal(rinv[:, :], zsum[:, :]))
            own.wait()
            own.step(nc.vector.tensor_tensor(lg1, cw, rinv[:, :].unsqueeze(2).to_broadcast([P, TT, E1]), ALU.mult))
            own.wait()
            for t in range(TT):
                own.step(nc.vector.max(mx[:, t, :], lg1[:, t, :]))
            own.wait()
            for t in range(TT):
                own.step(nc.vector.max_index(ix[:, t, :], mx[:, t, :], lg1[:, t, :]))
            own.step(nc.vector.tensor_reduce(zsum[:, :], mx[:, :, 0:K1], AX_X, ALU.add))
            own.wait()
            own.step(nc.vector.tensor_copy(ixf1[:, :, :], ix[:, :, :]))
            own.step(nc.vector.reciprocal(rinv[:, :], zsum[:, :]))
            own.wait()
            own.step(nc.vector.tensor_tensor(mx[:, :, :], mx[:, :, :], rinv[:, :].unsqueeze(2)
                                             .to_broadcast([P, TT, 8]), ALU.mult))
            own.wait()
            for t in range(TT):
                own.step(nc.vector.tensor_tensor(
                    OH1[:, t, :, :], ixf1[:, t, 0:K1].unsqueeze(2).to_broadcast([P, K1, E1]),
                    iota_e.unsqueeze(1).to_broadcast([P, K1, E1]), ALU.is_equal))
            own.wait()
            for t in range(TT):
                own.step(nc.vector.tensor_tensor(OH1[:, t, :, :], OH1[:, t, :, :],
                                                 mx[:, t, 0:K1].unsqueeze(2).to_broadcast([P, K1, E1]), ALU.mult))
            own.wait()
            own.step(nc.vector.tensor_reduce(cw, OH1.rearrange("p t k e -> p t e k"), AX_X, ALU.add))
            own.wait()

            def hidden(N, p, f, up_bank, up_at):
                dve.wait_ge(sem("e_silu"), N + 1)
                wait(dve, sem("e_hturned"), N - 1)
                nc.vector.tensor_tensor(HB1[:, p, 0:f], SG1[:, p, 0:f], PS[:, up_bank, up_at:up_at + f], ALU.mult)\
                    .then_inc(sem("e_h"), 1)

            def add_shared(t):
                dve.wait_ge(sem("e_down"), t + 1)
                nc.vector.tensor_tensor(R[:, t, :], R[:, t, :], PS[:, 6, 0:D], ALU.add).then_inc(sem("e_acc"), 1)

            def add_expert(N, t, e):
                dve.wait_ge(sem("e_down"), N + 1)
                dve.wait_ge(sem("e_acc"), N - 7)
                at = 37408 + t * E1 + e
                nc.vector.scalar_tensor_tensor(R[:, t, :], PS[:, 6, 0:D], A[:, bass.ds(at, 1)], R[:, t, :],
                                               ALU.mult, ALU.add).then_inc(sem("e_acc"), 1)

            for t in range(TT):
                hidden(t, t % 2, FS1, 2 + t % 2, 0)
                if t >= 2:
                    add_shared(t - 2)

            def expert(e, first=False):
                for t in range(TT):
                    N = TT * (e + 1) + t
                    hidden(N, t % 2, F1, t % 2, F1)
                    if first and t < 2:
                        add_shared(TT - 2 + t)
                    else:
                        add_expert(N - 2, (t - 2) % TT, e - (1 if t < 2 else 0))

            expert(0, first=True)
            with dve.Fori(1, E1) as e:
                expert(e)
            N = TT * (E1 + 1)
            add_expert(N - 2, TT - 2, E1 - 1)
            add_expert(N - 1, TT - 1, E1 - 1)
            dve.wait_ge(sem("e_acc"), N)
            own.step(nc.vector.tensor_tensor(R[:, :, :], R[:, :, :], X[:, :, :], ALU.add))
            dve_norm(dve, own, 4)

        @block.sync
        def _(sp):
            sp.dma_start(W_A[0], io["L0_attn_wq"].rearrange("(k p) n -> p k n", p=P)).then_inc(sem("w_qk0"), 16)
            sp.dma_start(XT[:, :, :], io["xT"].rearrange("(k p) t -> p k t", p=P)).then_inc(sem("xT_in"), 16)
            sp.dma_start(W_A[1], io["L0_attn_wk"].rearrange("(k p) n -> p k n", p=P)).then_inc(sem("w_qk0"), 16)
            for c in range(B):
                for w, src in ((0, io["q_bias_rows"]), (1, io["k_bias_rows"])):
                    dst = QK6[w].rearrange("p (h t) -> p h t", h=H)[96:P, :, c * S:(c + 1) * S]
                    sp.dma_start(dst, src.rearrange("h r t -> r h t")).then_inc(sem("bias_rows_in"), 16)
            for n in range(8):
                c, w, j = n // 4, n // 2 % 2, n % 2
                sp.wait_ge(sem("split_done"), n + 1)
                sp.dma_start(scratch[w, :, j * P:(j + 1) * P, c * S:(c + 1) * S].rearrange("q p t -> p q t"),
                             parts[:, n % 2]).then_inc(sem(f"parts_stored{n % 2}"), 16)
                if n % 4 == 3:
                    for i in range(2):
                        sp.wait_ge(sem(f"parts_stored{i}"), 32 * (c + 1))
                    for w2, slots in ((0, Q_SLOT), (1, K_SLOT)):
                        for s, part in enumerate(slots):
                            dst = QK6[w2].rearrange("p (h t) -> p h t", h=H)[16 * s:16 * s + 16, :, c * S:(c + 1) * S]
                            sp.dma_start(dst, scratch[w2, part, :, c * S:(c + 1) * S]
                                         .rearrange("(h d) t -> d h t", d=HD0)).then_inc(sem(f"stacked{c}"), 16)
            sp.dma_start(rw0[:, :, :], io["router_w0"].rearrange("(k p) e -> p k e", p=P)).then_inc(sem("route_in"), 16)
            sp.dma_start(rc[:, :], io["route_consts"]).then_inc(sem("route_in"), 16)
            for slot_n in range(E0 + 1):
                gu, dn = W_B(slot_n)
                if slot_n == 6:
                    sp.wait_ge(sem("a_proj"), TT)
                    sp.wait_ge(sem("a_scores"), 8 * H)
                src_gu = io["L0_shared_gate_up"] if slot_n == 0 else io["L0_w_gate_up"][slot_n - 1]
                src_dn = io["L0_shared_down"] if slot_n == 0 else io["L0_w_down"][slot_n - 1]
                name = "w_shared0" if slot_n == 0 else "w_routed0"
                sp.dma_start(gu, src_gu.rearrange("(k p) n -> p k n", p=P)).then_inc(sem(name), 16)
                sp.dma_start(dn, src_dn.rearrange("(j p) n -> p j n", p=P)).then_inc(sem(name), 16)
            sp_b(sp)

        @block.gpsimd
        def _(pool):
            nc.gpsimd.memset(eps5[:, :], LN_EPS).then_inc(sem("eps_set"), 1)
            nc.gpsimd.memset(eps6[:, :], RMS_EPS).then_inc(sem("eps_set"), 1)
            nc.gpsimd.memset(zeros[:, :], 0.0).then_inc(sem("zeros_set"), 1)
            pool.wait_ge(sem("zeros_set"), 1)
            pool.dma_start(xs_rows[T:, :].rearrange("(j p) n -> p j n", p=P),
                           zeros[:, :].unsqueeze(1).to_broadcast([P, N_TILES0, D])).then_inc(sem("rows_zeroed"), 16)
            pool.wait_ge(sem("rows_zeroed"), 16)
            pool_b(pool)

        def pe_transpose_tokens(pe, src, ready, ready_at, done):
            for c in range(B):
                for i in range(QT):
                    pe.wait_ge(sem(ready), ready_at(4 * c + i))
                    for k in range(KD):
                        ins = nc.tensor.transpose(PS[:, 2 * c + k, i * P:(i + 1) * P],
                                                  src[:, 4 * c + i, k * P:(k + 1) * P], ident[:, :])
                ins.then_inc(sem(done), 1)

        @block.tensor
        def _(pe):
            pe.wait_ge(sem("xT_in"), 16)
            pe.wait_ge(sem("w_qk0"), 32)
            for n in range(8):
                c, w, j = n // 4, n // 2 % 2, n % 2
                for k in range(KD):
                    ins = nc.tensor.matmul(PS[:, n, :], W_A[w][:, k, j * P:(j + 1) * P],
                                           XT[:, k, c * S:(c + 1) * S], start=k == 0, stop=k == KD - 1)
                ins.then_inc(sem("proj_done"), 1)
            pe.wait_ge(sem("w_v0"), 16)
            for t in range(TT):
                if t % 2 == 0:
                    pe.wait_ge(sem("q32_ready"), t // 2 + 1)
                for k in range(KD):
                    ins = nc.tensor.matmul(PS[:, t // 2, t % 2 * D:(t % 2 + 1) * D], XT[:, k, t * P:(t + 1) * P],
                                           W_A[2][:, k, :], start=k == 0, stop=k == KD - 1)
                if t % 2:
                    ins.then_inc(sem("v_done"), 1)

            def scores(h, m):
                N = 8 * h + m
                if m >= 8:
                    h, m = h + 1, m - 8
                b, i = m // 4, m % 4
                wait(pe, sem("a_exp"), N - 3)
                w = (i + 1) * P
                q0, k0 = h * T + b * S + i * P, h * T + b * S
                nc.tensor.matmul(PS[:, m % 4, 0:w], QK6[0][:, bass.ds(q0, P)], QK6[1][:, bass.ds(k0, w)],
                                 start=True, stop=False)
                nc.tensor.matmul(PS[:, m % 4, i * P:w], identb[:, :], maskb[:, :],
                                 start=False, stop=True).then_inc(sem("a_scores"), 1)

            def turn(h, m):
                N = 8 * h + m
                pe.wait_ge(sem("a_exp"), N + 1)
                wait(pe, sem("a_ptA") if m % 2 == 0 else sem("a_ptD"), 4 * h + m // 2)
                for j in range(m % 4 + 1):
                    ins = nc.tensor.transpose(PS[:, 4 + m % 2, j * P:(j + 1) * P], PB[:, m % 4, j * P:(j + 1) * P],
                                              ident[:, :])
                ins.then_inc(sem("a_turned"), 1)

            def values(h, m):
                b, i = m // 4, m % 4
                wait(pe, sem("a_ptA") if m % 2 == 0 else sem("a_ptD"), 4 * h + m // 2 + 1)
                if i == 0:
                    wait(pe, sem("a_out"), 2 * h + b - 1)
                for j in range(i + 1):
                    ins = nc.tensor.matmul(PS[:, 6 + b, i * HD0:(i + 1) * HD0], PTS[:, m % 2, j * P:(j + 1) * P],
                                           V0[:, 4 * b + j, bass.ds(h * HD0, HD0)], start=j == 0, stop=j == i)
                ins.then_inc(sem("a_values"), 1)

            pe.wait_ge(sem("consts_in"), 48)
            pe.wait_ge(sem("bias_rows_in"), 64)
            pe.wait_ge(sem("stacked0"), 192)
            pe.wait_ge(sem("v_copied"), 4)
            pe.wait_ge(sem("q32_ready"), 8)
            scores(0, 0)
            scores(0, 1)

            def head(h, first=False, last=False):
                for m in range(8):
                    if first and m == 2:
                        pe.wait_ge(sem("stacked1"), 192)
                    if not (last and m >= 6):
                        scores(h, m + 2)
                    turn(h, m)
                    if m > 0:
                        values(h, m - 1)
                    elif not first:
                        values(h - 1, 7)

            head(0, first=True)
            with pe.Fori(1, H - 1) as h:
                head(h)
            head(H - 1, last=True)
            values(H - 1, 7)

            pe.wait_ge(sem("a_exp"), 8 * H)
            pe_transpose_tokens(pe, AO, "a_out", lambda t: 2 * H, "ao_turned")
            pe.wait_ge(sem("aoT_copied"), 2)
            pe.wait_ge(sem("w_o0"), 16)
            for t in range(TT):
                for k in range(KD):
                    ins = nc.tensor.matmul(PS[:, 4 + t // 2, t % 2 * D:(t % 2 + 1) * D], XT[:, k, t * P:(t + 1) * P],
                                           W_A[3][:, k, :], start=k == 0, stop=k == KD - 1)
                ins.then_inc(sem("a_proj"), 1)
            pe_b(pe)

        @block.scalar
        def _(act):
            act.dma_start(bqk0[:, :, :], io["bqk0"]).then_inc(sem("bias_in"), 16)
            act.dma_start(W_A[2], io["L0_attn_wv"].rearrange("(k p) n -> p k n", p=P)).then_inc(sem("w_v0"), 16)
            act.dma_start(ident[:, :], io["ident"]).then_inc(sem("consts_in"), 16)
            act.dma_start(identb[:, :], io["identb"]).then_inc(sem("consts_in"), 16)
            act.dma_start(maskb[:, :], io["maskb"]).then_inc(sem("consts_in"), 16)
            act.dma_start(biasrow[:, 0, :], io["L0_attn_bv"].rearrange("(o n) -> o n", o=1).to_broadcast([P, D]))\
                .then_inc(sem("bv_in"), 16)
            act.dma_start(biasrow[:, 1, :], io["L0_attn_bo"].rearrange("(o n) -> o n", o=1).to_broadcast([P, D]))\
                .then_inc(sem("bo_in"), 16)
            act.dma_start(W_A[3], io["L0_attn_wo"].rearrange("(k p) n -> p k n", p=P)).then_inc(sem("w_o0"), 16)
            act.dma_start(X[:, :, :], io["x"].rearrange("(t p) n -> p t n", p=P)).then_inc(sem("x_in"), 16)

            def part1(n):
                act.wait_ge(sem("q32_ready"), n + 1)
                if n >= 2:
                    act.wait_ge(sem(f"parts_stored{n % 2}"), 16 * (n // 2))
                nc.scalar.activation(parts[:, n % 2, 0, :], q32[:, n % 2, :], ACT.Copy).then_inc(sem("part1_done"), 1)

            part1(0)
            for n in range(8):
                if n < 7:
                    part1(n + 1)
                act.wait_ge(sem("rest_ready"), n + 1)
                nc.scalar.activation(parts[:, n % 2, 1, :], rest, ACT.Copy).then_inc(sem("part2_done"), 1)

            def exps(h, m):
                N, unit = 8 * h + m, 2 * h + m // 4
                m = m % 8
                i = m % 4
                act.wait_ge(sem("a_max"), N + 1)
                wait(act, sem("a_turned"), N - 3)
                if i == 0:
                    wait(act, sem("a_out"), unit - 1)
                nc.scalar.activation(PB[:, i, 0:(i + 1) * P], PS[:, i, 0:(i + 1) * P], ACT.Exp,
                                     bias=negmax[:, m:m + 1], accum_out=rowsum[:, m:m + 1]).then_inc(sem("a_exp"), 1)

            def copy_pt(h, m):
                N = 8 * h + m
                act.wait_ge(sem("a_turned"), N + 1)
                wait(act, sem("a_values"), N - 1)
                w = (m % 4 + 1) * P
                nc.scalar.activation(PTS[:, m % 2, 0:w], PS[:, 4 + m % 2, 0:w], ACT.Copy).then_inc(sem("a_ptA"), 1)

            def head(h, last=False):
                for m in range(8):
                    if not (last and m == 7):
                        exps(h, m + 1)
                    if m % 2 == 0:
                        copy_pt(h, m)

            act.wait_ge(sem("split_done"), 8)
            for i in range(2):
                act.wait_ge(sem(f"parts_stored{i}"), 64)
            exps(0, 0)
            head(0)
            with act.Fori(1, H - 1) as h:
                head(h)
            head(H - 1, last=True)
            for n in range(2):
                act.wait_ge(sem("ao_turned"), n + 1)
                nc.scalar.activation(XT[:, :, n * S:(n + 1) * S], PS[:, 2 * n:2 * n + 2, :], ACT.Copy)\
                    .then_inc(sem("aoT_copied"), 1)
            act_sqrt(act, 1)
            act_b(act)

        @block.vector
        def _(dve):
            own = Chain(dve, sem("dve_own"))

            def to_q32(n):
                c, w, j = n // 4, n // 2 % 2, n % 2
                dve.wait_ge(sem("proj_done"), n + 1)
                if n == 0:
                    dve.wait_ge(sem("bias_in"), 16)
                nc.vector.tensor_scalar(q32[:, n % 2, :], PS[:, n, :], bqk0[:, w, j:j + 1], 0.25 if w == 0 else 1.0,
                                        ALU.add, ALU.mult).then_inc(sem("q32_ready"), 1)

            to_q32(0)
            to_q32(1)
            for n in range(8):
                dve.wait_ge(sem("part1_done"), n + 1)
                if n >= 1:
                    dve.wait_ge(sem("split_done"), n)
                nc.vector.tensor_tensor(rest, q32[:, n % 2, :], parts[:, n % 2, 0, :], ALU.subtract)\
                    .then_inc(sem("rest_ready"), 1)
                if n + 2 < 8:
                    dve.wait_ge(sem("rest_ready"), n + 1)
                    to_q32(n + 2)
                dve.wait_ge(sem("part2_done"), n + 1)
                nc.vector.tensor_tensor(parts[:, n % 2, 2, :], rest, parts[:, n % 2, 1, :], ALU.subtract)\
                    .then_inc(sem("split_done"), 1)
            dve.wait_ge(sem("bv_in"), 16)
            for u in range(4):
                dve.wait_ge(sem("v_done"), u + 1)
                nc.vector.tensor_tensor(V0[:, 2 * u:2 * u + 2, :], PS[:, u, :].rearrange("p (t n) -> p t n", t=2),
                                        biasrow[:, 0, :].unsqueeze(1).to_broadcast([P, 2, D]), ALU.add)\
                    .then_inc(sem("v_copied"), 1)
            dve.wait_ge(sem("x_in"), 16)
            dve.wait_ge(sem("bo_in"), 16)
            own.step(nc.vector.tensor_tensor(X[:, :, :], X[:, :, :],
                                             biasrow[:, 1, :].unsqueeze(1).to_broadcast([P, TT, D]), ALU.add))
            x_plus_bo = own.n

            def maxes(h, m):
                N = 8 * h + m
                i = m % 4
                dve.wait_ge(sem("a_scores"), N + 1)
                wait(dve, sem("a_exp"), N - 7)
                nc.vector.tensor_reduce(negmax[:, m % 8:m % 8 + 1], PS[:, i, 0:(i + 1) * P], AX_X, ALU.max,
                                        negate=True).then_inc(sem("a_max"), 1)

            def copy_pt(h, m):
                N = 8 * h + m
                dve.wait_ge(sem("a_turned"), N + 1)
                wait(dve, sem("a_values"), N - 1)
                w = (m % 4 + 1) * P
                nc.vector.tensor_copy(PTS[:, m % 2, 0:w], PS[:, 4 + m % 2, 0:w]).then_inc(sem("a_ptD"), 1)

            def normalise(h, b):
                dve.wait_ge(sem("a_values"), 8 * h + 4 * b + 4)
                dve.wait_ge(sem("a_exp"), 8 * h + 4 * b + 4)
                nc.vector.reciprocal(rinv[:, 4 * b:4 * b + 4], rowsum[:, 4 * b:4 * b + 4]).then_inc(sem("a_rinv"), 1)
                dve.wait_ge(sem("a_rinv"), 2 * h + b + 1)
                nc.vector.tensor_tensor(AO[:, 4 * b:4 * b + 4, bass.ds(h * HD0, HD0)],
                                        PS[:, 6 + b, 0:QT * HD0].rearrange("p (i d) -> p i d", i=QT),
                                        rinv[:, 4 * b:4 * b + 4].unsqueeze(2).to_broadcast([P, QT, HD0]),
                                        ALU.mult).then_inc(sem("a_out"), 1)

            def head(h, first=False, last=False):
                for m in range(8):
                    if not (last and m == 7):
                        maxes(h, m + 1)
                    if m % 2:
                        copy_pt(h, m)
                    if m == 4:
                        normalise(h, 0)
                    if m == 0 and not first:
                        normalise(h - 1, 1)

            maxes(0, 0)
            head(0, first=True)
            with dve.Fori(1, H - 1) as h:
                head(h)
            head(H - 1, last=True)
            normalise(H - 1, 1)
            dve.wait_ge(sem("dve_own"), x_plus_bo)
            for t in range(TT):
                if t % 2 == 0:
                    dve.wait_ge(sem("a_proj"), t + 2)
                    own.step(nc.vector.tensor_tensor(
                        R[:, t:t + 2, :], PS[:, 4 + t // 2, :].rearrange("p (t n) -> p t n", t=2),
                        X[:, t:t + 2, :], ALU.add))
            dve_norm(dve, own, 1)
            dve_b(dve, own)



def lay_out(arrays, w):
    import numpy as np
    turned = np.ascontiguousarray
    arrays["router_w0"] = turned(w["L0_ffn_router_w"].T)
    arrays["L0_w_gate_up"] = w["L0_ffn_w_gate_up"]
    arrays["L0_w_down"] = w["L0_ffn_w_down"]
    arrays["L0_shared_gate_up"] = w["L0_ffn_shared_gate_up"]
    arrays["L0_shared_down"] = w["L0_ffn_shared_down"]
    for name in ("Wq", "Wk", "Wkg1", "Wkg2", "Wo"):
        arrays[f"L1_attn_{name}T"] = turned(w["L1_attn_" + name].T)
    arrays["L1_attn_WvgT"] = turned(np.concatenate([w["L1_attn_Wv"], w["L1_attn_Wg"]]).T)
    arrays["L1_attn_bkg2"] = w["L1_attn_bkg2"]
    arrays["L1_attn_bg"] = w["L1_attn_bg"]
    def by_head(a):
        return a.reshape(KD, P, H, P).transpose(2, 1, 0, 3)

    arrays["w_qkv1"] = turned(np.stack([by_head(w["L1_ffn_wq"]), by_head(w["L1_ffn_wk"]), by_head(w["L1_ffn_wv"])],
                                       axis=2).reshape(H, P, 3 * KD * P))
    arrays["w_o1"] = turned(w["L1_ffn_wo"].reshape(H // 2, 2, P, D).transpose(0, 2, 1, 3).reshape(H // 2, P, 2 * D))
    arrays["L1_ffn_ln1_w"], arrays["L1_ffn_ln2_w"] = w["L1_ffn_ln1_w"], w["L1_ffn_ln2_w"]
    arrays["gate_w1"] = turned(w["L1_ffn_gate_w"].T)

    def gate_up(g, u):
        gu = np.concatenate([g, u], axis=-2)
        gu = np.moveaxis(gu, -1, -2).reshape(*gu.shape[:-2], KD, P, gu.shape[-2])
        return np.moveaxis(gu, -2, -3)

    gu = gate_up(w["L1_ffn_eg_w"], w["L1_ffn_eu_w"]).reshape(E1, P, -1)
    dn = w["L1_ffn_ed_w"].transpose(0, 2, 1).reshape(E1, 2, F1 // 2, D)
    dn = np.concatenate([dn, np.zeros((E1, 2, P - F1 // 2, D), dn.dtype)], axis=2)
    dn = dn.transpose(0, 2, 1, 3).reshape(E1, P, 2 * D)
    arrays["w_experts1"] = turned(np.concatenate([gu, dn], axis=2).transpose(1, 0, 2))
    arrays["w_shared_gu1"] = turned(gate_up(w["L1_ffn_sg_w"], w["L1_ffn_su_w"]).reshape(P, -1))
    sd = w["L1_ffn_sd_w"].T
    sd = np.concatenate([sd, np.zeros((3 * P - FS1, D), sd.dtype)]).reshape(3, P, D)
    arrays["w_shared_dn1"] = turned(sd.transpose(1, 0, 2).reshape(P, 3 * D))


def _constants():
    import numpy as np
    bf = mybir.dt.np(BF16)
    start = 2.0 ** (-8.0 / H)
    slopes = np.array([start * start ** i for i in range(H)], dtype=np.float32)
    parts, left = [], slopes.copy()
    for _ in range(3):
        part = left.astype(bf)
        parts.append(part)
        left = left - part.astype(np.float32)
    pos = np.arange(S)
    pos_parts = [(pos // 256 * 256).astype(bf), (pos % 256).astype(bf)]
    q_rows, k_rows = np.zeros((2, H, P - 96, S), bf)
    for i in range(3):
        for j in range(2):
            r = 2 * i + j
            q_rows[:, r, :], k_rows[:, r, :] = parts[i][:, None], pos_parts[j][None, :]
            q_rows[:, 6 + r, :], k_rows[:, 6 + r, :] = pos_parts[j][None, :], -parts[i][:, None]
    route = np.zeros((P, RC_WORDS), np.float32)
    route[:, 0:16] = np.arange(16)
    route[:, 16:24] = P * np.arange(8)
    route[:, 24:24 + N_TILES0] = np.arange(N_TILES0)
    route[:, 128:256] = np.arange(P)[:, None] < np.arange(P)[None, :]
    route[:, 256:384] = 1.0
    feature, token = np.arange(P), np.arange(T)
    gla = np.concatenate([feature[:, None] // 8 == np.arange(H)[None, :],
                          feature[:, None] // 8 == np.arange(D)[None, :] // 16,
                          feature[:, None] % CH <= np.arange(CH)[None, :]], axis=1).astype(np.float32)
    return {
        "run": (token % CH != 0).astype(np.float32), "gla_consts": gla,
        "route_consts": route,
        "ident": np.eye(P, dtype=np.float32),
        "identb": np.eye(P, dtype=np.float32).astype(bf),
        "maskb": np.where(np.arange(P)[None, :] > np.arange(P)[:, None], -1e30, 0.0).astype(bf),
        "q_bias_rows": q_rows, "k_bias_rows": k_rows,
    }


def kernel(**inputs):
    import numpy as _np
    import concourse.bacc as _bacc
    from concourse import mybir as _mybir
    from concourse.bass_utils import run_bass_kernel_spmd as _run

    w = {k: _np.ascontiguousarray(v) for k, v in inputs.items()}
    arrays = _constants()
    x = w["L0_attn_x"].reshape(T, D)
    arrays["x"] = x
    arrays["xT"] = _np.ascontiguousarray(x.T)
    arrays["bqk0"] = _np.ascontiguousarray(
        _np.stack([w["L0_attn_bq"], w["L0_attn_bk"]]).reshape(2, KD, P).transpose(2, 0, 1))
    for name in ("wq", "wk", "wv", "wo", "bv", "bo"):
        arrays["L0_attn_" + name] = w["L0_attn_" + name]
    lay_out(arrays, w)

    nc = _bacc.Bacc("TRN2", target_bir_lowering=False, num_devices=1)
    io, fed = {}, {}
    for name, a in arrays.items():
        fed[f"in_{name}"] = a
        io[name] = nc.dram_tensor(f"in_{name}", a.shape, _mybir.dt.from_np(a.dtype), kind="ExternalInput").ap()
    out = nc.dram_tensor("out", (T, D), F32, kind="ExternalOutput").ap()
    program(nc, io, out)
    r = _run(nc, [fed], core_ids=[0])
    return r.results[0]["out"].reshape(B, S, D)
```

```python
from contextlib import ExitStack

import concourse.bass as bass
from concourse import mybir

F32 = mybir.dt.float32
F32R = mybir.dt.float32r
BF16 = mybir.dt.bfloat16
I32 = mybir.dt.int32
U32 = mybir.dt.uint32
ALU = mybir.AluOpType
ACT = mybir.ActivationFunctionType
AX_X = mybir.AxisListType.X

P = 128
B, S, D = 2, 512, 256
T = B * S
TT = T // P
KD = D // P
QT = S // P
H = 16
HD0 = D // H
LN_EPS = 1e-5
E0, F0 = 8, 512
W0_SLOT = KD * 2 * F0 + F0 // P * D
N_TILES0 = T // P + E0 - 1
RC_WORDS = 384
CH = 64
NCH = T // CH
KSCALE = 128.0 ** -0.5
QSCALE1 = 128.0 ** -0.5
RMS_EPS = 1e-6
E1, K1, F1, FS1 = 16, 6, 176, 352
W1_SLOT = KD * 2 * F1 + 2 * D
W1_SHARED = KD * 2 * FS1 + 3 * D
CW_AT = 7072
ARENA = 43008
HL = ("high", "low")
FR_AT = 16384


def wait(eng, sem, value):
    if isinstance(value, int) and value <= 0:
        return
    eng.wait_ge(sem, value)


class Chain:

    def __init__(self, eng, sem, at=0):
        self.eng, self.sem, self.n = eng, sem, at

    def step(self, ins):
        ins.then_inc(self.sem, 1)
        self.n = self.n + 1
        return self.n

    def wait(self, n=None):
        self.eng.wait_ge(self.sem, self.n if n is None else n)


def program(nc, io, out):
    with ExitStack() as ctx:
        sems = {}

        def sem(name):
            if name not in sems:
                sems[name] = ctx.enter_context(nc.semaphore(name))
            return sems[name]

        def sb(name, shape, dt=F32):
            return ctx.enter_context(nc.sbuf_tensor(name, shape, dt))

        PS = ctx.enter_context(nc.psum_tensor("PS", [P, 8, 512], F32))

        X = sb("X", [P, TT, D])
        XT = sb("XT", [P, KD, T])
        R = sb("R", [P, TT, D])
        ident = sb("ident", [P, P])
        identb = sb("identb", [P, P], BF16)
        maskb = sb("maskb", [P, P], BF16)
        bn = sb("bn", [P, TT, 6])
        mv = sb("mv", [P, TT, 2])
        sd = sb("sd", [P, TT])
        rstd = sb("rstd", [P, TT])
        var = sb("var", [P, TT])
        eps5 = sb("eps5", [P, 1])
        negmax = sb("negmax", [P, 8])
        rowsum = sb("rowsum", [P, 8])
        rinv = sb("rinv", [P, 8])
        biasrow = sb("biasrow", [P, 2, D])
        bqk0 = sb("bqk0", [P, 2, KD])

        with nc.sbuf_tensor("A", [P, ARENA], F32) as A:
            pass
        sb("A_front", [P, FR_AT])
        XT_HL = [sb(f"XT_{n}", [P, KD, T], F32R) for n in HL]
        W_HL = [[sb(f"W1_{n}{i}", [P, W1_SLOT], F32R) for n in HL] for i in range(2)]
        HT_HL = [sb(f"HT_{n}", [P, 2, 2 * P], F32R) for n in HL]
        sb("A_end", [P, ARENA - FR_AT - 2 * KD * T - 4 * W1_SLOT - 8 * P])

        def cut(at, words, dt=F32):
            v = A[:, at:at + words]
            return v if dt == F32 else v.bitcast(dt)

        W_A = [cut(19456 + 512 * n, 512).rearrange("p (k n) -> p k n", k=KD) for n in range(4)]
        QK6 = [cut(21504 + 8192 * w, 8192, BF16) for w in range(2)]
        V32 = cut(15360, TT * H * 32).rearrange("p (t h d) -> p t h d", t=TT, h=H)
        PT = cut(37888, 2 * 2048).rearrange("p (i c n) -> p i c n", i=2, c=4)
        OT = cut(41984, 512)
        max_rest = cut(42496, P)[0:H * QT, :]
        max_parts = cut(42624, 192, BF16)[0:H * QT, :].rearrange("p (q n) -> p q n", q=3)
        negmax0 = sb("negmax0", [P, B, H * QT])
        rinv0 = sb("rinv0", [P, QT * 4])
        max_rows = nc.dram_tensor("max_rows", (B, 3, H * QT, P), BF16, kind="Internal").ap()
        masktb = sb("masktb", [P, P], BF16)
        q32 = cut(39936, 1024).rearrange("p (i n) -> p i n", i=2)
        rest = cut(40960, 512)
        parts = cut(41472, 1536, BF16).rearrange("p (i q n) -> p i q n", i=2, q=3)
        AO = R
        scratch = nc.dram_tensor("qk_parts", (2, 3, D, T), BF16, kind="Internal").ap()

        def W_B(slot):
            at = W0_SLOT * slot
            return (cut(at, KD * 2 * F0).rearrange("p (k n) -> p k n", k=KD),
                    cut(at + KD * 2 * F0, F0 // P * D).rearrange("p (j n) -> p j n", j=F0 // P))

        XS0 = R
        XI = cut(37888, 2 * D).rearrange("p (i n) -> p i n", i=2)
        XIT = cut(38400, 2 * D).rearrange("p (i k t) -> p i k t", i=2, k=KD)
        YO = cut(38912, 2 * D).rearrange("p (i n) -> p i n", i=2)
        SG = cut(39936, 2 * F0).rearrange("p (i n) -> p i n", i=2)
        HB = cut(40960, 2 * F0).rearrange("p (i n) -> p i n", i=2)
        HBT = cut(41984, 2 * F0).rearrange("p (i n) -> p i n", i=2)
        YS = cut(0, TT * D).rearrange("p (t n) -> p t n", t=TT)
        YR = cut(TT * D, TT * D).rearrange("p (t n) -> p t n", t=TT)
        rw0 = sb("rw0", [P, KD, E0])
        rc = sb("rc", [P, RC_WORDS])
        iota_e = rc[:, 0:16]
        tile_sizes = rc[:, 16:24]
        iota_j = rc[:, 24:24 + N_TILES0]
        before = rc[:, 128:256]
        ones = rc[:, 256:384]
        lg = sb("lg", [P, TT, E0])
        mx = sb("mx", [P, TT, 8])
        ix = sb("ix", [P, TT, 8], U32)
        ixf = sb("ixf", [P, TT])
        oh = sb("oh", [P, TT, E0])
        en = sb("en", [P, TT])
        gate = sb("gate", [P, TT])
        cmp0 = sb("cmp0", [P, E0, 8])
        nt = sb("nt", [P, E0])
        incl = sb("incl", [P, E0])
        first_row = sb("first_row", [P, E0])
        base = sb("base", [P, TT, E0])
        slotf = sb("slotf", [P, TT])
        slot = sb("slot", [P, TT], U32)
        cmpj = sb("cmpj", [1, N_TILES0, E0])
        texf = sb("texf", [1, TT + N_TILES0])
        tile_at = sb("tile_at", [1, TT + N_TILES0], I32)
        zeros = sb("zeros", [P, D])
        at_c = 27648
        wq1, wk1 = (cut(at_c + 256 * n, 256).rearrange("p (k n) -> p k n", k=KD) for n in range(2))
        wkg1 = cut(at_c + 512, 32).rearrange("p (k n) -> p k n", k=KD)
        wkg2 = cut(at_c + 544, P)[0:16, :]
        wvg = cut(at_c + 672, 1024).rearrange("p (k n) -> p k n", k=KD)
        wo1 = cut(at_c + 1696, 512).rearrange("p (k n) -> p k n", k=KD)
        run = cut(at_c + 2208, T)
        own_head = cut(at_c + 3232, H)
        own_block = cut(at_c + 3248, D)
        causal = cut(at_c + 3504, CH)
        bkg = cut(at_c + 3568, 1)
        ga, gb, gc_, gd, ge = (cut(21632 + T * n, T) for n in range(5))
        QX = [ga, gb]
        ATS = [gd, ge]
        kg1 = cut(31728, T)[0:16, :]
        e1, e2, e3, e4 = (cut(32752 + T * n, T) for n in range(4))
        V1 = cut(36848, TT * D).rearrange("p (t n) -> p t n", t=TT)
        GP = cut(38896, TT * D).rearrange("p (t n) -> p t n", t=TT)
        KH = cut(40944, TT * P).rearrange("p (t n) -> p t n", t=TT)
        ST = [cut(41968 + D * n, D) for n in range(2)]
        UP = cut(42480, D)
        dec = sb("dec", [P, NCH])
        gsum = sb("gsum", [P, TT * H])
        gvar = sb("gvar", [P, TT * H])
        WD = [cut(21632 + 768 * n, 768).rearrange("p (w k n) -> p w k n", w=3, k=KD) for n in range(2)]
        QKT = [cut(23168 + 2048 * n, 2048).rearrange("p (w t) -> p w t", w=2) for n in range(2)]
        VH = [cut(27264 + 1024 * n, 1024).rearrange("p (t d) -> p t d", t=TT) for n in range(2)]
        AOT = cut(29312, 2048).rearrange("p (g t) -> p g t", g=2)
        WOP = cut(31360, 512).rearrange("p (g n) -> p g n", g=2)
        PB1 = cut(31872, 2048).rearrange("p (i n) -> p i n", i=4)
        PTS1 = cut(33920, 1024).rearrange("p (i n) -> p i n", i=2)
        HN = cut(4608, TT * D).rearrange("p (t n) -> p t n", t=TT)
        sq = cut(6656, D)
        ssq = sb("ssq", [P, TT])
        eps6 = sb("eps6", [P, 1])
        W1R = [cut(W1_SLOT * n, W1_SLOT) for n in range(2)]
        WSH1 = cut(2 * W1_SLOT, W1_SHARED)
        SG1 = cut(8000, 2 * FS1).rearrange("p (i n) -> p i n", i=2)
        HB1 = cut(8704, 2 * FS1).rearrange("p (i n) -> p i n", i=2)
        HBT1 = cut(9408, 2 * 384).rearrange("p (i n) -> p i n", i=2)
        rw1 = cut(6912, KD * E1).rearrange("p (k e) -> p k e", k=KD)
        lg1 = cut(6944, TT * E1).rearrange("p (t e) -> p t e", t=TT)
        cw = cut(CW_AT, TT * E1).rearrange("p (t e) -> p t e", t=TT)
        OH1 = cut(7200, TT * K1 * E1).rearrange("p (t k e) -> p t k e", t=TT, k=K1)
        zsum = sb("zsum", [P, TT])
        ixf1 = sb("ixf1", [P, TT, 8])
        xs_rows = nc.dram_tensor("xs_rows", ((TT + N_TILES0) * P, D), F32, kind="Internal").ap()
        y_rows = nc.dram_tensor("y_rows", ((TT + N_TILES0) * P, D), F32, kind="Internal").ap()

        block = ctx.enter_context(nc.Block())

        Q_SLOT = [0, 0, 1, 1, 0, 2]
        K_SLOT = [0, 1, 0, 1, 2, 0]

        def dve_norm(dve, own, phase):
            own.wait()
            for t in range(TT):
                own.step(nc.vector.bn_stats(bn[:, t, :], R[:, t, :]))
            own.wait()
            for t in range(TT):
                ins = nc.vector.bn_aggr(mv[:, t, :], bn[:, t, :])
                own.step(ins)
            own.wait()
            nc.vector.tensor_copy(var[:, :], mv[:, :, 1]).then_inc(sem("var_ready"), 1)
            dve.wait_ge(sem("sd_ready"), phase)
            own.step(nc.vector.reciprocal(rstd[:, :], sd[:, :]))
            own.wait()
            for t in range(TT):
                nc.vector.tensor_scalar(X[:, t, :], R[:, t, :], mv[:, t, 0:1], rstd[:, t:t + 1],
                                        ALU.subtract, ALU.mult).then_inc(sem("x_ready"), 1)

        def act_sqrt(act, phase):
            if phase == 1:
                act.wait_ge(sem("eps_set"), 2)
            act.wait_ge(sem("var_ready"), phase)
            nc.scalar.activation(sd[:, :], var[:, :], ACT.Sqrt, bias=eps5[:, :]).then_inc(sem("sd_ready"), 1)

        N_IT = TT + N_TILES0

        def stream(eng, step, n_items=N_IT, peel=4):
            for n in range(peel):
                step(n, n % 2, n // 2)
            pairs = (n_items - peel - 2) // 2
            with eng.Fori(peel // 2, peel // 2 + pairs) as j:
                for p in range(2):
                    step(2 * j + p, p, j)
            for n in range(peel + 2 * pairs, n_items):
                step(n, n % 2, n // 2)

        def sp_b(sp):
            sp.wait_ge(sem("x_ready"), TT)
            sp.dma_start(xs_rows[0:T, :].rearrange("(t p) n -> p t n", p=P), X[:, :, :]).then_inc(sem("own_rows"), 16)
            sp.wait_ge(sem("own_rows"), 16)

            def load(n, p):
                at = n * P if isinstance(n, int) else sp.snap(n * P)
                wait(sp, sem("b_xturned"), n - 1)
                sp.dma_start(XI[:, p, :], xs_rows[bass.ds(at, P), :]).then_inc(sem(f"xi_in{p}"), 16)

            def store(n, p):
                at = n * P if isinstance(n, int) else sp.snap(n * P)
                sp.wait_ge(sem("b_y"), n + 1)
                sp.dma_start(y_rows[bass.ds(at, P), :], YO[:, p, :]).then_inc(sem(f"y_stored{p}"), 16)

            def step(n, p, half):
                if isinstance(n, int) and n + 2 == TT:
                    sp.wait_ge(sem("rows_scattered"), 16 * TT)
                if not (isinstance(n, int) and n + 2 >= N_IT):
                    load(n + 2, p)
                if not (isinstance(n, int) and n < 2):
                    store(n - 2, p)

            load(0, 0)
            load(1, 1)
            stream(sp, step, peel=TT)
            store(N_IT - 2, N_IT % 2)
            store(N_IT - 1, 1 - N_IT % 2)
            sp.wait_ge(sem("y_stored0"), 16 * (N_IT // 2 + 1))
            sp.wait_ge(sem("y_stored1"), 16 * (N_IT // 2))
            sp.wait_ge(sem("b_down"), N_IT)
            sp.dma_start(YS, y_rows[0:T, :].rearrange("(t p) n -> p t n", p=P)).then_inc(sem("ys_in"), 16)
            sp_c(sp)

        def pool_b(pool):
            pool.wait_ge(sem("slots"), 1)
            pool.wait_ge(sem("gated"), 1)
            for t in range(TT):
                nc.gpsimd.indirect_dma_start(
                    out=xs_rows[:, :], out_offset=bass.IndirectOffsetOnAxis(ap=slot[:, t:t + 1], axis=0),
                    in_=XS0[:, t, :], in_offset=None).then_inc(sem("rows_scattered"), 16)
            pool.wait_ge(sem("y_stored0"), 16 * (N_IT // 2 + 1))
            pool.wait_ge(sem("y_stored1"), 16 * (N_IT // 2))
            pool.wait_ge(sem("b_down"), N_IT)
            for t in range(TT):
                nc.gpsimd.indirect_dma_start(
                    out=YR[:, t, :], out_offset=None, in_=y_rows[:, :],
                    in_offset=bass.IndirectOffsetOnAxis(ap=slot[:, t:t + 1], axis=0))\
                    .then_inc(sem("yr_in"), 16)
            pool_c(pool)

        def pe_b(pe):
            pe_transpose_tokens(pe, X, "x_ready", lambda t: t + 1)
            pe.wait_ge(sem("route_in"), 32)
            pe.wait_ge(sem("xT_ready"), 4)
            for t in range(TT):
                for k in range(KD):
                    ins = nc.tensor.matmul(PS[:, 4, t * E0:(t + 1) * E0], XT[:, k, t * P:(t + 1) * P], rw0[:, k, :],
                                           start=k == 0, stop=k == KD - 1)
            ins.then_inc(sem("logits"), 1)
            pe.wait_ge(sem("onehot"), 1)
            for t in range(TT):
                for s in range(t + 1):
                    nc.tensor.matmul(PS[:, 5, t * E0:(t + 1) * E0], (before if s == t else ones), oh[:, s, :],
                                     start=s == 0, stop=s == t)
            for s in range(TT):
                ins = nc.tensor.matmul(PS[:, 5, TT * E0:(TT + 1) * E0], ones, oh[:, s, :],
                                       start=s == 0, stop=s == TT - 1)
            ins.then_inc(sem("ranks"), 1)

            def turn_x(n, p, half):
                pe.wait_ge(sem(f"xi_in{p}"), 16 * half + 16)
                wait(pe, sem("b_xit"), n)
                for k in range(KD):
                    ins = nc.tensor.transpose(PS[:, 6, k * P:(k + 1) * P],
                                              XI[:, p, k * P:(k + 1) * P], ident[:, :])
                ins.then_inc(sem("b_xturned"), 1)

            def gate_up(n, p, half):
                pe.wait_ge(sem("b_xit"), n + 1)
                at = pe.value_load(tile_at[0:1, bass.ds(n, 1)], min_val=0, max_val=W0_SLOT * E0)
                for g in range(2):
                    wait(pe, sem("b_silu" if g == 0 else "b_h"), n - 1)
                    for k in range(KD):
                        ins = nc.tensor.matmul(PS[:, 2 * g + p, :], XIT[:, p, k, :],
                                               A[:, bass.ds(at + (k * 2 + g) * F0, F0)],
                                               start=k == 0, stop=k == KD - 1)
                    ins.then_inc(sem("b_gate" if g == 0 else "b_up"), 1)

            def turn_h(n, p, half):
                pe.wait_ge(sem("b_h"), n + 1)
                wait(pe, sem("b_ht"), n - 1)
                for j in range(F0 // P):
                    ins = nc.tensor.transpose(PS[:, 4 + p, j * P:(j + 1) * P], HB[:, p, j * P:(j + 1) * P], ident[:, :])
                ins.then_inc(sem("b_hturned"), 1)

            def down(n, p, half):
                pe.wait_ge(sem("b_ht"), n + 1)
                wait(pe, sem("b_y"), n)
                at = pe.value_load(tile_at[0:1, bass.ds(n, 1)], min_val=0, max_val=W0_SLOT * E0)
                for j in range(F0 // P):
                    ins = nc.tensor.matmul(PS[:, 7, 0:D], HBT[:, p, j * P:(j + 1) * P],
                                           A[:, bass.ds(at + KD * 2 * F0 + j * D, D)],
                                           start=j == 0, stop=j == F0 // P - 1)
                ins.then_inc(sem("b_down"), 1)

            pe.wait_ge(sem("tile_table"), 1)
            pe.wait_ge(sem("w_shared0"), 32)
            pe.wait_ge(sem("w_routed0"), 32 * E0)
            turn_x(0, 0, 0)

            def step(n, p, half):
                gate_up(n, p, half)
                if not (isinstance(n, int) and n < 2):
                    down(n - 2, p, half - 1)
                if not (isinstance(n, int) and n < 1):
                    turn_h(n - 1, 1 - p, half - (1 - p))
                if not (isinstance(n, int) and n == N_IT - 1):
                    turn_x(n + 1, 1 - p, half + p)

            stream(pe, step)
            n = N_IT - 1
            down(n - 1, 1 - n % 2, (n - 1) // 2)
            turn_h(n, n % 2, n // 2)
            down(n, n % 2, n // 2)
            pe_c(pe)

        def act_xT(act, nth):
            for c in range(B):
                act.wait_ge(sem("tokens_turned"), 2 * nth + c + 1)
                nc.scalar.activation(XT[:, :, c * S:(c + 1) * S], PS[:, 2 * c:2 * c + 2, :], ACT.Copy)\
                    .then_inc(sem("xT_ready"), 1)

        def act_b(act):
            act.wait_ge(sem("a_proj"), TT)
            act_xT(act, 1)
            act.wait_ge(sem("top1"), 1)
            nc.scalar.activation(en[:, :], mx[:, :, 0], ACT.Exp, scale=-1.0).then_inc(sem("exp_neg"), 1)

            def copy_ht(n, p, half):
                act.wait_ge(sem("b_hturned"), n + 1)
                wait(act, sem("b_down"), n - 1)
                nc.scalar.activation(HBT[:, p, :], PS[:, 4 + p, :], ACT.Copy).then_inc(sem("b_ht"), 1)

            def step(n, p, half):
                act.wait_ge(sem("b_gate"), n + 1)
                wait(act, sem("b_h"), n - 1)
                nc.scalar.activation(SG[:, p, :], PS[:, p, :], ACT.Silu).then_inc(sem("b_silu"), 1)
                if not (isinstance(n, int) and n < 1):
                    copy_ht(n - 1, 1 - p, half)

            stream(act, step)
            copy_ht(N_IT - 1, (N_IT - 1) % 2, 0)
            act_sqrt(act, 2)
            act_c(act)

        def dve_b(dve, own):
            dve.wait_ge(sem("logits"), 1)
            own.step(nc.vector.tensor_copy(lg[:, :, :], PS[:, 4, 0:TT * E0].rearrange("p (t e) -> p t e", e=E0)))
            own.wait()
            for t in range(TT):
                own.step(nc.vector.max(mx[:, t, :], lg[:, t, :]))
            own.wait()
            for t in range(TT):
                own.step(nc.vector.max_index(ix[:, t, :], mx[:, t, :], lg[:, t, :]))
            own.wait()
            nc.vector.tensor_copy(ixf[:, :], ix[:, :, 0]).then_inc(sem("top1"), 1)
            dve.wait_ge(sem("top1"), 1)
            dve.wait_ge(sem("route_in"), 32)
            nc.vector.tensor_tensor(oh[:, :, :], ixf[:, :].unsqueeze(2).to_broadcast([P, TT, E0]),
                                    iota_e[:, 0:E0].unsqueeze(1).to_broadcast([P, TT, E0]), ALU.is_equal)\
                .then_inc(sem("onehot"), 1)
            dve.wait_ge(sem("exp_neg"), 1)
            own.step(nc.vector.tensor_scalar(en[:, :], en[:, :], 1.0, None, ALU.add))
            own.wait()
            own.step(nc.vector.reciprocal(gate[:, :], en[:, :]))
            own.wait()
            nc.vector.tensor_tensor(XS0[:, :, :], X[:, :, :], gate[:, :].unsqueeze(2).to_broadcast([P, TT, D]),
                                    ALU.mult).then_inc(sem("gated"), 1)
            dve.wait_ge(sem("ranks"), 1)
            own.step(nc.vector.tensor_tensor(
                cmp0[:, :, :], PS[:, 5, TT * E0:(TT + 1) * E0].unsqueeze(2).to_broadcast([P, E0, 8]),
                tile_sizes.unsqueeze(1).to_broadcast([P, E0, 8]), ALU.is_gt))
            own.wait()
            own.step(nc.vector.tensor_reduce(nt[:, :], cmp0[:, :, :], AX_X, ALU.add))
            own.wait()
            own.step(nc.vector.tensor_tensor_scan(incl[:, :], ones[:, 0:E0], nt[:, :], 0.0, ALU.mult, ALU.add))
            own.wait()
            own.step(nc.vector.tensor_tensor(first_row[:, :], incl[:, :], nt[:, :], ALU.subtract))
            own.step(nc.vector.tensor_tensor(
                cmpj[:, :, :], incl[0:1, :].unsqueeze(1).to_broadcast([1, N_TILES0, E0]),
                iota_j[0:1, :].unsqueeze(2).to_broadcast([1, N_TILES0, E0]), ALU.is_le))
            own.step(nc.vector.memset(texf[:, 0:TT], 0.0))
            own.wait()
            own.step(nc.vector.tensor_scalar(first_row[:, :], first_row[:, :], float(P), float(T), ALU.mult, ALU.add))
            own.step(nc.vector.tensor_reduce(texf[:, TT:], cmpj[:, :, :], AX_X, ALU.add))
            own.wait()
            own.step(nc.vector.tensor_tensor(
                base[:, :, :], PS[:, 5, 0:TT * E0].rearrange("p (t e) -> p t e", e=E0),
                first_row[:, :].unsqueeze(1).to_broadcast([P, TT, E0]), ALU.add))
            own.step(nc.vector.tensor_scalar(texf[:, TT:], texf[:, TT:], float(E0 - 1), 1.0, ALU.min, ALU.add))
            own.wait()
            own.step(nc.vector.tensor_tensor(base[:, :, :], base[:, :, :], oh[:, :, :], ALU.mult))
            nc.vector.tensor_scalar(tile_at[:, :], texf[:, :], float(W0_SLOT), None, ALU.mult)\
                .then_inc(sem("tile_table"), 1)
            own.wait()
            own.step(nc.vector.tensor_reduce(slotf[:, :], base[:, :, :], AX_X, ALU.add))
            own.wait()
            nc.vector.tensor_copy(slot[:, :], slotf[:, :]).then_inc(sem("slots"), 1)

            def copy_xit(n, p, half):
                dve.wait_ge(sem("b_xturned"), n + 1)
                wait(dve, sem("b_up"), n - 1)
                nc.vector.tensor_copy(XIT[:, p, :, :], PS[:, 6, 0:D].rearrange("p (k t) -> p k t", k=KD))\
                    .then_inc(sem("b_xit"), 1)

            def copy_y(n, p, half):
                dve.wait_ge(sem("b_down"), n + 1)
                wait(dve, sem(f"y_stored{p}"), 16 * half)
                nc.vector.tensor_copy(YO[:, p, :], PS[:, 7, 0:D]).then_inc(sem("b_y"), 1)

            copy_xit(0, 0, 0)

            def step(n, p, half):
                dve.wait_ge(sem("b_silu"), n + 1)
                dve.wait_ge(sem("b_up"), n + 1)
                wait(dve, sem("b_hturned"), n - 1)
                nc.vector.tensor_tensor(HB[:, p, :], SG[:, p, :], PS[:, 2 + p, :], ALU.mult).then_inc(sem("b_h"), 1)
                if not (isinstance(n, int) and n == N_IT - 1):
                    copy_xit(n + 1, 1 - p, half + p)
                if not (isinstance(n, int) and n < 2):
                    copy_y(n - 2, p, half - 1)

            stream(dve, step)
            n = N_IT - 1
            copy_y(n - 1, (n - 1) % 2, (n - 1) // 2)
            copy_y(n, n % 2, n // 2)
            dve.wait_ge(sem("ys_in"), 16)
            own.step(nc.vector.tensor_tensor(R[:, :, :], X[:, :, :], YS, ALU.add))
            own.wait()
            dve.wait_ge(sem("yr_in"), 16 * TT)
            own.step(nc.vector.tensor_tensor(R[:, :, :], R[:, :, :], YR, ALU.add))
            dve_norm(dve, own, 2)
            dve_c(dve, own)

        def sp_c(sp):
            loads = [(wq1, io["L1_attn_WqT"].rearrange("(k p) n -> p k n", p=P)),
                     (wk1, io["L1_attn_WkT"].rearrange("(k p) n -> p k n", p=P)),
                     (wkg1, io["L1_attn_Wkg1T"].rearrange("(k p) n -> p k n", p=P)),
                     (wkg2, io["L1_attn_Wkg2T"]),
                     (wvg, io["L1_attn_WvgT"].rearrange("(k p) n -> p k n", p=P)),
                     (wo1, io["L1_attn_WoT"].rearrange("(k p) n -> p k n", p=P)),
                     (run, io["run"].rearrange("(o n) -> o n", o=1).to_broadcast([P, T])),
                     (cut(at_c + 3232, H + D + CH), io["gla_consts"]),
                     (bkg, io["L1_attn_bkg2"].rearrange("(p o) -> p o", o=1)),
                     (biasrow[:, 0, :], io["L1_attn_bg"].rearrange("(o n) -> o n", o=1).to_broadcast([P, D]))]
            for dst, src in loads:
                sp.dma_start(dst, src).then_inc(sem("c_in"), 16)
            sp_d(sp)

        C_LOADS = 16 * 10

        def pool_c(pool):
            pool.wait_ge(sem("c_in"), C_LOADS)
            for c in range(NCH):
                if c == 0:
                    pool.wait_ge(sem("c_qt"), 1)
                if c >= 2:
                    pool.wait_ge(sem("c_at"), c - 1)
                nc.gpsimd.tensor_tensor(QX[c % 2].rearrange("p (h t) -> p h t", h=H),
                                        e1[:, c * CH:(c + 1) * CH].unsqueeze(1).to_broadcast([P, H, CH]),
                                        own_head.unsqueeze(2).to_broadcast([P, H, CH]), ALU.mult)\
                    .then_inc(sem("c_qx"), 1)
            pool_e(pool)

        def pe_c(pe):
            pe_transpose_tokens(pe, X, "x_ready", lambda t: TT + t + 1)
            pe.wait_ge(sem("c_in"), C_LOADS)
            pe.wait_ge(sem("xT_ready"), 6)
            for c in range(B):
                for k in range(KD):
                    ins = nc.tensor.matmul(PS[0:16, 6 + c, :], wkg1[:, k, :], XT[:, k, c * S:(c + 1) * S],
                                           start=k == 0, stop=k == KD - 1)
                ins.then_inc(sem("c_kg1"), 1)
            for w, wt in ((0, wq1), (1, wk1)):
                for c in range(B):
                    for k in range(KD):
                        ins = nc.tensor.matmul(PS[:, 2 * w + c, :], wt[:, k, :], XT[:, k, c * S:(c + 1) * S],
                                               start=k == 0, stop=k == KD - 1)
            ins.then_inc(sem("c_qk"), 1)
            for c in range(B):
                pe.wait_ge(sem("c_kg1s"), c + 1)
                nc.tensor.matmul(PS[:, 4 + c, :], wkg2, kg1[:, c * S:(c + 1) * S], start=True, stop=True)\
                    .then_inc(sem("c_kg"), 1)
            for t in range(TT):
                if t >= 2:
                    pe.wait_ge(sem("c_v"), t - 1)
                    pe.wait_ge(sem("c_vgb"), t - 1)
                for k in range(KD):
                    ins = nc.tensor.matmul(PS[:, 6 + t % 2, :], XT[:, k, t * P:(t + 1) * P], wvg[:, k, :],
                                           start=k == 0, stop=k == KD - 1)
                ins.then_inc(sem("c_vg"), 1)
            pe.wait_ge(sem("c_kh"), 1)
            for t in range(TT):
                ins = nc.tensor.transpose(PS[:, 4 + t // 4, t % 4 * P:(t % 4 + 1) * P], e4[:, t * P:(t + 1) * P],
                                          ident[:, :])
                if t % 4 == 3:
                    ins.then_inc(sem("c_khturned"), 1)
            pe.wait_ge(sem("c_khs"), 2)
            pe.wait_ge(sem("c_v"), TT)
            pe.wait_ge(sem("c_vgb"), TT)

            pe.wait_ge(sem("c_qk_used"), 1)

            def chunk_scores(c):
                pb = c % 2 * CH
                pe.wait_ge(sem("c_qx"), c + 1)
                if c >= 2:
                    pe.wait_ge(sem("c_masked"), c - 1)
                for half in range(2):
                    ins = nc.tensor.matmul(PS[pb:pb + CH, 2 * (c % 2) + half, :], e2[:, c * CH:(c + 1) * CH],
                                           QX[c % 2][:, half * 512:(half + 1) * 512], start=True, stop=True)
                ins.then_inc(sem("c_at"), 1)

            chunk_scores(0)
            for c in range(NCH):
                pb, t, first = c % 2 * CH, c // 2, c % (NCH // B) == 0
                if c + 1 < NCH:
                    chunk_scores(c + 1)
                if c >= 2:
                    pe.wait_ge(sem("c_state"), c - 1)
                nc.tensor.matmul(PS[:, 6 + c % 2, 0:D], KH[pb:pb + CH, t, :], V1[pb:pb + CH, t, :],
                                 start=True, stop=True).then_inc(sem("c_update"), 1)
                if c >= 2:
                    pe.wait_ge(sem("c_copied"), c - 1)
                if not first:
                    pe.wait_ge(sem("c_state"), c)
                    nc.tensor.matmul(PS[pb:pb + CH, 4 + c % 2, 0:D], e3[:, c * CH:(c + 1) * CH], ST[(c - 1) % 2],
                                     start=True, stop=False, skip_group_check=True)
                pe.wait_ge(sem("c_masked"), c + 1)
                for h in range(H):
                    ins = nc.tensor.matmul(PS[pb:pb + CH, 4 + c % 2, h * 16:(h + 1) * 16],
                                           ATS[t % 2][pb:pb + CH, h * CH:(h + 1) * CH],
                                           V1[pb:pb + CH, t, h * 16:(h + 1) * 16],
                                           start=first, stop=True, skip_group_check=True)
                ins.then_inc(sem("c_o"), 1)
            pe_transpose_tokens(pe, R, "c_gated", lambda t: 1)
            pe.wait_ge(sem("xT_ready"), 8)
            for t in range(TT):
                for k in range(KD):
                    ins = nc.tensor.matmul(PS[:, 4 + t // 2, t % 2 * D:(t % 2 + 1) * D], XT[:, k, t * P:(t + 1) * P],
                                           wo1[:, k, :], start=k == 0, stop=k == KD - 1)
                ins.then_inc(sem("c_proj"), 1)
            pe_d(pe)

        def act_c(act):
            act_xT(act, 2)
            for c in range(B):
                act.wait_ge(sem("c_kg1"), c + 1)
                nc.scalar.activation(kg1[:, c * S:(c + 1) * S], PS[0:16, 6 + c, :], ACT.Copy)\
                    .then_inc(sem("c_kg1s"), 1)
            act.wait_ge(sem("c_kg"), 2)
            act.wait_ge(sem("c_in"), C_LOADS)
            z = PS[:, 4:6, :].rearrange("p c t -> p (c t)")
            own = Chain(act, sem("act_own"))
            own.step(nc.scalar.activation(ga, z, ACT.Abs, bias=bkg))
            own.wait()
            own.step(nc.scalar.activation(gb, ga, ACT.Exp, scale=-1.0))
            own.wait()
            nc.scalar.activation(ga, gb, ACT.Ln, bias=1.0).then_inc(sem("c_ln"), 1)
            for t in range(TT):
                act.wait_ge(sem("c_vgb"), t + 1)
                nc.scalar.activation(V1[:, t, :], PS[:, 6 + t % 2, 0:D], ACT.Copy).then_inc(sem("c_v"), 1)
            act.wait_ge(sem("c_d"), 1)
            nc.scalar.activation(e1, gd, ACT.Exp, scale=1.0 / 16).then_inc(sem("c_e"), 1)
            nc.scalar.activation(e2, gd, ACT.Exp, scale=-1.0 / 16).then_inc(sem("c_e"), 1)
            nc.scalar.activation(e3, gc_, ACT.Exp, scale=1.0 / 16).then_inc(sem("c_e"), 1)
            nc.scalar.activation(e4, ge, ACT.Exp, scale=1.0 / 16).then_inc(sem("c_e"), 1)
            nc.scalar.activation(dec[:, :], gc_.rearrange("p (c t) -> p c t", c=NCH)[:, :, CH - 1], ACT.Exp,
                                 scale=1.0 / 16).then_inc(sem("c_e"), 1)
            for u in range(2):
                act.wait_ge(sem("c_khturned"), u + 1)
                nc.scalar.activation(KH[:, 4 * u:4 * u + 4, :], PS[:, 4 + u, :].rearrange("p (t n) -> p t n", t=4),
                                     ACT.Copy).then_inc(sem("c_khs"), 1)
            own.step(nc.scalar.activation(GP, GP, ACT.Silu))
            silu_done = own.n
            for c in range(NCH):
                pb, t = c % 2 * CH, c // 2
                act.wait_ge(sem("c_o"), c + 1)
                nc.scalar.activation(R[pb:pb + CH, t, :], PS[pb:pb + CH, 4 + c % 2, 0:D], ACT.Copy)\
                    .then_inc(sem("c_copied"), 1)
            act.wait_ge(sem("c_centred"), 1)
            act.wait_ge(sem("act_own"), silu_done)
            nc.scalar.activation(V1, R[:, :, :], ACT.Square).then_inc(sem("c_squared"), 1)
            act.wait_ge(sem("c_gvar"), 1)
            nc.scalar.activation(gvar[:, :], gvar[:, :], ACT.Sqrt, bias=eps5[:, :]).then_inc(sem("c_gsd"), 1)
            act_xT(act, 3)
            act_sqrt(act, 3)
            act_d(act)

        def dve_c(dve, own):
            dve.wait_ge(sem("c_kg"), 2)
            dve.wait_ge(sem("c_in"), C_LOADS)
            z = PS[:, 4:6, :].rearrange("p c t -> p (c t)")
            dve.wait_ge(sem("c_ln"), 1)
            own.step(nc.vector.tensor_scalar(gb, z, bkg, 0.0, ALU.add, ALU.min))
            own.wait()
            own.step(nc.vector.tensor_tensor(gb, gb, ga, ALU.subtract))
            own.wait()
            own.step(nc.vector.tensor_tensor_scan(gc_, run, gb, 0.0, ALU.mult, ALU.add))
            own.wait()
            g3 = gc_.rearrange("p (c t) -> p c t", c=NCH)
            own.step(nc.vector.tensor_tensor(gd.rearrange("p (c t) -> p c t", c=NCH), g3,
                                             g3[:, :, CH // 2 - 1:CH // 2].to_broadcast([P, NCH, CH]), ALU.subtract))
            nc.vector.tensor_tensor(ge.rearrange("p (c t) -> p c t", c=NCH),
                                    g3[:, :, CH - 1:CH].to_broadcast([P, NCH, CH]), g3, ALU.subtract)\
                .then_inc(sem("c_d"), 1)
            for t in range(TT):
                dve.wait_ge(sem("c_vg"), t + 1)
                nc.vector.tensor_tensor(GP[:, t, :], PS[:, 6 + t % 2, D:2 * D], biasrow[:, 0, :], ALU.add)\
                    .then_inc(sem("c_vgb"), 1)
            q = PS[:, 0:2, :].rearrange("p c t -> p (c t)")
            kk = PS[:, 2:4, :].rearrange("p c t -> p (c t)")
            dve.wait_ge(sem("c_qk"), 1)
            dve.wait_ge(sem("c_e"), 5)
            nc.vector.tensor_tensor(e1, q, e1, ALU.mult).then_inc(sem("c_qt"), 1)
            nc.vector.scalar_tensor_tensor(e4, kk, KSCALE, e4, ALU.mult, ALU.mult).then_inc(sem("c_kh"), 1)
            own.step(nc.vector.scalar_tensor_tensor(e2, kk, KSCALE, e2, ALU.mult, ALU.mult))
            own.wait()
            nc.vector.tensor_tensor(e3, q, e3, ALU.mult).then_inc(sem("c_qk_used"), 1)
            for c in range(NCH):
                pb, t, first = c % 2 * CH, c // 2, c % (NCH // B) == 0
                dve.wait_ge(sem("c_at"), c + 1)
                if c >= 4:
                    dve.wait_ge(sem("c_o"), c - 3)
                nc.vector.tensor_tensor(ATS[t % 2][pb:pb + CH, :].rearrange("p (h t) -> p h t", h=H),
                                        PS[pb:pb + CH, 2 * (c % 2):2 * (c % 2) + 2, :]
                                        .rearrange("p a (h t) -> p (a h) t", t=CH),
                                        causal[pb:pb + CH, :].unsqueeze(1).to_broadcast([CH, H, CH]),
                                        ALU.mult).then_inc(sem("c_masked"), 1)
                dve.wait_ge(sem("c_update"), c + 1)
                if c >= 2:
                    dve.wait_ge(sem("c_o"), c)
                if c >= 1:
                    dve.wait_ge(sem("c_state"), c)
                if first:
                    nc.vector.tensor_tensor(ST[c % 2], PS[:, 6 + c % 2, 0:D], own_block, ALU.mult)\
                        .then_inc(sem("c_state"), 1)
                else:
                    own.step(nc.vector.tensor_tensor(UP, PS[:, 6 + c % 2, 0:D], own_block, ALU.mult))
                    own.wait()
                    nc.vector.scalar_tensor_tensor(ST[c % 2], ST[(c - 1) % 2], dec[:, c:c + 1], UP,
                                                   ALU.mult, ALU.add).then_inc(sem("c_state"), 1)
            dve.wait_ge(sem("c_copied"), NCH)
            o4 = R[:, :, :].rearrange("p t (h d) -> p (t h) d", h=H)

            def by_head(v):
                return v.unsqueeze(2).to_broadcast([P, TT * H, D // H])

            own.step(nc.vector.tensor_reduce(gsum[:, :], o4, AX_X, ALU.add))
            own.wait()
            own.step(nc.vector.tensor_scalar(gsum[:, :], gsum[:, :], 1.0 / (D // H), None, ALU.mult))
            own.wait()
            nc.vector.tensor_tensor(o4, o4, by_head(gsum[:, :]), ALU.subtract).then_inc(sem("c_centred"), 1)
            dve.wait_ge(sem("c_squared"), 1)
            own.step(nc.vector.tensor_reduce(gvar[:, :], V1.rearrange("p t (h d) -> p (t h) d", h=H), AX_X, ALU.add))
            own.wait()
            nc.vector.tensor_scalar(gvar[:, :], gvar[:, :], 1.0 / (D // H), None, ALU.mult).then_inc(sem("c_gvar"), 1)
            dve.wait_ge(sem("c_gsd"), 1)
            own.step(nc.vector.reciprocal(gsum[:, :], gvar[:, :]))
            own.wait()
            own.step(nc.vector.tensor_tensor(o4, o4, by_head(gsum[:, :]), ALU.mult))
            own.wait()
            nc.vector.tensor_tensor(R[:, :, :], R[:, :, :], GP, ALU.mult).then_inc(sem("c_gated"), 1)
            for u in range(4):
                dve.wait_ge(sem("c_proj"), 2 * u + 2)
                own.step(nc.vector.tensor_tensor(
                    R[:, 2 * u:2 * u + 2, :], PS[:, 4 + u, :].rearrange("p (t n) -> p t n", t=2),
                    X[:, 2 * u:2 * u + 2, :], ALU.add))
            dve_norm(dve, own, 3)
            dve_d(dve, own)

        def sp_d(sp):
            sp.wait_ge(sem("x_ready"), 2 * TT)
            sp.wait_ge(sem("c_proj"), TT)

            def load_head(g, p):
                if not isinstance(g, int):
                    g = sp.snap(g)
                wait(sp, sem("d_pieced"), 8 * g - 8)
                sp.dma_start(WD[p].rearrange("p w k n -> p (w k n)"),
                             io["w_qkv1"][bass.ds(g, 1), :, :].rearrange("g p n -> p (g n)"))\
                    .then_inc(sem(f"wd_in{p}"), 16)

            def load_wo(pair):
                if not isinstance(pair, int):
                    pair = sp.snap(pair)
                wait(sp, sem("d_wo"), 8 * pair)
                sp.dma_start(WOP.rearrange("p g n -> p (g n)"),
                             io["w_o1"][bass.ds(pair, 1), :, :].rearrange("g p n -> p (g n)"))\
                    .then_inc(sem("wo_in"), 16)

            load_head(0, 0)
            load_head(1, 1)
            for src, dst in (("L1_ffn_ln1_w", 0), ("L1_ffn_ln2_w", 1)):
                sp.dma_start(biasrow[:, dst, :], io[src].rearrange("(o n) -> o n", o=1).to_broadcast([P, D]))\
                    .then_inc(sem("ln_w_in"), 16)
            load_head(2, 0)
            load_head(3, 1)
            load_wo(0)
            with sp.Fori(1, H // 2 - 1) as pair:
                load_head(2 * pair + 2, 0)
                load_head(2 * pair + 3, 1)
                load_wo(pair)
            load_wo(H // 2 - 1)
            sp.dma_start(rw1, io["gate_w1"].rearrange("(k p) e -> p k e", p=P)).then_inc(sem("rw1_in"), 16)
            sp.dma_start(WSH1[:, 0:KD * 2 * FS1], io["w_shared_gu1"]).then_inc(sem("w_shared1"), 16)
            sp.dma_start(WSH1[:, KD * 2 * FS1:W1_SHARED], io["w_shared_dn1"]).then_inc(sem("w_shared1"), 16)

            def load_expert(e, p):
                if not isinstance(e, int):
                    e = sp.snap(e)
                wait(sp, sem("e_w_split"), e - 1)
                sp.dma_start(W1R[p], io["w_experts1"][:, bass.ds(e, 1), :].rearrange("p e n -> p (e n)"))\
                    .then_inc(sem(f"w1_in{p}"), 16)

            load_expert(0, 0)
            load_expert(1, 1)
            with sp.Fori(1, E1 // 2) as j:
                for p in range(2):
                    load_expert(2 * j + p, p)
            sp.wait_ge(sem("x_ready"), 4 * TT)
            sp.dma_start(out.rearrange("(t p) n -> p t n", p=P), X[:, :, :]).then_inc(sem("out_done"), 16)
            sp.wait_ge(sem("out_done"), 16)

        def pe_d(pe):
            pe_transpose_tokens(pe, HN, "hn_ready", lambda t: t + 1)

            def project(g, n, p):
                if n == 0:
                    pe.wait_ge(sem(f"wd_in{p}"), (g - p) * 8 + 16)
                wait(pe, sem("d_piece"), 8 * g + n)
                if n < 4:
                    w, c = n // 2, n % 2
                    for k in range(KD):
                        ins = nc.tensor.matmul(PS[:, 6, :], WD[p][:, w, k, :], XT[:, k, c * S:(c + 1) * S],
                                               start=k == 0, stop=k == KD - 1)
                else:
                    for t in (2 * n - 8, 2 * n - 7):
                        for k in range(KD):
                            ins = nc.tensor.matmul(PS[:, 6, t % 2 * P:(t % 2 + 1) * P], XT[:, k, t * P:(t + 1) * P],
                                                   WD[p][:, 2, k, :], start=k == 0, stop=k == KD - 1)
                ins.then_inc(sem("d_pieced"), 1)

            def scores(N, g, n, p):
                b, i = n // 4, n % 4
                if n % 4 == 0:
                    pe.wait_ge(sem("d_piece"), 8 * g + 4)
                wait(pe, sem("d_exp"), N - 1)
                w = (i + 1) * P
                nc.tensor.matmul(PS[:, n % 2, 0:w], QKT[p][:, 0, b * S + i * P:b * S + w],
                                 QKT[p][:, 1, b * S:b * S + w], start=True, stop=False)
                nc.tensor.matmul(PS[:, n % 2, i * P:w], identb[:, :], maskb[:, :], start=False, stop=True)\
                    .then_inc(sem("d_scores"), 1)

            def turn(N, n):
                pe.wait_ge(sem("d_norm"), N + 1)
                wait(pe, sem("d_pt"), N - 1)
                for j in range(n % 4 + 1):
                    ins = nc.tensor.transpose(PS[:, 2 + n % 2, j * P:(j + 1) * P], PB1[:, n % 4, j * P:(j + 1) * P],
                                              ident[:, :])
                ins.then_inc(sem("d_turned"), 1)

            def values(N, g, n, p):
                b, i = n // 4, n % 4
                pe.wait_ge(sem("d_pt"), N + 1)
                if i == 0:
                    pe.wait_ge(sem("d_piece"), 8 * g + 8)
                    wait(pe, sem("d_aot"), 2 * g + b - 1)
                for j in range(i + 1):
                    ins = nc.tensor.matmul(PS[:, 4 + b, i * P:(i + 1) * P], VH[p][:, 4 * b + j, :],
                                           PTS1[:, n % 2, j * P:(j + 1) * P], start=j == 0, stop=j == i)
                ins.then_inc(sem("d_values"), 1)

            def project_out(pair, t):
                if t == 0:
                    pe.wait_ge(sem("wo_in"), 16 * pair + 16)
                if t % 4 == 0:
                    pe.wait_ge(sem("d_aot"), 4 * pair + 3 + t // 4)
                pe.wait_ge(sem("d_acc"), 8 * pair + t + 8)
                for g in range(2):
                    ins = nc.tensor.matmul(PS[:, 7, 0:D], AOT[:, g, t * P:(t + 1) * P], WOP[:, g, :],
                                           start=g == 0, stop=g == 1)
                ins.then_inc(sem("d_wo"), 1)

            pe.wait_ge(sem("xT_ready"), 10)
            for n in range(8):
                project(0, n, 0)
            scores(0, 0, 0, 0)

            def pair_steps(pair, first=False, last=False):
                for m in range(16):
                    N, p, n = 16 * pair + m, m // 8, m % 8
                    g = 2 * pair + p
                    if not (last and m == 15):
                        scores(N + 1, g + (n == 7), (n + 1) % 8, (m + 1) // 8 % 2)
                    if not (last and p == 1):
                        project(g + 1, n, 1 - p)
                    turn(N, n)
                    if m > 0:
                        values(N - 1, g - (n == 0), (n - 1) % 8, (m - 1) // 8)
                    elif not first:
                        values(N - 1, g - 1, 7, 1)
                    if m < 8 and not first:
                        project_out(pair - 1, m)

            pair_steps(0, first=True)
            with pe.Fori(1, H // 2 - 1) as pair:
                pair_steps(pair)
            pair_steps(H // 2 - 1, last=True)
            values(8 * H - 1, H - 1, 7, 1)
            for t in range(TT):
                project_out(H // 2 - 1, t)
            pe_e(pe)

        def act_rms(act, src, phase):
            for t in range(TT):
                if t > 0:
                    act.wait_ge(sem("squares"), TT * (phase - 1) + t)
                nc.scalar.activation(sq, src[:, t, :], ACT.Square, accum_out=ssq[:, t:t + 1])\
                    .then_inc(sem("squares"), 1)
            act.wait_ge(sem("squares"), TT * phase)
            nc.scalar.activation(sd[:, :], ssq[:, :], ACT.Sqrt, bias=eps6[:, :], scale=1.0 / D)\
                .then_inc(sem("rms_ready"), 1)

        def dve_rms(dve, own, src, phase):
            dve.wait_ge(sem("rms_ready"), phase)
            own.step(nc.vector.reciprocal(rstd[:, :], sd[:, :]))
            own.wait()
            dve.wait_ge(sem("ln_w_in"), 32)
            for t in range(TT):
                nc.vector.scalar_tensor_tensor(HN[:, t, :], src[:, t, :], rstd[:, t:t + 1], biasrow[:, phase - 1, :],
                                               ALU.mult, ALU.mult).then_inc(sem("hn_ready"), 1)

        def act_d(act):
            act.wait_ge(sem("x_ready"), 3 * TT)
            act.wait_ge(sem("eps_set"), 2)
            act_rms(act, X, 1)
            act_xT(act, 4)

            def copy_piece(g, n, p):
                act.wait_ge(sem("d_pieced"), 8 * g + n + 1)
                wait(act, sem("d_values"), 8 * g - 8)
                if n < 4:
                    w, c = n // 2, n % 2
                    ins = nc.scalar.activation(QKT[p][:, w, c * S:(c + 1) * S], PS[:, 6, :], ACT.Copy,
                                               scale=QSCALE1 if w == 0 else 1.0)
                else:
                    ins = nc.scalar.activation(VH[p][:, 2 * n - 8:2 * n - 6, :],
                                               PS[:, 6, 0:2 * P].rearrange("p (t d) -> p t d", t=2), ACT.Copy)
                ins.then_inc(sem("d_piece"), 1)

            def exps(N, n):
                act.wait_ge(sem("d_max"), N + 1)
                wait(act, sem("d_turned"), N - 3)
                i = n % 4
                nc.scalar.activation(PB1[:, i, 0:(i + 1) * P], PS[:, n % 2, 0:(i + 1) * P], ACT.Exp,
                                     bias=negmax[:, n:n + 1], accum_out=rowsum[:, n:n + 1]).then_inc(sem("d_exp"), 1)

            def copy_out(pair, unit):
                p, b = unit // 2, unit % 2
                act.wait_ge(sem("d_values"), 16 * pair + 4 * unit + 4)
                wait(act, sem("d_wo"), 8 * (pair - 1) + 4 * b + 4)
                nc.scalar.activation(AOT[:, p, b * S:(b + 1) * S], PS[:, 4 + b, :], ACT.Copy).then_inc(sem("d_aot"), 1)

            for n in range(8):
                copy_piece(0, n, 0)
            exps(0, 0)

            def pair_steps(pair, first=False, last=False):
                for m in range(16):
                    N, p, n = 16 * pair + m, m // 8, m % 8
                    if not (last and m == 15):
                        exps(N + 1, (n + 1) % 8)
                    if not (last and p == 1):
                        copy_piece(2 * pair + p + 1, n, 1 - p)
                    if m % 4 == 0:
                        if m > 0:
                            copy_out(pair, m // 4 - 1)
                        elif not first:
                            copy_out(pair - 1, 3)

            pair_steps(0, first=True)
            with act.Fori(1, H // 2 - 1) as pair:
                pair_steps(pair)
            pair_steps(H // 2 - 1, last=True)
            copy_out(H // 2 - 1, 3)
            act_e(act)

        def dve_d(dve, own):
            dve_rms(dve, own, X, 1)
            for t in range(TT):
                nc.vector.tensor_copy(R[:, t, :], X[:, t, :]).then_inc(sem("d_acc"), 1)

            def maxes(N, n):
                dve.wait_ge(sem("d_scores"), N + 1)
                wait(dve, sem("d_exp"), N - 7)
                i = n % 4
                nc.vector.tensor_reduce(negmax[:, n:n + 1], PS[:, n % 2, 0:(i + 1) * P], AX_X, ALU.max,
                                        negate=True).then_inc(sem("d_max"), 1)

            def normalise(N, n):
                i = n % 4
                dve.wait_ge(sem("d_exp"), N + 1)
                nc.vector.reciprocal(rinv[:, n:n + 1], rowsum[:, n:n + 1]).then_inc(sem("d_rinv"), 1)
                dve.wait_ge(sem("d_rinv"), N + 1)
                nc.vector.tensor_scalar(PB1[:, i, 0:(i + 1) * P], PB1[:, i, 0:(i + 1) * P], rinv[:, n:n + 1], None,
                                        ALU.mult).then_inc(sem("d_norm"), 1)

            def copy_pt(N, n):
                dve.wait_ge(sem("d_turned"), N + 1)
                wait(dve, sem("d_values"), N - 1)
                w = (n % 4 + 1) * P
                nc.vector.tensor_copy(PTS1[:, n % 2, 0:w], PS[:, 2 + n % 2, 0:w]).then_inc(sem("d_pt"), 1)

            def accumulate(pair, t):
                dve.wait_ge(sem("d_wo"), 8 * pair + t + 1)
                dve.wait_ge(sem("d_acc"), 8 * pair + t + 1)
                nc.vector.tensor_tensor(R[:, t, :], R[:, t, :], PS[:, 7, 0:D], ALU.add).then_inc(sem("d_acc"), 1)

            maxes(0, 0)

            def pair_steps(pair, first=False, last=False):
                for m in range(16):
                    N, n = 16 * pair + m, m % 8
                    normalise(N, n)
                    if not (last and m == 15):
                        maxes(N + 1, (n + 1) % 8)
                    copy_pt(N, n)
                    if 0 < m <= 8 and not first:
                        accumulate(pair - 1, m - 1)

            pair_steps(0, first=True)
            with dve.Fori(1, H // 2 - 1) as pair:
                pair_steps(pair)
            pair_steps(H // 2 - 1, last=True)
            for t in range(TT):
                accumulate(H // 2 - 1, t)
            dve_e(dve, own)

        def act_e(act):
            act.wait_ge(sem("d_acc"), 4 * H + TT)
            act_rms(act, R, 2)
            act_xT(act, 5)
            for t in range(TT):
                act.wait_ge(sem("e_max"), 1)
                nc.scalar.activation(cw[:, t, :], lg1[:, t, :], ACT.Exp, bias=negmax[:, t:t + 1],
                                     accum_out=zsum[:, t:t + 1]).then_inc(sem("e_exp"), 1)

            def silu(N, p, f):
                act.wait_ge(sem("e_gu"), N + 1)
                wait(act, sem("e_h"), N - 1)
                nc.scalar.activation(SG1[:, p, 0:f], PS[:, p, 0:f], ACT.Silu).then_inc(sem("e_silu"), 1)

            def high_ht(N, p):
                act.wait_ge(sem("e_hturned"), N + 1)
                wait(act, sem("e_down"), N - 1)
                nc.scalar.activation(HT_HL[0][0:F1 // 2, p, :], PS[0:F1 // 2, 4 + p, 0:2 * P], ACT.Copy)\
                    .then_inc(sem("e_ht"), 1)

            def shared(t):
                silu(t, t % 2, FS1)
                if t > 0:
                    shared_ht(t - 1)

            def shared_ht(t):
                p = t % 2
                act.wait_ge(sem("e_hturned"), t + 1)
                wait(act, sem("e_down"), t - 1)
                nc.scalar.activation(HBT1[:, p, 0:256], PS[:, 4 + p, 0:256], ACT.Copy)
                nc.scalar.activation(HBT1[0:96, p, 256:384], PS[0:96, 4 + p, 256:384], ACT.Copy)\
                    .then_inc(sem("e_ht"), 1)

            for t in range(TT):
                shared(t)

            def expert(e, first=False):
                for t in range(TT):
                    N = TT * (e + 1) + t
                    silu(N, t % 2, F1)
                    if first and t == 0:
                        shared_ht(TT - 1)
                    else:
                        high_ht(N - 1, (t - 1) % 2)

            expert(0, first=True)
            with act.Fori(1, E1) as e:
                expert(e)
            high_ht(TT * (E1 + 1) - 1, 1)
            act_sqrt(act, 4)

        def pe_e(pe):
            pe_transpose_tokens(pe, HN, "hn_ready", lambda t: TT + t + 1)
            pe.wait_ge(sem("rw1_in"), 16)
            pe.wait_ge(sem("xT_ready"), 12)
            for t in range(TT):
                for k in range(KD):
                    ins = nc.tensor.matmul(PS[:, 7, t * E1:(t + 1) * E1], XT[:, k, t * P:(t + 1) * P], rw1[:, k, :],
                                           start=k == 0, stop=k == KD - 1)
            ins.then_inc(sem("e_logits"), 1)
            pe.wait_ge(sem("w_shared1"), 32)

            def turn_h(N, chunks, width, p):
                pe.wait_ge(sem("e_h"), N + 1)
                if isinstance(N, int) and N < TT + 2:
                    wait(pe, sem("e_ht"), N - 1)
                else:
                    pe.wait_ge(sem("e_ht_low"), N - TT - 1)
                for j, (rows, c) in enumerate(chunks):
                    ins = nc.tensor.transpose(PS[0:rows, 4 + p, c:c + P], HB1[:, p, j * width:j * width + rows],
                                              ident[:, :])
                ins.then_inc(sem("e_hturned"), 1)

            SH = [(P, 0), (P, P), (96, 2 * P)]

            def shared_gate_up(t):
                for g in range(2):
                    wait(pe, sem("e_silu" if g == 0 else "e_h"), t - 1)
                    for k in range(KD):
                        ins = nc.tensor.matmul(PS[:, 2 * g + t % 2, 0:FS1], XT[:, k, t * P:(t + 1) * P],
                                               WSH1[:, (2 * k + g) * FS1:(2 * k + g + 1) * FS1],
                                               start=k == 0, stop=k == KD - 1)
                ins.then_inc(sem("e_gu"), 1)

            def shared_down(t):
                pe.wait_ge(sem("e_ht"), t + 1)
                wait(pe, sem("e_acc"), t)
                for j, (rows, c) in enumerate(SH):
                    ins = nc.tensor.matmul(PS[:, 6, 0:D], HBT1[0:rows, t % 2, c:c + P],
                                           WSH1[0:rows, KD * 2 * FS1 + j * D:KD * 2 * FS1 + (j + 1) * D],
                                           start=j == 0, stop=j == len(SH) - 1)
                ins.then_inc(sem("e_down"), 1)

            for t in range(TT):
                shared_gate_up(t)
                if t >= 1:
                    turn_h(t - 1, SH, P, (t - 1) % 2)
                if t >= 2:
                    shared_down(t - 2)

            EX = [(F1 // 2, 0), (F1 // 2, P)]
            PRODUCTS = [(0, 0), (0, 1), (1, 0)]

            def gate_up(N, t, W):
                wait(pe, sem("e_h"), N - 1)
                for k in range(KD):
                    for x, w in PRODUCTS:
                        ins = nc.tensor.matmul(PS[:, t % 2, 0:2 * F1], XT_HL[x][:, k, t * P:(t + 1) * P],
                                               W[w][:, k * 2 * F1:(k + 1) * 2 * F1],
                                               start=k == 0 and x + w == 0, stop=k == KD - 1 and x == 1)
                ins.then_inc(sem("e_gu"), 1)

            def down(N, W, p):
                pe.wait_ge(sem("e_ht_low"), N + 1 - TT)
                pe.wait_ge(sem("e_acc"), N)
                for j, (rows, c) in enumerate(EX):
                    for x, w in PRODUCTS:
                        at = KD * 2 * F1 + j * D
                        ins = nc.tensor.matmul(PS[:, 6, 0:D], HT_HL[x][0:rows, p, c:c + P], W[w][0:rows, at:at + D],
                                               start=j == 0 and x + w == 0, stop=j == 1 and x == 1)
                ins.then_inc(sem("e_down"), 1)

            def expert(e, p, first=False):
                pe.wait_ge(sem("e_w_split"), e + 1)
                for t in range(TT):
                    N = TT * (e + 1) + t
                    gate_up(N, t, W_HL[p])
                    if first and t < 1:
                        turn_h(N - 1, SH, P, 1)
                    else:
                        turn_h(N - 1, EX, F1 // 2, (t - 1) % 2)
                    if first and t < 2:
                        shared_down(TT - 2 + t)
                    else:
                        down(N - 2, W_HL[1 - p if t < 2 else p], t % 2)

            pe.wait_ge(sem("xT_split"), 2)
            expert(0, 0, first=True)
            expert(1, 1)
            with pe.Fori(1, E1 // 2) as j:
                for p in range(2):
                    expert(2 * j + p, p)
            N = TT * (E1 + 1)
            turn_h(N - 1, EX, F1 // 2, 1)
            down(N - 2, W_HL[1], 0)
            down(N - 1, W_HL[1], 1)

        def pool_e(pool):
            pool.wait_ge(sem("xT_ready"), 12)
            nc.gpsimd.tensor_copy(XT_HL[0][:, :, :], XT[:, :, :]).then_inc(sem("xT_high"), 1)
            pool.wait_ge(sem("xT_high"), 1)
            nc.gpsimd.tensor_tensor(XT_HL[1][:, :, :], XT[:, :, :], XT_HL[0][:, :, :].bitcast(F32), ALU.subtract)\
                .then_inc(sem("xT_split"), 2)

            def split(e, p):
                pool.wait_ge(sem(f"w1_in{p}"), (e - p) * 8 + 16)
                wait(pool, sem("e_down"), TT * e)
                nc.gpsimd.tensor_copy(W_HL[p][0][:, :], W1R[p]).then_inc(sem("e_w_high"), 1)
                pool.wait_ge(sem("e_w_high"), e + 1)
                nc.gpsimd.tensor_tensor(W_HL[p][1][:, :], W1R[p], W_HL[p][0][:, :].bitcast(F32), ALU.subtract)\
                    .then_inc(sem("e_w_split"), 1)

            pool.wait_ge(sem("d_acc"), 4 * H + TT)
            for e in range(E1):
                split(e, e % 2)

        def dve_e(dve, own):
            dve_rms(dve, own, R, 2)
            dve.wait_ge(sem("e_logits"), 1)
            own.step(nc.vector.tensor_copy(lg1, PS[:, 7, 0:TT * E1].rearrange("p (t e) -> p t e", e=E1)))
            own.wait()
            nc.vector.tensor_reduce(negmax[:, :], lg1, AX_X, ALU.max, negate=True).then_inc(sem("e_max"), 1)
            dve.wait_ge(sem("e_exp"), TT)
            own.step(nc.vector.reciprocal(rinv[:, :], zsum[:, :]))
            own.wait()
            own.step(nc.vector.tensor_tensor(lg1, cw, rinv[:, :].unsqueeze(2).to_broadcast([P, TT, E1]), ALU.mult))
            own.wait()
            for t in range(TT):
                own.step(nc.vector.max(mx[:, t, :], lg1[:, t, :]))
            own.wait()
            for t in range(TT):
                own.step(nc.vector.max_index(ix[:, t, :], mx[:, t, :], lg1[:, t, :]))
            own.step(nc.vector.tensor_reduce(zsum[:, :], mx[:, :, 0:K1], AX_X, ALU.add))
            own.wait()
            own.step(nc.vector.tensor_copy(ixf1[:, :, :], ix[:, :, :]))
            own.step(nc.vector.reciprocal(rinv[:, :], zsum[:, :]))
            own.wait()
            own.step(nc.vector.tensor_tensor(mx[:, :, :], mx[:, :, :], rinv[:, :].unsqueeze(2)
                                             .to_broadcast([P, TT, 8]), ALU.mult))
            own.wait()
            for t in range(TT):
                own.step(nc.vector.tensor_tensor(
                    OH1[:, t, :, :], ixf1[:, t, 0:K1].unsqueeze(2).to_broadcast([P, K1, E1]),
                    iota_e.unsqueeze(1).to_broadcast([P, K1, E1]), ALU.is_equal))
            own.wait()
            for t in range(TT):
                own.step(nc.vector.tensor_tensor(OH1[:, t, :, :], OH1[:, t, :, :],
                                                 mx[:, t, 0:K1].unsqueeze(2).to_broadcast([P, K1, E1]), ALU.mult))
            own.wait()
            own.step(nc.vector.tensor_reduce(cw, OH1.rearrange("p t k e -> p t e k"), AX_X, ALU.add))
            own.wait()

            def hidden(N, p, f, up_bank, up_at):
                dve.wait_ge(sem("e_silu"), N + 1)
                wait(dve, sem("e_hturned"), N - 1)
                nc.vector.tensor_tensor(HB1[:, p, 0:f], SG1[:, p, 0:f], PS[:, up_bank, up_at:up_at + f], ALU.mult)\
                    .then_inc(sem("e_h"), 1)

            def add_shared(t):
                dve.wait_ge(sem("e_down"), t + 1)
                nc.vector.tensor_tensor(R[:, t, :], R[:, t, :], PS[:, 6, 0:D], ALU.add).then_inc(sem("e_acc"), 1)

            def add_expert(N, t, e):
                dve.wait_ge(sem("e_down"), N + 1)
                dve.wait_ge(sem("e_acc"), N - 7)
                at = CW_AT + t * E1 + e
                nc.vector.scalar_tensor_tensor(R[:, t, :], PS[:, 6, 0:D], A[:, bass.ds(at, 1)], R[:, t, :],
                                               ALU.mult, ALU.add).then_inc(sem("e_acc"), 1)

            def low_ht(N, p):
                dve.wait_ge(sem("e_ht"), N + 1)
                nc.vector.tensor_tensor(HT_HL[1][0:F1 // 2, p, :], PS[0:F1 // 2, 4 + p, 0:2 * P],
                                        HT_HL[0][0:F1 // 2, p, :].bitcast(F32), ALU.subtract)\
                    .then_inc(sem("e_ht_low"), 1)

            for t in range(TT):
                hidden(t, t % 2, FS1, 2 + t % 2, 0)
                if t >= 2:
                    add_shared(t - 2)

            def expert(e, first=False):
                for t in range(TT):
                    N = TT * (e + 1) + t
                    hidden(N, t % 2, F1, t % 2, F1)
                    if not (first and t == 0):
                        low_ht(N - 1, (t - 1) % 2)
                    if first and t < 2:
                        add_shared(TT - 2 + t)
                    else:
                        add_expert(N - 2, (t - 2) % TT, e - (1 if t < 2 else 0))

            expert(0, first=True)
            with dve.Fori(1, E1) as e:
                expert(e)
            N = TT * (E1 + 1)
            low_ht(N - 1, 1)
            add_expert(N - 2, TT - 2, E1 - 1)
            add_expert(N - 1, TT - 1, E1 - 1)
            dve.wait_ge(sem("e_acc"), N)
            own.step(nc.vector.tensor_tensor(R[:, :, :], R[:, :, :], X[:, :, :], ALU.add))
            dve_norm(dve, own, 4)

        @block.sync
        def _(sp):
            sp.dma_start(W_A[0], io["L0_attn_wq"].rearrange("(k p) n -> p k n", p=P)).then_inc(sem("w_qk0"), 16)
            sp.dma_start(XT[:, :, :], io["xT"].rearrange("(k p) t -> p k t", p=P)).then_inc(sem("xT_in"), 16)
            sp.dma_start(W_A[1], io["L0_attn_wk"].rearrange("(k p) n -> p k n", p=P)).then_inc(sem("w_qk0"), 16)
            for c in range(B):
                for w, src in ((0, io["q_bias_rows"]), (1, io["k_bias_rows"])):
                    dst = QK6[w].rearrange("p (h t) -> p h t", h=H)[96:P, :, c * S:(c + 1) * S]
                    sp.dma_start(dst, src.rearrange("h r t -> r h t")).then_inc(sem("bias_rows_in"), 16)
            for n in range(8):
                c, w, j = n // 4, n // 2 % 2, n % 2
                sp.wait_ge(sem("split_done"), n + 1)
                sp.dma_start(scratch[w, :, j * P:(j + 1) * P, c * S:(c + 1) * S].rearrange("q p t -> p q t"),
                             parts[:, n % 2]).then_inc(sem(f"parts_stored{n % 2}"), 16)
                if n % 4 == 3:
                    for i in range(2):
                        sp.wait_ge(sem(f"parts_stored{i}"), 32 * (c + 1))
                    for w2, slots in ((0, Q_SLOT), (1, K_SLOT)):
                        for s, part in enumerate(slots):
                            dst = QK6[w2].rearrange("p (h t) -> p h t", h=H)[16 * s:16 * s + 16, :, c * S:(c + 1) * S]
                            sp.dma_start(dst, scratch[w2, part, :, c * S:(c + 1) * S]
                                         .rearrange("(h d) t -> d h t", d=HD0)).then_inc(sem(f"stacked{c}"), 16)
            for b in range(B):
                sp.wait_ge(sem("max_part3"), b + 1)
                sp.dma_start(max_rows[b].rearrange("q x n -> x q n"), max_parts[:, :, :])\
                    .then_inc(sem("maxima_stored"), 16)
                sp.wait_ge(sem("maxima_stored"), 16 * (b + 1))
                sp.dma_start(QK6[0].rearrange("p (h t) -> p h t", h=H)[108:111, :, b * S:(b + 1) * S],
                             max_rows[b].rearrange("q (h i) n -> q h (i n)", h=H)).then_inc(sem(f"max_rows_in{b}"), 16)
            sp.dma_start(rw0[:, :, :], io["router_w0"].rearrange("(k p) e -> p k e", p=P)).then_inc(sem("route_in"), 16)
            sp.dma_start(rc[:, :], io["route_consts"]).then_inc(sem("route_in"), 16)
            for slot_n in range(E0 + 1):
                gu, dn = W_B(slot_n)
                if slot_n == 5:
                    sp.wait_ge(sem("a_values"), 32)
                if slot_n == 6:
                    sp.wait_ge(sem("a_proj"), TT)
                src_gu = io["L0_shared_gate_up"] if slot_n == 0 else io["L0_w_gate_up"][slot_n - 1]
                src_dn = io["L0_shared_down"] if slot_n == 0 else io["L0_w_down"][slot_n - 1]
                name = "w_shared0" if slot_n == 0 else "w_routed0"
                sp.dma_start(gu, src_gu.rearrange("(k p) n -> p k n", p=P)).then_inc(sem(name), 16)
                sp.dma_start(dn, src_dn.rearrange("(j p) n -> p j n", p=P)).then_inc(sem(name), 16)
            sp_b(sp)

        @block.gpsimd
        def _(pool):
            nc.gpsimd.memset(eps5[:, :], LN_EPS).then_inc(sem("eps_set"), 1)
            nc.gpsimd.memset(eps6[:, :], RMS_EPS).then_inc(sem("eps_set"), 1)
            nc.gpsimd.memset(V32[:, :, :, :], 0.0).then_inc(sem("v_padded"), 1)
            pool.wait_ge(sem("v_padded"), 1)
            nc.gpsimd.memset(V32[:, :, :, HD0:HD0 + 1], 1.0).then_inc(sem("v_padded"), 1)
            nc.gpsimd.memset(zeros[:, :], 0.0).then_inc(sem("zeros_set"), 1)
            pool.wait_ge(sem("zeros_set"), 1)
            pool.dma_start(xs_rows[T:, :].rearrange("(j p) n -> p j n", p=P),
                           zeros[:, :].unsqueeze(1).to_broadcast([P, N_TILES0, D])).then_inc(sem("rows_zeroed"), 16)
            pool.wait_ge(sem("rows_zeroed"), 16)
            pool_b(pool)

        def pe_transpose_tokens(pe, src, ready, ready_at):
            for c in range(B):
                for i in range(QT):
                    pe.wait_ge(sem(ready), ready_at(4 * c + i))
                    for k in range(KD):
                        ins = nc.tensor.transpose(PS[:, 2 * c + k, i * P:(i + 1) * P],
                                                  src[:, 4 * c + i, k * P:(k + 1) * P], ident[:, :])
                ins.then_inc(sem("tokens_turned"), 1)

        @block.tensor
        def _(pe):
            pe.wait_ge(sem("xT_in"), 16)
            pe.wait_ge(sem("w_qk0"), 32)
            for n in range(8):
                c, w, j = n // 4, n // 2 % 2, n % 2
                for k in range(KD):
                    ins = nc.tensor.matmul(PS[:, n, :], W_A[w][:, k, j * P:(j + 1) * P],
                                           XT[:, k, c * S:(c + 1) * S], start=k == 0, stop=k == KD - 1)
                ins.then_inc(sem("proj_done"), 1)
            pe.wait_ge(sem("w_v0"), 16)
            for t in range(TT):
                if t % 2 == 0:
                    pe.wait_ge(sem("q32_ready"), t // 2 + 1)
                for k in range(KD):
                    ins = nc.tensor.matmul(PS[:, t // 2, t % 2 * D:(t % 2 + 1) * D], XT[:, k, t * P:(t + 1) * P],
                                           W_A[2][:, k, :], start=k == 0, stop=k == KD - 1)
                if t % 2:
                    ins.then_inc(sem("v_done"), 1)

            def scores(b, h, i):
                M = b * H * QT + QT * h + i
                wait(pe, sem("a_max"), M - 1)
                w = (i + 1) * P
                q0, k0 = h * T + b * S + i * P, h * T + b * S
                nc.tensor.matmul(PS[:, 6 + i % 2, 0:w], QK6[0][:, bass.ds(q0, P)], QK6[1][:, bass.ds(k0, w)],
                                 start=True, stop=False)
                nc.tensor.matmul(PS[:, 6 + i % 2, i * P:w], identb[:, :], maskb[:, :],
                                 start=False, stop=True).then_inc(sem("a_scores"), 1)

            def turn_maxima(b):
                pe.wait_ge(sem("a_max"), (b + 1) * H * QT)
                wait(pe, sem("a_out"), 4 * b)
                nc.tensor.transpose(PS[0:H * QT, 5, 0:P], negmax0[:, b, :], ident[:, :])\
                    .then_inc(sem("a_maxima"), 1)

            def scores_t(b, g, j, x):
                n = 2 * (16 * b + 4 * g + j) + x
                wait(pe, sem("a_exp"), n - 1)
                w = (QT - j) * P
                for c in range(2 * x, 2 * x + 2):
                    at = (4 * g + c) * T + b * S + j * P
                    nc.tensor.matmul(PS[:, c, 0:w], QK6[1][:, at:at + P], QK6[0][:, at:at + w],
                                     start=True, stop=False)
                    ins = nc.tensor.matmul(PS[:, c, 0:P], identb[:, :], masktb[:, :], start=False, stop=True)
                ins.then_inc(sem("a_scores_t"), 1)

            def values(b, g, j):
                u = 16 * b + 4 * g + j
                pe.wait_ge(sem("a_exp"), 2 * u + 2)
                if j == 0:
                    wait(pe, sem("a_ot"), 4 * b + g)
                for c in range(4):
                    ins = nc.tensor.matmul(PS[32 * c:32 * c + 32, 4, j * P:S], V32[:, 4 * b + j, 4 * g + c, :],
                                           PT[:, u % 2, c, 0:S - j * P], start=j == 0, stop=j == QT - 1,
                                           skip_group_check=True)
                ins.then_inc(sem("a_values"), 1)

            def turn_back(b, g):
                G = 4 * b + g
                pe.wait_ge(sem("a_ot"), G + 1)
                wait(pe, sem("a_out"), G)
                if g == 0:
                    pe.wait_ge(sem("max_part3"), b + 1)
                for i in range(QT):
                    ins = nc.tensor.transpose(PS[:, 5, i * P:(i + 1) * P], OT[:, i * P:(i + 1) * P], ident[:, :])
                ins.then_inc(sem("a_turned"), 1)

            pe.wait_ge(sem("consts_in"), 64)
            pe.wait_ge(sem("bias_rows_in"), 64)
            pe.wait_ge(sem("stacked0"), 192)
            pe.wait_ge(sem("v_copied"), 4)
            pe.wait_ge(sem("q32_ready"), 8)
            for i in range(QT):
                scores(0, 0, i)
            with pe.Fori(1, H) as h:
                for i in range(QT):
                    scores(0, h, i)
            turn_maxima(0)
            pe.wait_ge(sem("stacked1"), 192)
            units = [(b, g, j) for b in range(B) for g in range(4) for j in range(QT)]
            ahead = [(1, h, i) for h in range(H) for i in range(QT)]
            for n in range(12):
                scores(*ahead.pop(0))
            for u, (b, g, j) in enumerate(units):
                if (g, j) == (0, 0):
                    if b == 1:
                        turn_maxima(1)
                    pe.wait_ge(sem(f"max_rows_in{b}"), 16)
                    for x in range(2):
                        scores_t(b, g, j, x)
                if u + 1 < len(units) and units[u + 1][1:] != (0, 0):
                    for x in range(2):
                        scores_t(*units[u + 1], x)
                for n in range(min(4, len(ahead))):
                    scores(*ahead.pop(0))
                values(b, g, j)
                if j == 0 and g > 0:
                    turn_back(b, g - 1)
                if (g, j) == (3, QT - 1):
                    turn_back(b, g)

            pe.wait_ge(sem("a_exp"), 64)
            pe_transpose_tokens(pe, AO, "a_out", lambda t: 4 + t // QT * 4)
            pe.wait_ge(sem("xT_ready"), 2)
            pe.wait_ge(sem("w_o0"), 16)
            for t in range(TT):
                for k in range(KD):
                    ins = nc.tensor.matmul(PS[:, 4 + t // 2, t % 2 * D:(t % 2 + 1) * D], XT[:, k, t * P:(t + 1) * P],
                                           W_A[3][:, k, :], start=k == 0, stop=k == KD - 1)
                ins.then_inc(sem("a_proj"), 1)
            pe_b(pe)

        @block.scalar
        def _(act):
            act.dma_start(bqk0[:, :, :], io["bqk0"]).then_inc(sem("bias_in"), 16)
            act.dma_start(W_A[2], io["L0_attn_wv"].rearrange("(k p) n -> p k n", p=P)).then_inc(sem("w_v0"), 16)
            act.dma_start(ident[:, :], io["ident"]).then_inc(sem("consts_in"), 16)
            act.dma_start(identb[:, :], io["identb"]).then_inc(sem("consts_in"), 16)
            act.dma_start(maskb[:, :], io["maskb"]).then_inc(sem("consts_in"), 16)
            act.dma_start(masktb[:, :], io["masktb"]).then_inc(sem("consts_in"), 16)
            act.dma_start(biasrow[:, 0, :], io["L0_attn_bv"].rearrange("(o n) -> o n", o=1).to_broadcast([P, D]))\
                .then_inc(sem("bv_in"), 16)
            act.dma_start(biasrow[:, 1, :], io["L0_attn_bo"].rearrange("(o n) -> o n", o=1).to_broadcast([P, D]))\
                .then_inc(sem("bo_in"), 16)
            act.dma_start(W_A[3], io["L0_attn_wo"].rearrange("(k p) n -> p k n", p=P)).then_inc(sem("w_o0"), 16)
            act.dma_start(X[:, :, :], io["x"].rearrange("(t p) n -> p t n", p=P)).then_inc(sem("x_in"), 16)

            def part1(n):
                act.wait_ge(sem("q32_ready"), n + 1)
                if n >= 2:
                    act.wait_ge(sem(f"parts_stored{n % 2}"), 16 * (n // 2))
                nc.scalar.activation(parts[:, n % 2, 0, :], q32[:, n % 2, :], ACT.Copy).then_inc(sem("part1_done"), 1)

            part1(0)
            for n in range(8):
                if n < 7:
                    part1(n + 1)
                act.wait_ge(sem("rest_ready"), n + 1)
                nc.scalar.activation(parts[:, n % 2, 1, :], rest, ACT.Copy).then_inc(sem("part2_done"), 1)

            def split_maxima(b):
                act.wait_ge(sem("a_maxima"), b + 1)
                wait(act, sem("maxima_stored"), 16 * b)
                nc.scalar.activation(max_parts[:, 0, :], PS[0:H * QT, 5, 0:P], ACT.Copy).then_inc(sem("max_part1"), 1)
                act.wait_ge(sem("max_rest"), b + 1)
                nc.scalar.activation(max_parts[:, 1, :], max_rest, ACT.Copy).then_inc(sem("max_part2"), 1)

            act.wait_ge(sem("split_done"), 8)
            for i in range(2):
                act.wait_ge(sem(f"parts_stored{i}"), 64)
            for b in range(B):
                split_maxima(b)
                for u in range(16 * b, 16 * b + 16):
                    w = (QT - u % 4) * P
                    for x in range(2):
                        act.wait_ge(sem("a_scores_t"), 2 * u + x + 1)
                        wait(act, sem("a_values"), u - 1)
                        nc.scalar.activation(PT[:, u % 2, 2 * x:2 * x + 2, 0:w], PS[:, 2 * x:2 * x + 2, 0:w],
                                             ACT.Exp).then_inc(sem("a_exp"), 1)
            act_xT(act, 0)
            act_sqrt(act, 1)
            act_b(act)

        @block.vector
        def _(dve):
            own = Chain(dve, sem("dve_own"))

            def to_q32(n):
                c, w, j = n // 4, n // 2 % 2, n % 2
                dve.wait_ge(sem("proj_done"), n + 1)
                if n == 0:
                    dve.wait_ge(sem("bias_in"), 16)
                nc.vector.tensor_scalar(q32[:, n % 2, :], PS[:, n, :], bqk0[:, w, j:j + 1], 0.25 if w == 0 else 1.0,
                                        ALU.add, ALU.mult).then_inc(sem("q32_ready"), 1)

            to_q32(0)
            to_q32(1)
            for n in range(8):
                dve.wait_ge(sem("part1_done"), n + 1)
                if n >= 1:
                    dve.wait_ge(sem("split_done"), n)
                nc.vector.tensor_tensor(rest, q32[:, n % 2, :], parts[:, n % 2, 0, :], ALU.subtract)\
                    .then_inc(sem("rest_ready"), 1)
                if n + 2 < 8:
                    dve.wait_ge(sem("rest_ready"), n + 1)
                    to_q32(n + 2)
                dve.wait_ge(sem("part2_done"), n + 1)
                nc.vector.tensor_tensor(parts[:, n % 2, 2, :], rest, parts[:, n % 2, 1, :], ALU.subtract)\
                    .then_inc(sem("split_done"), 1)
            dve.wait_ge(sem("bv_in"), 16)
            dve.wait_ge(sem("v_padded"), 2)
            for u in range(4):
                dve.wait_ge(sem("v_done"), u + 1)
                for t in range(2):
                    ins = nc.vector.tensor_tensor(
                        V32[:, 2 * u + t, :, 0:HD0], PS[:, u, t * D:(t + 1) * D].rearrange("p (h d) -> p h d", h=H),
                        biasrow[:, 0, :].rearrange("p (h d) -> p h d", h=H), ALU.add)
                ins.then_inc(sem("v_copied"), 1)
            dve.wait_ge(sem("x_in"), 16)
            dve.wait_ge(sem("bo_in"), 16)
            own.step(nc.vector.tensor_tensor(X[:, :, :], X[:, :, :],
                                             biasrow[:, 1, :].unsqueeze(1).to_broadcast([P, TT, D]), ALU.add))
            x_plus_bo = own.n

            def maxes(b, h, i):
                M = b * H * QT + QT * h + i
                dve.wait_ge(sem("a_scores"), M + 1)
                nc.vector.tensor_reduce(negmax0[:, b, bass.ds(QT * h + i, 1)], PS[:, 6 + i % 2, 0:(i + 1) * P], AX_X,
                                        ALU.max, negate=True).then_inc(sem("a_max"), 1)

            def split_maxima(b):
                dve.wait_ge(sem("max_part1"), b + 1)
                nc.vector.tensor_tensor(max_rest, PS[0:H * QT, 5, 0:P], max_parts[:, 0, :], ALU.subtract)\
                    .then_inc(sem("max_rest"), 1)
                dve.wait_ge(sem("max_part2"), b + 1)
                nc.vector.tensor_tensor(max_parts[:, 2, :], max_rest, max_parts[:, 1, :], ALU.subtract)\
                    .then_inc(sem("max_part3"), 1)

            def copy_ot(b, g):
                G = 4 * b + g
                dve.wait_ge(sem("a_values"), 4 * G + 4)
                wait(dve, sem("a_turned"), G)
                nc.vector.tensor_copy(OT, PS[:, 4, :]).then_inc(sem("a_ot"), 1)

            def normalise(b, g):
                G = 4 * b + g
                dve.wait_ge(sem("a_turned"), G + 1)
                o = PS[:, 5, :].rearrange("p (i c d) -> p i c d", i=QT, c=4)
                nc.vector.reciprocal(rinv0[:, :].rearrange("p (i c) -> p i c", i=QT), o[:, :, :, HD0])\
                    .then_inc(sem("a_rinv"), 1)
                dve.wait_ge(sem("a_rinv"), G + 1)
                nc.vector.tensor_tensor(
                    AO[:, 4 * b:4 * b + 4, 4 * g * HD0:4 * (g + 1) * HD0].rearrange("p i (c d) -> p i c d", c=4),
                    o[:, :, :, 0:HD0],
                    rinv0[:, :].rearrange("p (i c) -> p i c", i=QT).unsqueeze(3).to_broadcast([P, QT, 4, HD0]),
                    ALU.mult).then_inc(sem("a_out"), 1)

            for i in range(QT):
                maxes(0, 0, i)
            with dve.Fori(1, H) as h:
                for i in range(QT):
                    maxes(0, h, i)
            split_maxima(0)
            ahead = [(1, h, i) for h in range(H) for i in range(QT)]
            for n in range(12):
                maxes(*ahead.pop(0))
            for b in range(B):
                if b == 1:
                    split_maxima(1)
                for g in range(4):
                    for j in range(QT):
                        for n in range(min(4, len(ahead))):
                            maxes(*ahead.pop(0))
                        if j == 0 and g > 0:
                            normalise(b, g - 1)
                    copy_ot(b, g)
                normalise(b, 3)
            dve.wait_ge(sem("dve_own"), x_plus_bo)
            for t in range(TT):
                if t % 2 == 0:
                    dve.wait_ge(sem("a_proj"), t + 2)
                    own.step(nc.vector.tensor_tensor(
                        R[:, t:t + 2, :], PS[:, 4 + t // 2, :].rearrange("p (t n) -> p t n", t=2),
                        X[:, t:t + 2, :], ALU.add))
            dve_norm(dve, own, 1)
            dve_b(dve, own)



def lay_out(arrays, w):
    import numpy as np
    turned = np.ascontiguousarray
    arrays["router_w0"] = turned(w["L0_ffn_router_w"].T)
    arrays["L0_w_gate_up"] = w["L0_ffn_w_gate_up"]
    arrays["L0_w_down"] = w["L0_ffn_w_down"]
    arrays["L0_shared_gate_up"] = w["L0_ffn_shared_gate_up"]
    arrays["L0_shared_down"] = w["L0_ffn_shared_down"]
    for name in ("Wq", "Wk", "Wkg1", "Wkg2", "Wo"):
        arrays[f"L1_attn_{name}T"] = turned(w["L1_attn_" + name].T)
    arrays["L1_attn_WvgT"] = turned(np.concatenate([w["L1_attn_Wv"], w["L1_attn_Wg"]]).T)
    arrays["L1_attn_bkg2"] = w["L1_attn_bkg2"]
    arrays["L1_attn_bg"] = w["L1_attn_bg"]
    def by_head(a):
        return a.reshape(KD, P, H, P).transpose(2, 1, 0, 3)

    arrays["w_qkv1"] = turned(np.stack([by_head(w["L1_ffn_wq"]), by_head(w["L1_ffn_wk"]), by_head(w["L1_ffn_wv"])],
                                       axis=2).reshape(H, P, 3 * KD * P))
    arrays["w_o1"] = turned(w["L1_ffn_wo"].reshape(H // 2, 2, P, D).transpose(0, 2, 1, 3).reshape(H // 2, P, 2 * D))
    arrays["L1_ffn_ln1_w"], arrays["L1_ffn_ln2_w"] = w["L1_ffn_ln1_w"], w["L1_ffn_ln2_w"]
    arrays["gate_w1"] = turned(w["L1_ffn_gate_w"].T)

    def gate_up(g, u):
        gu = np.concatenate([g, u], axis=-2)
        gu = np.moveaxis(gu, -1, -2).reshape(*gu.shape[:-2], KD, P, gu.shape[-2])
        return np.moveaxis(gu, -2, -3)

    gu = gate_up(w["L1_ffn_eg_w"], w["L1_ffn_eu_w"]).reshape(E1, P, -1)
    dn = w["L1_ffn_ed_w"].transpose(0, 2, 1).reshape(E1, 2, F1 // 2, D)
    dn = np.concatenate([dn, np.zeros((E1, 2, P - F1 // 2, D), dn.dtype)], axis=2)
    dn = dn.transpose(0, 2, 1, 3).reshape(E1, P, 2 * D)
    arrays["w_experts1"] = turned(np.concatenate([gu, dn], axis=2).transpose(1, 0, 2))
    arrays["w_shared_gu1"] = turned(gate_up(w["L1_ffn_sg_w"], w["L1_ffn_su_w"]).reshape(P, -1))
    sd = w["L1_ffn_sd_w"].T
    sd = np.concatenate([sd, np.zeros((3 * P - FS1, D), sd.dtype)]).reshape(3, P, D)
    arrays["w_shared_dn1"] = turned(sd.transpose(1, 0, 2).reshape(P, 3 * D))


def _constants():
    import numpy as np
    bf = mybir.dt.np(BF16)
    start = 2.0 ** (-8.0 / H)
    slopes = np.array([start * start ** i for i in range(H)], dtype=np.float32)
    parts, left = [], slopes.copy()
    for _ in range(3):
        part = left.astype(bf)
        parts.append(part)
        left = left - part.astype(np.float32)
    pos = np.arange(S)
    pos_parts = [(pos // 256 * 256).astype(bf), (pos % 256).astype(bf)]
    q_rows, k_rows = np.zeros((2, H, P - 96, S), bf)
    for i in range(3):
        for j in range(2):
            r = 2 * i + j
            q_rows[:, r, :], k_rows[:, r, :] = parts[i][:, None], pos_parts[j][None, :]
            q_rows[:, 6 + r, :], k_rows[:, 6 + r, :] = pos_parts[j][None, :], -parts[i][:, None]
    route = np.zeros((P, RC_WORDS), np.float32)
    route[:, 0:16] = np.arange(16)
    route[:, 16:24] = P * np.arange(8)
    route[:, 24:24 + N_TILES0] = np.arange(N_TILES0)
    route[:, 128:256] = np.arange(P)[:, None] < np.arange(P)[None, :]
    route[:, 256:384] = 1.0
    feature, token = np.arange(P), np.arange(T)
    gla = np.concatenate([feature[:, None] // 8 == np.arange(H)[None, :],
                          feature[:, None] // 8 == np.arange(D)[None, :] // 16,
                          feature[:, None] % CH <= np.arange(CH)[None, :]], axis=1).astype(np.float32)
    k_rows[:, 12:15, :] = 1
    mask = np.where(np.arange(P)[None, :] > np.arange(P)[:, None], -1e30, 0.0).astype(bf)
    return {
        "masktb": np.ascontiguousarray(mask.T),
        "run": (token % CH != 0).astype(np.float32), "gla_consts": gla,
        "route_consts": route,
        "ident": np.eye(P, dtype=np.float32),
        "identb": np.eye(P, dtype=np.float32).astype(bf),
        "maskb": mask,
        "q_bias_rows": q_rows, "k_bias_rows": k_rows,
    }


def kernel(**inputs):
    import numpy as _np
    import concourse.bacc as _bacc
    from concourse import mybir as _mybir
    from concourse.bass_utils import run_bass_kernel_spmd as _run

    w = {k: _np.ascontiguousarray(v) for k, v in inputs.items()}
    arrays = _constants()
    x = w["L0_attn_x"].reshape(T, D)
    arrays["x"] = x
    arrays["xT"] = _np.ascontiguousarray(x.T)
    arrays["bqk0"] = _np.ascontiguousarray(
        _np.stack([w["L0_attn_bq"], w["L0_attn_bk"]]).reshape(2, KD, P).transpose(2, 0, 1))
    for name in ("wq", "wk", "wv", "wo", "bv", "bo"):
        arrays["L0_attn_" + name] = w["L0_attn_" + name]
    lay_out(arrays, w)

    nc = _bacc.Bacc("TRN2", target_bir_lowering=False, num_devices=1)
    io, fed = {}, {}
    for name, a in arrays.items():
        fed[f"in_{name}"] = a
        io[name] = nc.dram_tensor(f"in_{name}", a.shape, _mybir.dt.from_np(a.dtype), kind="ExternalInput").ap()
    out = nc.dram_tensor("out", (T, D), F32, kind="ExternalOutput").ap()
    program(nc, io, out)
    r = _run(nc, [fed], core_ids=[0])
    return r.results[0]["out"].reshape(B, S, D)
```

```python
from contextlib import ExitStack

import concourse.bass as bass
from concourse import mybir

F32 = mybir.dt.float32
F32R = mybir.dt.float32r
BF16 = mybir.dt.bfloat16
I32 = mybir.dt.int32
U32 = mybir.dt.uint32
ALU = mybir.AluOpType
ACT = mybir.ActivationFunctionType
AX_X = mybir.AxisListType.X

P = 128
B, S, D = 2, 512, 256
T = B * S
TT = T // P
KD = D // P
QT = S // P
H = 16
GROUPS = B * H // 4
HD0 = D // H
LN_EPS = 1e-5
E0, F0 = 8, 512
W0_SLOT = KD * 2 * F0 + F0 // P * D
N_TILES0 = T // P + E0 - 1
RC_WORDS = 384
CH = 64
NCH = T // CH
KSCALE = 128.0 ** -0.5
QSCALE1 = 128.0 ** -0.5
RMS_EPS = 1e-6
E1, K1, F1, FS1 = 16, 6, 176, 352
W1_SLOT = KD * 2 * F1 + 2 * D
W1_SHARED = KD * 2 * FS1 + 3 * D
CW_AT = 7072
ARENA = 43008
HL = ("high", "low")
FR_AT = 16384
WD_HL_AT = 34944


def wait(eng, sem, value):
    if isinstance(value, int) and value <= 0:
        return
    eng.wait_ge(sem, value)


class Chain:

    def __init__(self, eng, sem, at=0):
        self.eng, self.sem, self.n = eng, sem, at

    def step(self, ins):
        ins.then_inc(self.sem, 1)
        self.n = self.n + 1
        return self.n

    def wait(self, n=None):
        self.eng.wait_ge(self.sem, self.n if n is None else n)


def program(nc, io, out):
    with ExitStack() as ctx:
        sems = {}

        def sem(name):
            if name not in sems:
                sems[name] = ctx.enter_context(nc.semaphore(name))
            return sems[name]

        def sb(name, shape, dt=F32):
            return ctx.enter_context(nc.sbuf_tensor(name, shape, dt))

        PS = ctx.enter_context(nc.psum_tensor("PS", [P, 8, 512], F32))

        X = sb("X", [P, TT, D])
        XT = sb("XT", [P, KD, T])
        R = sb("R", [P, TT, D])
        ident = sb("ident", [P, P])
        identb = sb("identb", [P, P], BF16)
        maskb = sb("maskb", [P, P], BF16)
        bn = sb("bn", [P, TT, 6])
        mv = sb("mv", [P, TT, 2])
        sd = sb("sd", [P, TT])
        rstd = sb("rstd", [P, TT])
        var = sb("var", [P, TT])
        eps5 = sb("eps5", [P, 1])
        table_use = sb("table_use", [P, 1])
        negmax = sb("negmax", [P, 8])
        rowsum = sb("rowsum", [P, 8])
        rinv = sb("rinv", [P, 8])
        biasrow = sb("biasrow", [P, 4, D])
        bqk0 = sb("bqk0", [P, 2, KD])

        with nc.sbuf_tensor("A", [P, ARENA], F32) as A:
            pass
        sb("A_front", [P, FR_AT])
        XT_HL = [sb(f"XT_{n}", [P, KD, T], F32R) for n in HL]
        W_HL = [[sb(f"W1_{n}{i}", [P, W1_SLOT], F32R) for n in HL] for i in range(2)]
        HT_HL = [sb(f"HT_{n}", [P, 2, 2 * P], F32R) for n in HL]
        E_END = FR_AT + 2 * KD * T + 4 * W1_SLOT + 8 * P
        sb("A_middle", [P, WD_HL_AT - E_END])
        WD_HL = [[sb(f"WD_{n}{i}", [P, 3, KD, P], F32R) for n in HL] for i in range(2)]
        sb("A_end", [P, ARENA - WD_HL_AT - 4 * 3 * D])

        def cut(at, words, dt=F32):
            v = A[:, at:at + words]
            return v if dt == F32 else v.bitcast(dt)

        W_A = [cut(19456 + 512 * n, 512).rearrange("p (k n) -> p k n", k=KD) for n in range(4)]
        QK6 = [cut(21504 + 8192 * w, 8192, BF16) for w in range(2)]
        V32 = cut(15360, TT * H * 32).rearrange("p (t h d) -> p t h d", t=TT, h=H)
        PT = cut(37888, 2 * 2048).rearrange("p (i c n) -> p i c n", i=2, c=4)
        OT = cut(41984, 512)
        max_rest = cut(42496, P)[0:4 * QT, :]
        max_parts = cut(42624, 384, BF16)[0:4 * QT, :].rearrange("p (i q n) -> p i q n", i=2, q=3)
        negmax0 = sb("negmax0", [P, B, H * QT])
        rinv0 = sb("rinv0", [P, QT * 4])
        max_rows = nc.dram_tensor("max_rows", (GROUPS, 3, 4 * QT, P), BF16, kind="Internal").ap()
        masktb = sb("masktb", [P, P], BF16)
        q32 = cut(0, 8 * S).rearrange("p (i n) -> p i n", i=8)
        parts = cut(8 * S, 12 * S, BF16).rearrange("p (i q n) -> p i q n", i=8, q=3)
        rest = cut(20 * S, 2 * S).rearrange("p (i n) -> p i n", i=2)
        AO = R
        scratch = nc.dram_tensor("qk_parts", (2, 3, D, T), BF16, kind="Internal").ap()

        def W_B(slot):
            at = W0_SLOT * slot
            return (cut(at, KD * 2 * F0).rearrange("p (k n) -> p k n", k=KD),
                    cut(at + KD * 2 * F0, F0 // P * D).rearrange("p (j n) -> p j n", j=F0 // P))

        XS0 = R
        XI = cut(37888, 2 * D).rearrange("p (i n) -> p i n", i=2)
        XIT = cut(38400, 2 * D).rearrange("p (i k t) -> p i k t", i=2, k=KD)
        YO = cut(38912, 2 * D).rearrange("p (i n) -> p i n", i=2)
        SG = cut(39936, 2 * F0).rearrange("p (i n) -> p i n", i=2)
        HB = cut(40960, 2 * F0).rearrange("p (i n) -> p i n", i=2)
        HBT = cut(41984, 2 * F0).rearrange("p (i n) -> p i n", i=2)
        YR = cut(TT * D, TT * D).rearrange("p (t n) -> p t n", t=TT)
        rw0 = sb("rw0", [P, KD, E0])
        rc = sb("rc", [P, RC_WORDS])
        iota_e = rc[:, 0:16]
        tile_sizes = rc[:, 16:24]
        iota_j = rc[:, 24:24 + N_TILES0]
        same_expert = rc[:, 40:40 + E0 * TT]
        before = rc[:, 128:256]
        ones = rc[:, 256:384]
        lg = sb("lg", [P, TT, E0])
        mx = sb("mx", [P, TT, 8])
        ix = sb("ix", [P, TT, 8], U32)
        ixf = sb("ixf", [P, TT])
        oh = sb("oh", [P, TT, E0])
        en = sb("en", [P, TT])
        gate = sb("gate", [P, TT])
        cmp0 = sb("cmp0", [P, E0, 8])
        upto = sb("upto", [P, E0 * TT])
        earlier = sb("earlier", [P, E0, TT])
        nt = sb("nt", [P, E0])
        incl = sb("incl", [P, E0])
        first_row = sb("first_row", [P, E0])
        base = sb("base", [P, TT, E0])
        slotf = sb("slotf", [P, TT])
        slot = sb("slot", [P, TT], U32)
        cmpj = sb("cmpj", [1, N_TILES0, E0])
        texf = sb("texf", [1, N_TILES0])
        tile_at = sb("tile_at", [1, N_TILES0], I32)
        zeros = sb("zeros", [P, D])
        at_c = 27648
        wq1, wk1 = (cut(at_c + 256 * n, 256).rearrange("p (k n) -> p k n", k=KD) for n in range(2))
        wkg1 = cut(at_c + 512, 32).rearrange("p (k n) -> p k n", k=KD)
        wkg2 = cut(at_c + 544, P)[0:16, :]
        wvg = cut(at_c + 672, 1024).rearrange("p (k n) -> p k n", k=KD)
        wo1 = cut(at_c + 1696, 512).rearrange("p (k n) -> p k n", k=KD)
        run = cut(at_c + 2208, T)
        own_head = cut(at_c + 3232, H)
        own_block = cut(at_c + 3248, D)
        causal = cut(at_c + 3504, CH)
        bkg = cut(at_c + 3568, 1)
        ga, gb, gc_, gd, ge = (cut(21632 + T * n, T) for n in range(5))
        QX = [ga, gb]
        ATS = [cut(12288 + 2048 * n, 2048).rearrange("p (h t) -> p h t", h=H) for n in range(2)]
        VC32 = cut(16384, TT * H * 32).rearrange("p (t h d) -> p t h d", t=TT, h=H)
        OTC = cut(20480, 512)
        kg1 = cut(31728, T)[0:16, :]
        e1, e2, e3, e4 = (cut(32752 + T * n, T) for n in range(4))
        VG = cut(36848, TT * 2 * D).rearrange("p (t n) -> p t n", t=TT)
        V1, GP = VG[:, :, 0:D], VG[:, :, D:2 * D]
        KH = cut(40944, TT * P).rearrange("p (t n) -> p t n", t=TT)
        ST = [cut(4096 + 512 * n, 512) for n in range(2)]
        UP = cut(42480, D)
        dec = sb("dec", [P, NCH])
        gsum = sb("gsum", [P, TT * H])
        gvar = sb("gvar", [P, TT * H])
        PRODUCTS = [(0, 0), (0, 1), (1, 0)]
        WD = [cut(10240 + 768 * n, 768).rearrange("p (w k n) -> p w k n", w=3, k=KD) for n in range(2)]
        QKT = [cut(23168 + 2048 * n, 2048).rearrange("p (w t) -> p w t", w=2) for n in range(2)]
        VH = [cut(27264 + 1024 * n, 1024).rearrange("p (t d) -> p t d", t=TT) for n in range(2)]
        AOT = cut(29312, 2048).rearrange("p (g t) -> p g t", g=2)
        WOP = cut(11776, 512).rearrange("p (g n) -> p g n", g=2)
        PB1 = cut(31872, 2048).rearrange("p (i n) -> p i n", i=4)
        PTS1 = cut(33920, 1024).rearrange("p (i n) -> p i n", i=2)
        HN = cut(4608, TT * D).rearrange("p (t n) -> p t n", t=TT)
        sq = cut(6656, D)
        ssq = sb("ssq", [P, TT])
        eps6 = sb("eps6", [P, 1])
        W1R = [cut(W1_SLOT * n, W1_SLOT) for n in range(2)]
        WSH1 = cut(2 * W1_SLOT, W1_SHARED)
        SG1 = cut(8000, 2 * FS1).rearrange("p (i n) -> p i n", i=2)
        HB1 = cut(8704, 2 * FS1).rearrange("p (i n) -> p i n", i=2)
        HBT1 = cut(9408, 2 * 384).rearrange("p (i n) -> p i n", i=2)
        rw1 = cut(6912, KD * E1).rearrange("p (k e) -> p k e", k=KD)
        lg1 = cut(6944, TT * E1).rearrange("p (t e) -> p t e", t=TT)
        cw = cut(CW_AT, TT * E1).rearrange("p (t e) -> p t e", t=TT)
        OH1 = cut(7200, TT * K1 * E1).rearrange("p (t k e) -> p t k e", t=TT, k=K1)
        zsum = sb("zsum", [P, TT])
        ixf1 = sb("ixf1", [P, TT, 8])
        xs_rows = nc.dram_tensor("xs_rows", (N_TILES0 * P, D), F32, kind="Internal").ap()
        y_rows = nc.dram_tensor("y_rows", (N_TILES0 * P, D), F32, kind="Internal").ap()

        block = ctx.enter_context(nc.Block())

        Q_SLOT = [0, 0, 1, 1, 0, 2]
        K_SLOT = [0, 1, 0, 1, 2, 0]

        def dve_norm(dve, own, phase, add):
            for c in range(B):
                tiles = range(QT * c, QT * (c + 1))
                part = slice(QT * c, QT * (c + 1))
                add(c)
                own.wait()
                for t in tiles:
                    own.step(nc.vector.bn_stats(bn[:, t, :], R[:, t, :]))
                own.wait()
                for t in tiles:
                    own.step(nc.vector.bn_aggr(mv[:, t, :], bn[:, t, :]))
                own.wait()
                nc.vector.tensor_copy(var[:, part], mv[:, part, 1]).then_inc(sem("var_ready"), 1)
                dve.wait_ge(sem("sd_ready"), B * (phase - 1) + c + 1)
                own.step(nc.vector.reciprocal(rstd[:, part], sd[:, part]))
                own.wait()
                for t in tiles:
                    nc.vector.tensor_scalar(X[:, t, :], R[:, t, :], mv[:, t, 0:1], rstd[:, t:t + 1],
                                            ALU.subtract, ALU.mult).then_inc(sem("x_ready"), 1)

        def load_table(function):
            nc.scalar.activation(table_use[:, :], eps5[:, :], function)

        def act_sqrt(act, phase):
            if phase == 1:
                act.wait_ge(sem("eps_set"), 2)
            load_table(ACT.Sqrt)
            for c in range(B):
                act.wait_ge(sem("var_ready"), B * (phase - 1) + c + 1)
                nc.scalar.activation(sd[:, QT * c:QT * (c + 1)], var[:, QT * c:QT * (c + 1)], ACT.Sqrt, bias=eps5[:, :])\
                    .then_inc(sem("sd_ready"), 1)

        N_IT = TT + N_TILES0

        def stream(eng, step, start=0, peel=TT + 4):
            for n in range(start, peel):
                step(n, n % 2, n // 2)
            pairs = (N_IT - peel - 2) // 2
            with eng.Fori(peel // 2, peel // 2 + pairs) as j:
                for p in range(2):
                    step(2 * j + p, p, j)
            for n in range(peel + 2 * pairs, N_IT):
                step(n, n % 2, n // 2)

        def sp_b(sp):
            def load(n, p):
                at = (n - TT) * P if isinstance(n, int) else sp.snap((n - TT) * P)
                wait(sp, sem("b_xturned"), n - TT - 1)
                sp.dma_start(XI[:, p, :], xs_rows[bass.ds(at, P), :]).then_inc(sem(f"xi_in{p}"), 16)

            def store(n, p):
                at = (n - TT) * P if isinstance(n, int) else sp.snap((n - TT) * P)
                sp.wait_ge(sem("b_y"), n + 1)
                sp.dma_start(y_rows[bass.ds(at, P), :], YO[:, p, :]).then_inc(sem(f"y_stored{p}"), 16)

            def step(n, p, half):
                if not (isinstance(n, int) and n + 2 >= N_IT):
                    load(n + 2, p)
                if not (isinstance(n, int) and n < TT + 2):
                    store(n - 2, p)

            sp.wait_ge(sem("rows_scattered"), 16 * TT)
            load(TT, 0)
            load(TT + 1, 1)
            stream(sp, step, start=TT)
            store(N_IT - 2, N_IT % 2)
            store(N_IT - 1, 1 - N_IT % 2)
            sp.wait_ge(sem("b_down"), N_IT)
            sp_c(sp)

        def pool_b(pool):
            pool.wait_ge(sem("slots"), 1)
            pool.wait_ge(sem("gated"), 1)
            for t in range(TT):
                nc.gpsimd.indirect_dma_start(
                    out=xs_rows[:, :], out_offset=bass.IndirectOffsetOnAxis(ap=slot[:, t:t + 1], axis=0),
                    in_=XS0[:, t, :], in_offset=None).then_inc(sem("rows_scattered"), 16)
            pool.wait_ge(sem("y_stored0"), 16 * (N_TILES0 // 2 + 1))
            pool.wait_ge(sem("y_stored1"), 16 * (N_TILES0 // 2))
            pool.wait_ge(sem("b_down"), N_IT)
            for t in range(TT):
                nc.gpsimd.indirect_dma_start(
                    out=YR[:, t, :], out_offset=None, in_=y_rows[:, :],
                    in_offset=bass.IndirectOffsetOnAxis(ap=slot[:, t:t + 1], axis=0))\
                    .then_inc(sem(f"yr_in{t // QT}"), 16)
            pool_c(pool)

        def pe_b(pe):
            pe_transpose_tokens(pe, X, "x_ready", lambda t: t + 1)
            pe.wait_ge(sem("route_in"), 32)
            pe.wait_ge(sem("xT_ready"), 4)
            for t in range(TT):
                for k in range(KD):
                    ins = nc.tensor.matmul(PS[:, 4, t * E0:(t + 1) * E0], XT[:, k, t * P:(t + 1) * P], rw0[:, k, :],
                                           start=k == 0, stop=k == KD - 1)
            ins.then_inc(sem("logits"), 1)

            def rank():
                pe.wait_ge(sem("onehot"), 1)
                for j, earlier in enumerate((before, ones)):
                    ins = nc.tensor.matmul(PS[:, 7, j * TT * E0:(j + 1) * TT * E0], earlier, oh[:, :, :],
                                           start=True, stop=True)
                ins.then_inc(sem("ranks"), 1)

            def turn_x(n, p, half):
                pe.wait_ge(sem(f"xi_in{p}"), 16 * (half - TT // 2) + 16)
                wait(pe, sem("b_xit"), n - TT)
                for k in range(KD):
                    ins = nc.tensor.transpose(PS[:, 6, k * P:(k + 1) * P],
                                              XI[:, p, k * P:(k + 1) * P], ident[:, :])
                ins.then_inc(sem("b_xturned"), 1)

            def gate_up(n, p, half):
                shared = isinstance(n, int) and n < TT
                if shared:
                    at = 0
                else:
                    pe.wait_ge(sem("b_xit"), n - TT + 1)
                    at = pe.value_load(tile_at[0:1, bass.ds(n - TT, 1)], min_val=0, max_val=W0_SLOT * E0)
                for g in range(2):
                    wait(pe, sem("b_silu" if g == 0 else "b_h"), n - 1)
                    for k in range(KD):
                        ins = nc.tensor.matmul(PS[:, 2 * g + p, :],
                                               XT[:, k, n * P:(n + 1) * P] if shared else XIT[:, p, k, :],
                                               A[:, bass.ds(at + (k * 2 + g) * F0, F0)],
                                               start=k == 0, stop=k == KD - 1)
                    ins.then_inc(sem("b_gate" if g == 0 else "b_up"), 1)

            def turn_h(n, p, half):
                pe.wait_ge(sem("b_h"), n + 1)
                wait(pe, sem("b_ht"), n - 1)
                for j in range(F0 // P):
                    ins = nc.tensor.transpose(PS[:, 4 + p, j * P:(j + 1) * P], HB[:, p, j * P:(j + 1) * P], ident[:, :])
                ins.then_inc(sem("b_hturned"), 1)

            def down(n, p, at):
                pe.wait_ge(sem("b_ht"), n + 1)
                wait(pe, sem("b_y"), n)
                for j in range(F0 // P):
                    ins = nc.tensor.matmul(PS[:, 7, 0:D], HBT[:, p, j * P:(j + 1) * P],
                                           A[:, bass.ds(at + KD * 2 * F0 + j * D, D)],
                                           start=j == 0, stop=j == F0 // P - 1)
                ins.then_inc(sem("b_down"), 1)

            def weights_at(n):
                if isinstance(n, int) and n < TT:
                    return 0
                return pe.value_load(tile_at[0:1, bass.ds(n - TT, 1)], min_val=0, max_val=W0_SLOT * E0)

            def step(n, p, half):
                if isinstance(n, int) and n == TT:
                    pe.wait_ge(sem("tile_table"), 1)
                    pe.wait_ge(sem("w_routed0"), 32 * E0)
                gate_up(n, p, half)
                if not (isinstance(n, int) and n < 2):
                    at = weights_at(n - 2)
                if not (isinstance(n, int) and (n + 1 < TT or n == N_IT - 1)):
                    turn_x(n + 1, 1 - p, half + p)
                if isinstance(n, int) and n == 0:
                    rank()
                    return
                turn_h(n - 1, 1 - p, half - (1 - p))
                if isinstance(n, int) and n == 2:
                    pe.wait_ge(sem("slots"), 1)
                if not (isinstance(n, int) and n < 2):
                    down(n - 2, p, at)

            pe.wait_ge(sem("w_shared0"), 32)
            stream(pe, step)
            n = N_IT - 1
            turn_h(n, n % 2, n // 2)
            down(n - 1, 1 - n % 2, weights_at(n - 1))
            down(n, n % 2, weights_at(n))
            pe_c(pe)

        def act_xT(act, nth, batches=range(B)):
            for c in batches:
                act.wait_ge(sem("tokens_turned"), 2 * nth + c + 1)
                nc.scalar.activation(XT[:, :, c * S:(c + 1) * S], PS[:, 2 * c:2 * c + 2, :], ACT.Copy)\
                    .then_inc(sem("xT_ready"), 1)

        def act_b(act):
            act.wait_ge(sem("a_proj"), TT)
            act_xT(act, 1)
            act.wait_ge(sem("top1"), 1)
            nc.scalar.activation(en[:, :], mx[:, :, 0], ACT.Exp, scale=-1.0).then_inc(sem("exp_neg"), 1)

            def copy_ht(n, p, half):
                act.wait_ge(sem("b_hturned"), n + 1)
                wait(act, sem("b_down"), n - 1)
                nc.scalar.activation(HBT[:, p, :], PS[:, 4 + p, :], ACT.Copy).then_inc(sem("b_ht"), 1)

            def step(n, p, half):
                act.wait_ge(sem("b_gate"), n + 1)
                wait(act, sem("b_h"), n - 1)
                nc.scalar.activation(SG[:, p, :], PS[:, p, :], ACT.Silu).then_inc(sem("b_silu"), 1)
                if not (isinstance(n, int) and n < 1):
                    copy_ht(n - 1, 1 - p, half)

            stream(act, step)
            copy_ht(N_IT - 1, (N_IT - 1) % 2, 0)
            act_sqrt(act, 2)
            act_c(act)

        def dve_b(dve, own):
            dve.wait_ge(sem("logits"), 1)
            own.step(nc.vector.tensor_copy(lg[:, :, :], PS[:, 4, 0:TT * E0].rearrange("p (t e) -> p t e", e=E0)))
            own.wait()
            for t in range(TT):
                own.step(nc.vector.max(mx[:, t, :], lg[:, t, :]))
            own.wait()
            for t in range(TT):
                own.step(nc.vector.max_index(ix[:, t, :], mx[:, t, :], lg[:, t, :]))
            own.wait()
            nc.vector.tensor_copy(ixf[:, :], ix[:, :, 0]).then_inc(sem("top1"), 1)
            dve.wait_ge(sem("top1"), 1)
            dve.wait_ge(sem("route_in"), 32)
            nc.vector.tensor_tensor(oh[:, :, :], ixf[:, :].unsqueeze(2).to_broadcast([P, TT, E0]),
                                    iota_e[:, 0:E0].unsqueeze(1).to_broadcast([P, TT, E0]), ALU.is_equal)\
                .then_inc(sem("onehot"), 1)
            dve.wait_ge(sem("exp_neg"), 1)
            own.step(nc.vector.tensor_scalar(en[:, :], en[:, :], 1.0, None, ALU.add))
            own.wait()
            own.step(nc.vector.reciprocal(gate[:, :], en[:, :]))
            own.wait()
            nc.vector.tensor_tensor(XS0[:, :, :], X[:, :, :], gate[:, :].unsqueeze(2).to_broadcast([P, TT, D]),
                                    ALU.mult).then_inc(sem("gated"), 1)

            def find_slots():
                in_tile = PS[:, 7, TT * E0:2 * TT * E0].rearrange("p (t e) -> p e t", e=E0)
                dve.wait_ge(sem("ranks"), 1)
                own.step(nc.vector.tensor_copy(cmp0[:, :, :], in_tile))
                own.wait()
                own.step(nc.vector.tensor_tensor_scan(upto[:, :], same_expert, cmp0.rearrange("p e t -> p (e t)"), 0.0,
                                                      ALU.mult, ALU.add))
                own.wait()
                by_expert = upto[:, :].rearrange("p (e t) -> p e t", e=E0)
                own.step(nc.vector.tensor_tensor(earlier[:, :, :], by_expert, cmp0[:, :, :], ALU.subtract))
                own.wait()
                own.step(nc.vector.tensor_tensor(
                    cmp0[:, :, :], by_expert[:, :, TT - 1:TT].to_broadcast([P, E0, 8]),
                    tile_sizes.unsqueeze(1).to_broadcast([P, E0, 8]), ALU.is_gt))
                own.wait()
                own.step(nc.vector.tensor_reduce(nt[:, :], cmp0[:, :, :], AX_X, ALU.add))
                own.wait()
                own.step(nc.vector.tensor_tensor_scan(incl[:, :], ones[:, 0:E0], nt[:, :], 0.0, ALU.mult, ALU.add))
                own.wait()
                own.step(nc.vector.tensor_tensor(first_row[:, :], incl[:, :], nt[:, :], ALU.subtract))
                own.step(nc.vector.tensor_tensor(
                    cmpj[:, :, :], incl[0:1, :].unsqueeze(1).to_broadcast([1, N_TILES0, E0]),
                    iota_j[0:1, :].unsqueeze(2).to_broadcast([1, N_TILES0, E0]), ALU.is_le))
                own.wait()
                own.step(nc.vector.tensor_scalar(first_row[:, :], first_row[:, :], float(P), None, ALU.mult))
                own.step(nc.vector.tensor_reduce(texf[:, :], cmpj[:, :, :], AX_X, ALU.add))
                own.wait()
                own.step(nc.vector.tensor_tensor(
                    base[:, :, :], PS[:, 7, 0:TT * E0].rearrange("p (t e) -> p t e", e=E0),
                    first_row[:, :].unsqueeze(1).to_broadcast([P, TT, E0]), ALU.add))
                own.step(nc.vector.tensor_scalar(texf[:, :], texf[:, :], float(E0 - 1), 1.0, ALU.min, ALU.add))
                own.wait()
                own.step(nc.vector.tensor_tensor(base[:, :, :], base[:, :, :],
                                                 earlier[:, :, :].rearrange("p e t -> p t e"), ALU.add))
                nc.vector.tensor_scalar(tile_at[:, :], texf[:, :], float(W0_SLOT), None, ALU.mult)\
                    .then_inc(sem("tile_table"), 1)
                own.wait()
                own.step(nc.vector.tensor_tensor(base[:, :, :], base[:, :, :], oh[:, :, :], ALU.mult))
                own.wait()
                own.step(nc.vector.tensor_reduce(slotf[:, :], base[:, :, :], AX_X, ALU.add))
                own.wait()
                nc.vector.tensor_copy(slot[:, :], slotf[:, :]).then_inc(sem("slots"), 1)

            def copy_xit(n, p, half):
                dve.wait_ge(sem("b_xturned"), n - TT + 1)
                wait(dve, sem("b_up"), n - 1)
                nc.vector.tensor_copy(XIT[:, p, :, :], PS[:, 6, 0:D].rearrange("p (k t) -> p k t", k=KD))\
                    .then_inc(sem("b_xit"), 1)

            def copy_y(n, p, half):
                dve.wait_ge(sem("b_down"), n + 1)
                if isinstance(n, int) and n < TT:
                    nc.vector.tensor_tensor(X[:, n, :], X[:, n, :], PS[:, 7, 0:D], ALU.add).then_inc(sem("b_y"), 1)
                    return
                wait(dve, sem(f"y_stored{p}"), 16 * (half - TT // 2))
                nc.vector.tensor_copy(YO[:, p, :], PS[:, 7, 0:D]).then_inc(sem("b_y"), 1)

            def step(n, p, half):
                dve.wait_ge(sem("b_silu"), n + 1)
                dve.wait_ge(sem("b_up"), n + 1)
                wait(dve, sem("b_hturned"), n - 1)
                nc.vector.tensor_tensor(HB[:, p, :], SG[:, p, :], PS[:, 2 + p, :], ALU.mult).then_inc(sem("b_h"), 1)
                if isinstance(n, int) and n == 0:
                    find_slots()
                if not (isinstance(n, int) and (n + 1 < TT or n == N_IT - 1)):
                    copy_xit(n + 1, 1 - p, half + p)
                if not (isinstance(n, int) and n < 2):
                    copy_y(n - 2, p, half - 1)

            stream(dve, step)
            n = N_IT - 1
            copy_y(n - 1, (n - 1) % 2, (n - 1) // 2)
            copy_y(n, n % 2, n // 2)
            dve.wait_ge(sem("rows_scattered"), 16 * TT)
            dve.wait_ge(sem("b_y"), TT)

            def add(c):
                dve.wait_ge(sem(f"yr_in{c}"), 16 * QT)
                own.step(nc.vector.tensor_tensor(R[:, QT * c:QT * (c + 1), :], X[:, QT * c:QT * (c + 1), :],
                                                 YR[:, QT * c:QT * (c + 1), :], ALU.add))

            dve_norm(dve, own, 2, add)
            dve_c(dve, own)

        def sp_c(sp):
            loads = [(wq1, io["L1_attn_WqT"].rearrange("(k p) n -> p k n", p=P)),
                     (wk1, io["L1_attn_WkT"].rearrange("(k p) n -> p k n", p=P)),
                     (wkg1, io["L1_attn_Wkg1T"].rearrange("(k p) n -> p k n", p=P)),
                     (wkg2, io["L1_attn_Wkg2T"]),
                     (wvg, io["L1_attn_WvgT"].rearrange("(k p) n -> p k n", p=P)),
                     (wo1, io["L1_attn_WoT"].rearrange("(k p) n -> p k n", p=P)),
                     (run, io["run"].rearrange("(o n) -> o n", o=1).to_broadcast([P, T])),
                     (cut(at_c + 3232, H + D + CH), io["gla_consts"]),
                     (bkg, io["L1_attn_bkg2"].rearrange("(p o) -> p o", o=1)),
                     (biasrow[:, 0, :], io["L1_attn_bg"].rearrange("(o n) -> o n", o=1).to_broadcast([P, D]))]
            for dst, src in loads:
                sp.dma_start(dst, src).then_inc(sem("c_in"), 16)
            sp_d(sp)

        C_LOADS = 16 * 10

        def pool_c(pool):
            nc.gpsimd.memset(A[:, 12288:20480], 0.0).then_inc(sem("c_zeroed"), 1)
            nc.gpsimd.memset(A[:, 4096:5120], 0.0).then_inc(sem("c_zeroed"), 1)
            pool.wait_ge(sem("c_in"), C_LOADS)
            for c in range(NCH):
                if c == 0:
                    pool.wait_ge(sem("c_qt"), 1)
                if c in (4, 8):
                    pool.wait_ge(sem("c_v"), TT)
                    part = GP[:, QT * (c // 8):QT * (c // 8 + 1), :]
                    nc.gpsimd.tensor_tensor(part, part, biasrow[:, 0, :].unsqueeze(1).to_broadcast([P, QT, D]),
                                            ALU.add).then_inc(sem("c_gp"), 1)
                if c >= 2:
                    pool.wait_ge(sem("c_at"), c - 1)
                nc.gpsimd.tensor_tensor(QX[c % 2].rearrange("p (h t) -> p h t", h=H),
                                        e1[:, c * CH:(c + 1) * CH].unsqueeze(1).to_broadcast([P, H, CH]),
                                        own_head.unsqueeze(2).to_broadcast([P, H, CH]), ALU.mult)\
                    .then_inc(sem("c_qx"), 1)
            pool_d(pool)

        NORM_AT = NCH // B + 1
        VG_BANK = [0, 1, 2, 3, 6, 7, 4, 5]

        def pe_c(pe):
            pe_transpose_tokens(pe, X, "x_ready", lambda t: TT + t + 1)
            pe.wait_ge(sem("c_in"), C_LOADS)
            pe.wait_ge(sem("xT_ready"), 6)
            for c in range(B):
                for k in range(KD):
                    ins = nc.tensor.matmul(PS[0:16, 6 + c, :], wkg1[:, k, :], XT[:, k, c * S:(c + 1) * S],
                                           start=k == 0, stop=k == KD - 1)
                ins.then_inc(sem("c_kg1"), 1)

            def values_and_gate(t, bank):
                for k in range(KD):
                    ins = nc.tensor.matmul(PS[:, bank, :], XT[:, k, t * P:(t + 1) * P], wvg[:, k, :],
                                           start=k == 0, stop=k == KD - 1)
                ins.then_inc(sem("c_vg"), 1)

            values_and_gate(0, VG_BANK[0])
            for c in range(B):
                pe.wait_ge(sem("c_kg1s"), c + 1)
                nc.tensor.matmul(PS[:, 4 + c, :], wkg2, kg1[:, c * S:(c + 1) * S], start=True, stop=True)\
                    .then_inc(sem("c_kg"), 1)
            for t in range(1, TT):
                if VG_BANK[t] == 4:
                    pe.wait_ge(sem("c_z_used"), 1)
                values_and_gate(t, VG_BANK[t])
            for w, wt in ((1, wk1), (0, wq1)):
                pe.wait_ge(sem("c_v"), 4 if w else 2)
                for c in range(B):
                    for k in range(KD):
                        ins = nc.tensor.matmul(PS[:, 2 * w + c, :], wt[:, k, :], XT[:, k, c * S:(c + 1) * S],
                                               start=k == 0, stop=k == KD - 1)
                ins.then_inc(sem("c_qk"), 1)
            pe.wait_ge(sem("c_kh"), 1)
            pe.wait_ge(sem("c_v"), TT)
            for t in range(TT):
                ins = nc.tensor.transpose(PS[:, 4 + t // 4, t % 4 * P:(t % 4 + 1) * P], e4[:, t * P:(t + 1) * P],
                                          ident[:, :])
                if t % 4 == 3:
                    ins.then_inc(sem("c_khturned"), 1)
            pe.wait_ge(sem("c_khs"), 2)
            pe.wait_ge(sem("c_qk_used"), 1)

            def chunk_scores(c):
                pb = c % 2 * CH
                pe.wait_ge(sem("c_qx"), c + 1)
                if c >= 2:
                    pe.wait_ge(sem("c_masked"), c - 1)
                for half in range(2):
                    ins = nc.tensor.matmul(PS[pb:pb + CH, 2 * (c % 2) + half, :], e2[:, c * CH:(c + 1) * CH],
                                           QX[c % 2][:, half * 512:(half + 1) * 512], start=True, stop=True)
                ins.then_inc(sem("c_at"), 1)

            def inter(c):
                t, q0 = c // 2, c % 2 * CH
                pe.wait_ge(sem("c_state"), c)
                for g in range(H // 4):
                    ins = nc.tensor.matmul(PS[:, 4 + t % 2, g * P + q0:g * P + q0 + CH],
                                           ST[(c - 1) % 2][:, g * P:(g + 1) * P], e3[:, c * CH:(c + 1) * CH],
                                           start=t % QT > 0 and q0 + g == 0, stop=True, skip_group_check=True)
                return ins

            def update(c):
                pb, t = c % 2 * CH, c // 2
                wait(pe, sem("c_state"), c)
                nc.tensor.matmul(PS[:, 6, 0:D], KH[pb:pb + CH, t, :], V1[pb:pb + CH, t, :],
                                 start=True, stop=True).then_inc(sem("c_update"), 1)

            def intra(t):
                pe.wait_ge(sem("c_masked"), 2 * t + 2)
                if t == 0:
                    pe.wait_ge(sem("c_spread"), 1)
                for h in range(H):
                    g, j = h // 4, h % 4
                    ins = nc.tensor.matmul(PS[32 * j:32 * j + 32, 4 + t % 2, g * P:(g + 1) * P], VC32[:, t, h, :],
                                           ATS[t % 2][:, h, :], start=t % QT == 0 and g == 0, stop=True,
                                           skip_group_check=True)
                return ins

            def by_token(t):
                pe.wait_ge(sem("c_ot"), t + 1)
                wait(pe, sem("c_copied"), t)
                for g in range(H // 4):
                    ins = nc.tensor.transpose(PS[:, 7, g * P:(g + 1) * P], OTC[:, g * P:(g + 1) * P], ident[:, :])
                ins.then_inc(sem("c_back"), 1)

            chunk_scores(0)
            for c in range(NCH):
                t, first_tile = c // 2, c // 2 % QT == 0
                if c + 1 < NCH:
                    chunk_scores(c + 1)
                if c % 2 and t > 0:
                    by_token(t - 1)
                if c % 2 == 0:
                    wait(pe, sem("c_ot"), t - 1)
                    if not first_tile:
                        inter(c)
                    update(c)
                elif first_tile:
                    intra(t)
                    inter(c).then_inc(sem("c_o"), 1)
                    update(c)
                else:
                    inter(c)
                    update(c)
                    intra(t).then_inc(sem("c_o"), 1)
            by_token(TT - 1)
            pe.wait_ge(sem("c_copied"), TT)
            for t in range(TT):
                if t % QT == 0:
                    pe_transpose_tokens(pe, R, "c_gated", lambda t: 1 + t // QT, batches=(t // QT,))
                    pe.wait_ge(sem("xT_ready"), 7 + t // QT)
                for k in range(KD):
                    ins = nc.tensor.matmul(PS[:, 4 + t // 2, t % 2 * D:(t % 2 + 1) * D], XT[:, k, t * P:(t + 1) * P],
                                           wo1[:, k, :], start=k == 0, stop=k == KD - 1)
                ins.then_inc(sem("c_proj"), 1)
            pe_d(pe)

        def act_c(act):
            act_xT(act, 2)
            for c in range(B):
                act.wait_ge(sem("c_kg1"), c + 1)
                nc.scalar.activation(kg1[:, c * S:(c + 1) * S], PS[0:16, 6 + c, :], ACT.Copy)\
                    .then_inc(sem("c_kg1s"), 1)
            act.wait_ge(sem("c_kg"), 2)
            act.wait_ge(sem("c_in"), C_LOADS)
            z = PS[:, 4:6, :].rearrange("p c t -> p (c t)")
            own = Chain(act, sem("act_own"))
            own.step(nc.scalar.activation(ga, z, ACT.Abs, bias=bkg))
            own.wait()
            own.step(nc.scalar.activation(gb, ga, ACT.Exp, scale=-1.0))
            own.wait()
            nc.scalar.activation(ga, gb, ACT.Ln, bias=1.0).then_inc(sem("c_ln"), 1)

            def copy_vg(t):
                act.wait_ge(sem("c_vg"), t + 1)
                nc.scalar.activation(VG[:, t, :], PS[:, VG_BANK[t], :], ACT.Copy).then_inc(sem("c_v"), 1)

            for t in range(6):
                copy_vg(t)
            act.wait_ge(sem("c_d"), 1)
            nc.scalar.activation(e2, gd, ACT.Exp, scale=-1.0 / 16).then_inc(sem("c_e"), 1)
            nc.scalar.activation(e4, ge, ACT.Exp, scale=1.0 / 16).then_inc(sem("c_e"), 1)
            nc.scalar.activation(e1, gd, ACT.Exp, scale=1.0 / 16).then_inc(sem("c_e"), 1)
            nc.scalar.activation(e3, gc_, ACT.Exp, scale=1.0 / 16).then_inc(sem("c_e"), 1)
            nc.scalar.activation(dec[:, :], gc_.rearrange("p (c t) -> p c t", c=NCH)[:, :, CH - 1], ACT.Exp,
                                 scale=1.0 / 16).then_inc(sem("c_e"), 1)
            for t in range(6, TT):
                copy_vg(t)
            for u in range(2):
                act.wait_ge(sem("c_khturned"), u + 1)
                nc.scalar.activation(KH[:, 4 * u:4 * u + 4, :], PS[:, 4 + u, :].rearrange("p (t n) -> p t n", t=4),
                                     ACT.Copy).then_inc(sem("c_khs"), 1)

            act.wait_ge(sem("c_zeroed"), 1)
            act.wait_ge(sem("c_v"), TT)
            nc.scalar.activation(VC32[:, :, :, 0:D // H],
                                 V1.rearrange("p t (h d) -> p t h d", h=H), ACT.Copy).then_inc(sem("c_spread"), 1)

            def squares(b):
                act.wait_ge(sem("c_centred"), b + 1)
                nc.scalar.activation(gc_.rearrange("p (t n) -> p t n", t=QT), R[:, QT * b:QT * (b + 1), :], ACT.Square)\
                    .then_inc(sem("c_squared"), 1)

            def deviations(b):
                load_table(ACT.Sqrt)
                act.wait_ge(sem("c_gvar"), b + 1)
                part = gvar[:, QT * H * b:QT * H * (b + 1)]
                nc.scalar.activation(part, part, ACT.Sqrt, bias=eps5[:, :]).then_inc(sem("c_gsd"), 1)

            def copy_out(t):
                act.wait_ge(sem("c_back"), t + 1)
                nc.scalar.activation(R[:, t, :].rearrange("p (h d) -> p h d", h=H),
                                     PS[:, 7, :].rearrange("p (h x) -> p h x", h=H)[:, :, 0:D // H], ACT.Copy)\
                    .then_inc(sem("c_copied"), 1)

            for t in range(TT):
                if t > 0:
                    copy_out(t - 1)
                act.wait_ge(sem("c_o"), t + 1)
                nc.scalar.activation(OTC, PS[:, 4 + t % 2, :], ACT.Copy).then_inc(sem("c_ot"), 1)
                if t in (3, 6):
                    b = t // 6
                    act.wait_ge(sem("c_gp"), b + 1)
                    part = GP[:, QT * b:QT * (b + 1), :]
                    own.step(nc.scalar.activation(part, part, ACT.Silu))
                if t == QT:
                    own.wait()
                    squares(0)
                if t == QT + 1:
                    deviations(0)
            copy_out(TT - 1)
            act_xT(act, 3, batches=(0,))
            own.wait()
            squares(1)
            deviations(1)
            act_xT(act, 3, batches=(1,))
            act_sqrt(act, 3)
            act_d(act)

        def dve_c(dve, own):
            dve.wait_ge(sem("c_kg"), 2)
            dve.wait_ge(sem("c_in"), C_LOADS)
            z = PS[:, 4:6, :].rearrange("p c t -> p (c t)")
            dve.wait_ge(sem("c_ln"), 1)
            nc.vector.tensor_scalar(gb, z, bkg, 0.0, ALU.add, ALU.min).then_inc(sem("c_z_used"), 1)
            dve.wait_ge(sem("c_z_used"), 1)
            own.step(nc.vector.tensor_tensor(gb, gb, ga, ALU.subtract))
            own.wait()
            own.step(nc.vector.tensor_tensor_scan(gc_, run, gb, 0.0, ALU.mult, ALU.add))
            own.wait()
            g3 = gc_.rearrange("p (c t) -> p c t", c=NCH)
            own.step(nc.vector.tensor_tensor(gd.rearrange("p (c t) -> p c t", c=NCH), g3,
                                             g3[:, :, CH // 2 - 1:CH // 2].to_broadcast([P, NCH, CH]), ALU.subtract))
            nc.vector.tensor_tensor(ge.rearrange("p (c t) -> p c t", c=NCH),
                                    g3[:, :, CH - 1:CH].to_broadcast([P, NCH, CH]), g3, ALU.subtract)\
                .then_inc(sem("c_d"), 1)
            q = PS[:, 0:2, :].rearrange("p c t -> p (c t)")
            kk = PS[:, 2:4, :].rearrange("p c t -> p (c t)")
            dve.wait_ge(sem("c_qk"), 1)
            dve.wait_ge(sem("c_e"), 1)
            own.step(nc.vector.scalar_tensor_tensor(e2, kk, KSCALE, e2, ALU.mult, ALU.mult))
            dve.wait_ge(sem("c_e"), 2)
            nc.vector.scalar_tensor_tensor(e4, kk, KSCALE, e4, ALU.mult, ALU.mult).then_inc(sem("c_kh"), 1)
            dve.wait_ge(sem("c_qk"), 2)
            dve.wait_ge(sem("c_e"), 3)
            nc.vector.tensor_tensor(e1, q, e1, ALU.mult).then_inc(sem("c_qt"), 1)
            own.wait()
            dve.wait_ge(sem("c_e"), 4)
            nc.vector.tensor_tensor(e3, q, e3, ALU.mult).then_inc(sem("c_qk_used"), 1)
            dve.wait_ge(sem("c_e"), 5)

            def values_of(state):
                return state.rearrange("p (h x) -> p h x", h=H)[:, :, 0:D // H]

            def by_head3(v):
                return v.rearrange("p (h d) -> p h d", h=H)

            def by_head(v):
                return v.unsqueeze(2).to_broadcast([P, QT * H, D // H])

            def centre(b):
                dve.wait_ge(sem("c_copied"), (b + 1) * QT)
                o = R[:, QT * b:QT * (b + 1), :].rearrange("p t (h d) -> p (t h) d", h=H)
                gs = gsum[:, QT * H * b:QT * H * (b + 1)]
                own.step(nc.vector.tensor_reduce(gs, o, AX_X, ALU.add))
                own.wait()
                own.step(nc.vector.tensor_scalar(gs, gs, 1.0 / (D // H), None, ALU.mult))
                own.wait()
                nc.vector.tensor_tensor(o, o, by_head(gs), ALU.subtract).then_inc(sem("c_centred"), 1)

            def variances(b):
                dve.wait_ge(sem("c_squared"), b + 1)
                gv = gvar[:, QT * H * b:QT * H * (b + 1)]
                own.step(nc.vector.tensor_reduce(gv, gc_.rearrange("p (n d) -> p n d", d=D // H), AX_X, ALU.add))
                own.wait()
                nc.vector.tensor_scalar(gv, gv, 1.0 / (D // H), None, ALU.mult).then_inc(sem("c_gvar"), 1)

            def scale_and_gate(b):
                dve.wait_ge(sem("c_gsd"), b + 1)
                tiles = slice(QT * b, QT * (b + 1))
                o = R[:, tiles, :].rearrange("p t (h d) -> p (t h) d", h=H)
                gs, gv = (v[:, QT * H * b:QT * H * (b + 1)] for v in (gsum, gvar))
                own.step(nc.vector.reciprocal(gs, gv))
                own.wait()
                own.step(nc.vector.tensor_tensor(o, o, by_head(gs), ALU.mult))
                own.wait()
                nc.vector.tensor_tensor(R[:, tiles, :], R[:, tiles, :], GP[:, tiles, :], ALU.mult)\
                    .then_inc(sem("c_gated"), 1)

            for c in range(NCH):
                pb, t, first = c % 2 * CH, c // 2, c % (NCH // B) == 0
                dve.wait_ge(sem("c_at"), c + 1)
                if c == 0:
                    dve.wait_ge(sem("c_zeroed"), 2)
                wait(dve, sem("c_o"), t - 1)
                nc.vector.tensor_tensor(ATS[t % 2][pb:pb + CH, :, pb:pb + CH],
                                        PS[pb:pb + CH, 2 * (c % 2):2 * (c % 2) + 2, :]
                                        .rearrange("p a (h t) -> p (a h) t", t=CH),
                                        causal[pb:pb + CH, :].unsqueeze(1).to_broadcast([CH, H, CH]),
                                        ALU.mult).then_inc(sem("c_masked"), 1)
                dve.wait_ge(sem("c_update"), c + 1)
                if c >= 1:
                    dve.wait_ge(sem("c_state"), c)
                if first:
                    nc.vector.tensor_tensor(values_of(ST[c % 2]), by_head3(PS[:, 6, 0:D]), by_head3(own_block),
                                            ALU.mult)\
                        .then_inc(sem("c_state"), 1)
                else:
                    own.step(nc.vector.tensor_tensor(UP, PS[:, 6, 0:D], own_block, ALU.mult))
                    own.wait()
                    nc.vector.scalar_tensor_tensor(values_of(ST[c % 2]), values_of(ST[(c - 1) % 2]),
                                                   dec[:, c:c + 1], by_head3(UP), ALU.mult, ALU.add).then_inc(sem("c_state"), 1)
                if c == NORM_AT:
                    centre(0)
                if c == NORM_AT + 2:
                    variances(0)
                if c == NORM_AT + 3:
                    scale_and_gate(0)
            centre(1)
            variances(1)
            scale_and_gate(1)

            def add(c):
                for u in (2 * c, 2 * c + 1):
                    dve.wait_ge(sem("c_proj"), 2 * u + 2)
                    own.step(nc.vector.tensor_tensor(
                        R[:, 2 * u:2 * u + 2, :], PS[:, 4 + u, :].rearrange("p (t n) -> p t n", t=2),
                        X[:, 2 * u:2 * u + 2, :], ALU.add))

            dve_norm(dve, own, 3, add)
            dve_d(dve, own)

        def sp_d(sp):
            sp.wait_ge(sem("x_ready"), 2 * TT)

            def load_head(g, p):
                if not isinstance(g, int):
                    g = sp.snap(g)
                wait(sp, sem("d_pieced"), 8 * g - 8)
                sp.dma_start(WD[p].rearrange("p w k n -> p (w k n)"),
                             io["w_qkv1"][bass.ds(g, 1), :, :].rearrange("g p n -> p (g n)"))\
                    .then_inc(sem(f"wd_in{p}"), 16)

            def load_wo(pair):
                if not isinstance(pair, int):
                    pair = sp.snap(pair)
                wait(sp, sem("d_wo"), 8 * pair)
                sp.dma_start(WOP.rearrange("p g n -> p (g n)"),
                             io["w_o1"][bass.ds(pair, 1), :, :].rearrange("g p n -> p (g n)"))\
                    .then_inc(sem("wo_in"), 16)

            load_head(0, 0)
            load_head(1, 1)
            for src, dst in (("L1_ffn_ln1_w", 2), ("L1_ffn_ln2_w", 3)):
                sp.dma_start(biasrow[:, dst, :], io[src].rearrange("(o n) -> o n", o=1).to_broadcast([P, D]))\
                    .then_inc(sem("ln_w_in"), 16)
            load_head(2, 0)
            load_head(3, 1)
            load_wo(0)
            with sp.Fori(1, H // 2 - 1) as pair:
                load_head(2 * pair + 2, 0)
                load_head(2 * pair + 3, 1)
                load_wo(pair)
            load_wo(H // 2 - 1)
            sp.dma_start(rw1, io["gate_w1"].rearrange("(k p) e -> p k e", p=P)).then_inc(sem("rw1_in"), 16)
            sp.dma_start(WSH1[:, 0:KD * 2 * FS1], io["w_shared_gu1"]).then_inc(sem("w_shared1"), 16)
            sp.dma_start(WSH1[:, KD * 2 * FS1:W1_SHARED], io["w_shared_dn1"]).then_inc(sem("w_shared1"), 16)

            def load_expert(e, p):
                if not isinstance(e, int):
                    e = sp.snap(e)
                wait(sp, sem("e_w_split"), e - 1)
                sp.dma_start(W1R[p], io["w_experts1"][:, bass.ds(e, 1), :].rearrange("p e n -> p (e n)"))\
                    .then_inc(sem(f"w1_in{p}"), 16)

            load_expert(0, 0)
            load_expert(1, 1)
            with sp.Fori(1, E1 // 2) as j:
                for p in range(2):
                    load_expert(2 * j + p, p)
            for c in range(B):
                sp.wait_ge(sem("x_ready"), 3 * TT + QT * (c + 1))
                sp.dma_start(out.rearrange("(t p) n -> p t n", p=P)[:, QT * c:QT * (c + 1), :],
                             X[:, QT * c:QT * (c + 1), :]).then_inc(sem("out_done"), 16)
            sp.wait_ge(sem("out_done"), 32)

        def pe_d(pe):
            pe_transpose_tokens(pe, HN, "hn_ready", lambda t: t + 1)

            def project(g, n, p):
                if n == 0:
                    pe.wait_ge(sem(f"wd_in{p}"), (g - p) * 8 + 16)
                bank = 6
                if isinstance(g, int) and g == 0:
                    bank = n
                else:
                    pe.wait_ge(sem("d_piece"), 8 * g + n)
                if n < 4:
                    w, c = n // 2, n % 2
                    if isinstance(g, int) and g == 0:
                        for k in range(KD):
                            ins = nc.tensor.matmul(PS[:, bank, :], WD[p][:, w, k, :], XT[:, k, c * S:(c + 1) * S],
                                                   start=k == 0, stop=k == KD - 1)
                    else:
                        if n == 0:
                            pe.wait_ge(sem("xT_split"), 1)
                            pe.wait_ge(sem("d_w_split"), g)
                        for k in range(KD):
                            for x, y in PRODUCTS:
                                ins = nc.tensor.matmul(PS[:, bank, :], WD_HL[p][y][:, w, k, :],
                                                       XT_HL[x][:, k, c * S:(c + 1) * S],
                                                       start=k == 0 and x + y == 0, stop=k == KD - 1 and x == 1)
                else:
                    for t in (2 * n - 8, 2 * n - 7):
                        for k in range(KD):
                            ins = nc.tensor.matmul(PS[:, bank, t % 2 * P:(t % 2 + 1) * P], XT[:, k, t * P:(t + 1) * P],
                                                   WD[p][:, 2, k, :], start=k == 0, stop=k == KD - 1)
                ins.then_inc(sem("d_pieced"), 1)

            def scores(N, g, n, p):
                b, i = n // 4, n % 4
                if n % 4 == 0:
                    pe.wait_ge(sem("d_piece"), 8 * g + 4)
                wait(pe, sem("d_exp"), N - 1)
                w = (i + 1) * P
                nc.tensor.matmul(PS[:, n % 2, 0:w], QKT[p][:, 0, b * S + i * P:b * S + w],
                                 QKT[p][:, 1, b * S:b * S + w], start=True, stop=False)
                nc.tensor.matmul(PS[:, n % 2, i * P:w], identb[:, :], maskb[:, :], start=False, stop=True)\
                    .then_inc(sem("d_scores"), 1)

            def turn(N, n):
                pe.wait_ge(sem("d_norm"), N + 1)
                wait(pe, sem("d_pt"), N - 1)
                for j in range(n % 4 + 1):
                    ins = nc.tensor.transpose(PS[:, 2 + n % 2, j * P:(j + 1) * P], PB1[:, n % 4, j * P:(j + 1) * P],
                                              ident[:, :])
                ins.then_inc(sem("d_turned"), 1)

            def values(N, g, n, p):
                b, i = n // 4, n % 4
                pe.wait_ge(sem("d_pt"), N + 1)
                if i == 0:
                    pe.wait_ge(sem("d_piece"), 8 * g + 8)
                    wait(pe, sem("d_aot"), 2 * g + b - 1)
                for j in range(i + 1):
                    ins = nc.tensor.matmul(PS[:, 4 + b, i * P:(i + 1) * P], VH[p][:, 4 * b + j, :],
                                           PTS1[:, n % 2, j * P:(j + 1) * P], start=j == 0, stop=j == i)
                ins.then_inc(sem("d_values"), 1)

            def project_out(pair, t):
                if t == 0:
                    pe.wait_ge(sem("wo_in"), 16 * pair + 16)
                if t % 4 == 0:
                    pe.wait_ge(sem("d_aot"), 4 * pair + 3 + t // 4)
                pe.wait_ge(sem("d_acc"), 8 * pair + t + 8)
                for g in range(2):
                    ins = nc.tensor.matmul(PS[:, 7, 0:D], AOT[:, g, t * P:(t + 1) * P], WOP[:, g, :],
                                           start=g == 0, stop=g == 1)
                ins.then_inc(sem("d_wo"), 1)

            pe.wait_ge(sem("xT_ready"), 10)
            for n in range(8):
                project(0, n, 0)
            scores(0, 0, 0, 0)

            def pair_steps(pair, first=False, last=False):
                for m in range(16):
                    N, p, n = 16 * pair + m, m // 8, m % 8
                    g = 2 * pair + p
                    if not (last and m == 15):
                        scores(N + 1, g + (n == 7), (n + 1) % 8, (m + 1) // 8 % 2)
                    if not (last and p == 1):
                        project(g + 1, n, 1 - p)
                    turn(N, n)
                    if m > 0:
                        values(N - 1, g - (n == 0), (n - 1) % 8, (m - 1) // 8)
                    elif not first:
                        values(N - 1, g - 1, 7, 1)
                    if m < 8 and not first:
                        project_out(pair - 1, m)

            pair_steps(0, first=True)
            with pe.Fori(1, H // 2 - 1) as pair:
                pair_steps(pair)
            pair_steps(H // 2 - 1, last=True)
            values(8 * H - 1, H - 1, 7, 1)
            for t in range(TT):
                project_out(H // 2 - 1, t)
            pe_e(pe)

        def act_rms(act, src, phase, wait_tile):
            for t in range(TT):
                wait_tile(t)
                if t > 0:
                    act.wait_ge(sem("squares"), TT * (phase - 1) + t)
                nc.scalar.activation(sq, src[:, t, :], ACT.Square, accum_out=ssq[:, t:t + 1])\
                    .then_inc(sem("squares"), 1)
                if t % QT == QT - 1:
                    part = slice(t + 1 - QT, t + 1)
                    act.wait_ge(sem("squares"), TT * (phase - 1) + t + 1)
                    nc.scalar.activation(sd[:, part], ssq[:, part], ACT.Sqrt, bias=eps6[:, :], scale=1.0 / D)\
                        .then_inc(sem("rms_ready"), 1)

        def dve_rms(dve, own, src, phase):
            dve.wait_ge(sem("ln_w_in"), 32)
            for c in range(B):
                part = slice(QT * c, QT * (c + 1))
                dve.wait_ge(sem("rms_ready"), B * (phase - 1) + c + 1)
                own.step(nc.vector.reciprocal(rstd[:, part], sd[:, part]))
                own.wait()
                for t in range(QT * c, QT * (c + 1)):
                    nc.vector.scalar_tensor_tensor(HN[:, t, :], src[:, t, :], rstd[:, t:t + 1],
                                                   biasrow[:, phase + 1, :], ALU.mult, ALU.mult)\
                        .then_inc(sem("hn_ready"), 1)

        def act_d(act):
            act_rms(act, X, 1, lambda t: act.wait_ge(sem("x_ready"), 2 * TT + t + 1))
            act_xT(act, 4)

            def copy_piece(g, n, p):
                act.wait_ge(sem("d_pieced"), 8 * g + n + 1)
                wait(act, sem("d_values"), 8 * g - 8)
                bank = n if isinstance(g, int) and g == 0 else 6
                if n < 4:
                    w, c = n // 2, n % 2
                    ins = nc.scalar.activation(QKT[p][:, w, c * S:(c + 1) * S], PS[:, bank, :], ACT.Copy,
                                               scale=QSCALE1 if w == 0 else 1.0)
                else:
                    ins = nc.scalar.activation(VH[p][:, 2 * n - 8:2 * n - 6, :],
                                               PS[:, bank, 0:2 * P].rearrange("p (t d) -> p t d", t=2), ACT.Copy)
                ins.then_inc(sem("d_piece"), 1)

            def exps(N, n):
                act.wait_ge(sem("d_max"), N + 1)
                wait(act, sem("d_turned"), N - 3)
                i = n % 4
                nc.scalar.activation(PB1[:, i, 0:(i + 1) * P], PS[:, n % 2, 0:(i + 1) * P], ACT.Exp,
                                     bias=negmax[:, n:n + 1], accum_out=rowsum[:, n:n + 1]).then_inc(sem("d_exp"), 1)

            def copy_out(pair, unit):
                p, b = unit // 2, unit % 2
                act.wait_ge(sem("d_values"), 16 * pair + 4 * unit + 4)
                wait(act, sem("d_wo"), 8 * (pair - 1) + 4 * b + 4)
                nc.scalar.activation(AOT[:, p, b * S:(b + 1) * S], PS[:, 4 + b, :], ACT.Copy).then_inc(sem("d_aot"), 1)

            for n in range(8):
                copy_piece(0, n, 0)
            exps(0, 0)

            def pair_steps(pair, first=False, last=False):
                for m in range(16):
                    N, p, n = 16 * pair + m, m // 8, m % 8
                    if not (last and m == 15):
                        exps(N + 1, (n + 1) % 8)
                    if not (last and p == 1):
                        copy_piece(2 * pair + p + 1, n, 1 - p)
                    if m % 4 == 0:
                        if m > 0:
                            copy_out(pair, m // 4 - 1)
                        elif not first:
                            copy_out(pair - 1, 3)

            pair_steps(0, first=True)
            with act.Fori(1, H // 2 - 1) as pair:
                pair_steps(pair)
            pair_steps(H // 2 - 1, last=True)
            copy_out(H // 2 - 1, 3)
            act_e(act)

        def dve_d(dve, own):
            dve_rms(dve, own, X, 1)
            for t in range(TT):
                nc.vector.tensor_copy(R[:, t, :], X[:, t, :]).then_inc(sem("d_acc"), 1)

            def maxes(N, n):
                dve.wait_ge(sem("d_scores"), N + 1)
                wait(dve, sem("d_exp"), N - 7)
                i = n % 4
                nc.vector.tensor_reduce(negmax[:, n:n + 1], PS[:, n % 2, 0:(i + 1) * P], AX_X, ALU.max,
                                        negate=True).then_inc(sem("d_max"), 1)

            def normalise(N, n):
                i = n % 4
                dve.wait_ge(sem("d_exp"), N + 1)
                nc.vector.reciprocal(rinv[:, n:n + 1], rowsum[:, n:n + 1]).then_inc(sem("d_rinv"), 1)
                dve.wait_ge(sem("d_rinv"), N + 1)
                nc.vector.tensor_scalar(PB1[:, i, 0:(i + 1) * P], PB1[:, i, 0:(i + 1) * P], rinv[:, n:n + 1], None,
                                        ALU.mult).then_inc(sem("d_norm"), 1)

            def copy_pt(N, n):
                dve.wait_ge(sem("d_turned"), N + 1)
                wait(dve, sem("d_values"), N - 1)
                w = (n % 4 + 1) * P
                nc.vector.tensor_copy(PTS1[:, n % 2, 0:w], PS[:, 2 + n % 2, 0:w]).then_inc(sem("d_pt"), 1)

            def accumulate(pair, t):
                dve.wait_ge(sem("d_wo"), 8 * pair + t + 1)
                dve.wait_ge(sem("d_acc"), 8 * pair + t + 1)
                nc.vector.tensor_tensor(R[:, t, :], R[:, t, :], PS[:, 7, 0:D], ALU.add).then_inc(sem("d_acc"), 1)

            maxes(0, 0)

            def pair_steps(pair, first=False, last=False):
                for m in range(16):
                    N, n = 16 * pair + m, m % 8
                    if 0 < m <= 8 and not first:
                        accumulate(pair - 1, m - 1)
                    normalise(N, n)
                    if not (last and m == 15):
                        maxes(N + 1, (n + 1) % 8)
                    copy_pt(N, n)

            pair_steps(0, first=True)
            with dve.Fori(1, H // 2 - 1) as pair:
                pair_steps(pair)
            pair_steps(H // 2 - 1, last=True)
            for t in range(TT):
                accumulate(H // 2 - 1, t)
            dve_e(dve, own)

        def act_e(act):
            act_rms(act, R, 2, lambda t: act.wait_ge(sem("d_acc"), 4 * H + t + 1))
            act_xT(act, 5)
            for t in range(TT):
                act.wait_ge(sem("e_max"), 1)
                nc.scalar.activation(cw[:, t, :], lg1[:, t, :], ACT.Exp, bias=negmax[:, t:t + 1],
                                     accum_out=zsum[:, t:t + 1]).then_inc(sem("e_exp"), 1)

            def silu(N, p, f):
                act.wait_ge(sem("e_gu"), N + 1)
                wait(act, sem("e_h"), N - 1)
                nc.scalar.activation(SG1[:, p, 0:f], PS[:, p, 0:f], ACT.Silu).then_inc(sem("e_silu"), 1)

            def high_ht(N, p):
                act.wait_ge(sem("e_hturned"), N + 1)
                wait(act, sem("e_down"), N - 1)
                nc.scalar.activation(HT_HL[0][0:F1 // 2, p, :], PS[0:F1 // 2, 4 + p, 0:2 * P], ACT.Copy)\
                    .then_inc(sem("e_ht"), 1)

            def shared(t):
                silu(t, t % 2, FS1)
                if t > 0:
                    shared_ht(t - 1)

            def shared_ht(t):
                p = t % 2
                act.wait_ge(sem("e_hturned"), t + 1)
                wait(act, sem("e_down"), t - 1)
                nc.scalar.activation(HBT1[:, p, 0:256], PS[:, 4 + p, 0:256], ACT.Copy)
                nc.scalar.activation(HBT1[0:96, p, 256:384], PS[0:96, 4 + p, 256:384], ACT.Copy)\
                    .then_inc(sem("e_ht"), 1)

            for t in range(TT):
                shared(t)

            def expert(e, first=False):
                for t in range(TT):
                    N = TT * (e + 1) + t
                    silu(N, t % 2, F1)
                    if first and t == 0:
                        shared_ht(TT - 1)
                    else:
                        high_ht(N - 1, (t - 1) % 2)

            expert(0, first=True)
            with act.Fori(1, E1) as e:
                expert(e)
            high_ht(TT * (E1 + 1) - 1, 1)
            act_sqrt(act, 4)

        def pe_e(pe):
            pe_transpose_tokens(pe, HN, "hn_ready", lambda t: TT + t + 1)
            pe.wait_ge(sem("rw1_in"), 16)
            pe.wait_ge(sem("xT_ready"), 12)
            for t in range(TT):
                for k in range(KD):
                    ins = nc.tensor.matmul(PS[:, 7, t * E1:(t + 1) * E1], XT[:, k, t * P:(t + 1) * P], rw1[:, k, :],
                                           start=k == 0, stop=k == KD - 1)
            ins.then_inc(sem("e_logits"), 1)
            pe.wait_ge(sem("w_shared1"), 32)

            def turn_h(N, chunks, width, p):
                pe.wait_ge(sem("e_h"), N + 1)
                if isinstance(N, int) and N < TT + 2:
                    wait(pe, sem("e_ht"), N - 1)
                else:
                    pe.wait_ge(sem("e_ht_low"), N - TT - 1)
                for j, (rows, c) in enumerate(chunks):
                    ins = nc.tensor.transpose(PS[0:rows, 4 + p, c:c + P], HB1[:, p, j * width:j * width + rows],
                                              ident[:, :])
                ins.then_inc(sem("e_hturned"), 1)

            SH = [(P, 0), (P, P), (96, 2 * P)]

            def shared_gate_up(t):
                for g in range(2):
                    wait(pe, sem("e_silu" if g == 0 else "e_h"), t - 1)
                    for k in range(KD):
                        ins = nc.tensor.matmul(PS[:, 2 * g + t % 2, 0:FS1], XT[:, k, t * P:(t + 1) * P],
                                               WSH1[:, (2 * k + g) * FS1:(2 * k + g + 1) * FS1],
                                               start=k == 0, stop=k == KD - 1)
                ins.then_inc(sem("e_gu"), 1)

            def shared_down(t):
                pe.wait_ge(sem("e_ht"), t + 1)
                wait(pe, sem("e_acc"), t)
                for j, (rows, c) in enumerate(SH):
                    ins = nc.tensor.matmul(PS[:, 6, 0:D], HBT1[0:rows, t % 2, c:c + P],
                                           WSH1[0:rows, KD * 2 * FS1 + j * D:KD * 2 * FS1 + (j + 1) * D],
                                           start=j == 0, stop=j == len(SH) - 1)
                ins.then_inc(sem("e_down"), 1)

            for t in range(TT):
                shared_gate_up(t)
                if t >= 1:
                    turn_h(t - 1, SH, P, (t - 1) % 2)
                if t >= 2:
                    shared_down(t - 2)

            EX = [(F1 // 2, 0), (F1 // 2, P)]

            def gate_up(N, t, W):
                wait(pe, sem("e_h"), N - 1)
                for k in range(KD):
                    for x, w in PRODUCTS:
                        ins = nc.tensor.matmul(PS[:, t % 2, 0:2 * F1], XT_HL[x][:, k, t * P:(t + 1) * P],
                                               W[w][:, k * 2 * F1:(k + 1) * 2 * F1],
                                               start=k == 0 and x + w == 0, stop=k == KD - 1 and x == 1)
                ins.then_inc(sem("e_gu"), 1)

            def down(N, W, p):
                pe.wait_ge(sem("e_ht_low"), N + 1 - TT)
                pe.wait_ge(sem("e_acc"), N)
                for j, (rows, c) in enumerate(EX):
                    for x, w in PRODUCTS:
                        at = KD * 2 * F1 + j * D
                        ins = nc.tensor.matmul(PS[:, 6, 0:D], HT_HL[x][0:rows, p, c:c + P], W[w][0:rows, at:at + D],
                                               start=j == 0 and x + w == 0, stop=j == 1 and x == 1)
                ins.then_inc(sem("e_down"), 1)

            def expert(e, p, first=False):
                pe.wait_ge(sem("e_w_split"), e + 1)
                for t in range(TT):
                    N = TT * (e + 1) + t
                    gate_up(N, t, W_HL[p])
                    if first and t < 1:
                        turn_h(N - 1, SH, P, 1)
                    else:
                        turn_h(N - 1, EX, F1 // 2, (t - 1) % 2)
                    if first and t < 2:
                        shared_down(TT - 2 + t)
                    else:
                        down(N - 2, W_HL[1 - p if t < 2 else p], t % 2)

            pe.wait_ge(sem("xT_split"), 2)
            expert(0, 0, first=True)
            expert(1, 1)
            with pe.Fori(1, E1 // 2) as j:
                for p in range(2):
                    expert(2 * j + p, p)
            N = TT * (E1 + 1)
            turn_h(N - 1, EX, F1 // 2, 1)
            down(N - 2, W_HL[1], 0)
            down(N - 1, W_HL[1], 1)

        def pool_split_tokens(pool, nth):
            pool.wait_ge(sem("xT_ready"), 8 + 2 * nth)
            nc.gpsimd.tensor_copy(XT_HL[0][:, :, :], XT[:, :, :]).then_inc(sem("xT_high"), 1)
            pool.wait_ge(sem("xT_high"), nth)
            nc.gpsimd.tensor_tensor(XT_HL[1][:, :, :], XT[:, :, :], XT_HL[0][:, :, :].bitcast(F32), ALU.subtract)\
                .then_inc(sem("xT_split"), 1)

        def pool_d(pool):
            pool_split_tokens(pool, 1)

            def split(g, p):
                pool.wait_ge(sem(f"wd_in{p}"), (g - p) * 8 + 16)
                wait(pool, sem("d_pieced"), 8 * g - 8)
                nc.gpsimd.tensor_tensor(WD_HL[p][0].rearrange("p w k n -> p (w k n)"),
                                        WD[p].rearrange("p w k n -> p (w k n)"),
                                        ones[:, 0:1].to_broadcast([P, 3 * D]), ALU.mult).then_inc(sem("d_w_high"), 1)
                pool.wait_ge(sem("d_w_high"), g)
                nc.gpsimd.tensor_tensor(WD_HL[p][1].rearrange("p w k n -> p (w k n)"),
                                        WD[p].rearrange("p w k n -> p (w k n)"),
                                        WD_HL[p][0].rearrange("p w k n -> p (w k n)").bitcast(F32), ALU.subtract)\
                    .then_inc(sem("d_w_split"), 1)

            split(1, 1)
            with pool.Fori(1, H // 2) as pair:
                for p in range(2):
                    split(2 * pair + p, p)
            pool_e(pool)

        def pool_e(pool):
            pool_split_tokens(pool, 2)

            def split(e, p):
                pool.wait_ge(sem(f"w1_in{p}"), (e - p) * 8 + 16)
                wait(pool, sem("e_down"), TT * e)
                nc.gpsimd.tensor_tensor(W_HL[p][0][:, :], W1R[p], ones[:, 0:1].to_broadcast([P, W1_SLOT]),
                                        ALU.mult).then_inc(sem("e_w_high"), 1)
                pool.wait_ge(sem("e_w_high"), e + 1)
                nc.gpsimd.tensor_tensor(W_HL[p][1][:, :], W1R[p], W_HL[p][0][:, :].bitcast(F32), ALU.subtract)\
                    .then_inc(sem("e_w_split"), 1)

            pool.wait_ge(sem("d_acc"), 4 * H + TT)
            split(0, 0)
            split(1, 1)
            with pool.Fori(1, E1 // 2) as j:
                for p in range(2):
                    split(2 * j + p, p)

        def dve_e(dve, own):
            dve_rms(dve, own, R, 2)
            dve.wait_ge(sem("e_logits"), 1)
            own.step(nc.vector.tensor_copy(lg1, PS[:, 7, 0:TT * E1].rearrange("p (t e) -> p t e", e=E1)))
            own.wait()
            nc.vector.tensor_reduce(negmax[:, :], lg1, AX_X, ALU.max, negate=True).then_inc(sem("e_max"), 1)
            own.step(nc.vector.tensor_tensor(R[:, :, :], R[:, :, :], X[:, :, :], ALU.add))
            dve.wait_ge(sem("e_exp"), TT)
            own.step(nc.vector.reciprocal(rinv[:, :], zsum[:, :]))
            own.wait()
            own.step(nc.vector.tensor_tensor(lg1, cw, rinv[:, :].unsqueeze(2).to_broadcast([P, TT, E1]), ALU.mult))
            own.wait()
            for t in range(TT):
                own.step(nc.vector.max(mx[:, t, :], lg1[:, t, :]))
            own.wait()
            for t in range(TT):
                own.step(nc.vector.max_index(ix[:, t, :], mx[:, t, :], lg1[:, t, :]))
            own.step(nc.vector.tensor_reduce(zsum[:, :], mx[:, :, 0:K1], AX_X, ALU.add))
            own.wait()
            own.step(nc.vector.tensor_copy(ixf1[:, :, :], ix[:, :, :]))
            own.step(nc.vector.reciprocal(rinv[:, :], zsum[:, :]))
            own.wait()
            own.step(nc.vector.tensor_tensor(mx[:, :, :], mx[:, :, :], rinv[:, :].unsqueeze(2)
                                             .to_broadcast([P, TT, 8]), ALU.mult))
            own.wait()
            for t in range(TT):
                own.step(nc.vector.tensor_tensor(
                    OH1[:, t, :, :], ixf1[:, t, 0:K1].unsqueeze(2).to_broadcast([P, K1, E1]),
                    iota_e.unsqueeze(1).to_broadcast([P, K1, E1]), ALU.is_equal))
            own.wait()
            for t in range(TT):
                own.step(nc.vector.tensor_tensor(OH1[:, t, :, :], OH1[:, t, :, :],
                                                 mx[:, t, 0:K1].unsqueeze(2).to_broadcast([P, K1, E1]), ALU.mult))
            own.wait()
            own.step(nc.vector.tensor_reduce(cw, OH1.rearrange("p t k e -> p t e k"), AX_X, ALU.add))
            own.wait()

            def hidden(N, p, f, up_bank, up_at):
                dve.wait_ge(sem("e_silu"), N + 1)
                wait(dve, sem("e_hturned"), N - 1)
                nc.vector.tensor_tensor(HB1[:, p, 0:f], SG1[:, p, 0:f], PS[:, up_bank, up_at:up_at + f], ALU.mult)\
                    .then_inc(sem("e_h"), 1)

            def add_shared(t):
                dve.wait_ge(sem("e_down"), t + 1)
                nc.vector.tensor_tensor(R[:, t, :], R[:, t, :], PS[:, 6, 0:D], ALU.add).then_inc(sem("e_acc"), 1)

            def add_expert(N, t, e):
                dve.wait_ge(sem("e_down"), N + 1)
                dve.wait_ge(sem("e_acc"), N - 7)
                at = CW_AT + t * E1 + e
                nc.vector.scalar_tensor_tensor(R[:, t, :], PS[:, 6, 0:D], A[:, bass.ds(at, 1)], R[:, t, :],
                                               ALU.mult, ALU.add).then_inc(sem("e_acc"), 1)

            def low_ht(N, p):
                dve.wait_ge(sem("e_ht"), N + 1)
                nc.vector.tensor_tensor(HT_HL[1][0:F1 // 2, p, :], PS[0:F1 // 2, 4 + p, 0:2 * P],
                                        HT_HL[0][0:F1 // 2, p, :].bitcast(F32), ALU.subtract)\
                    .then_inc(sem("e_ht_low"), 1)

            for t in range(TT):
                hidden(t, t % 2, FS1, 2 + t % 2, 0)
                if t >= 2:
                    add_shared(t - 2)

            def expert(e, first=False):
                for t in range(TT):
                    N = TT * (e + 1) + t
                    hidden(N, t % 2, F1, t % 2, F1)
                    if not (first and t == 0):
                        low_ht(N - 1, (t - 1) % 2)
                    if first and t < 2:
                        add_shared(TT - 2 + t)
                    else:
                        add_expert(N - 2, (t - 2) % TT, e - (1 if t < 2 else 0))

            expert(0, first=True)
            with dve.Fori(1, E1) as e:
                expert(e)
            N = TT * (E1 + 1)
            low_ht(N - 1, 1)
            add_expert(N - 2, TT - 2, E1 - 1)
            add_expert(N - 1, TT - 1, E1 - 1)
            dve_norm(dve, own, 4, lambda c: dve.wait_ge(sem("e_acc"), N - TT + QT * (c + 1)))

        @block.sync
        def _(sp):
            sp.dma_start(W_A[0], io["L0_attn_wq"].rearrange("(k p) n -> p k n", p=P)).then_inc(sem("w_qk0"), 16)
            for c in range(B):
                sp.dma_start(XT[:, :, c * S:(c + 1) * S], io["xT"].rearrange("(k p) t -> p k t", p=P)
                             [:, :, c * S:(c + 1) * S]).then_inc(sem(f"xT_in{c}"), 16)
                if c == 0:
                    sp.dma_start(W_A[1], io["L0_attn_wk"].rearrange("(k p) n -> p k n", p=P))\
                        .then_inc(sem("w_qk0"), 16)
            for c in range(B):
                for w, src in ((0, io["q_bias_rows"]), (1, io["k_bias_rows"])):
                    dst = QK6[w].rearrange("p (h t) -> p h t", h=H)[96:P, :, c * S:(c + 1) * S]
                    sp.dma_start(dst, src.rearrange("h r t -> r h t")).then_inc(sem("bias_rows_in"), 16)
            for n in range(8):
                c, w, j = n // 4, n // 2 % 2, n % 2
                sp.wait_ge(sem("split_done"), n + 1)
                sp.dma_start(scratch[w, :, j * P:(j + 1) * P, c * S:(c + 1) * S].rearrange("q p t -> p q t"),
                             parts[:, n]).then_inc(sem("parts_stored"), 16)
                if n % 4 == 3:
                    sp.wait_ge(sem("parts_stored"), 64 * (c + 1))
                    for w2, slots in ((0, Q_SLOT), (1, K_SLOT)):
                        for s, part in enumerate(slots):
                            dst = QK6[w2].rearrange("p (h t) -> p h t", h=H)[16 * s:16 * s + 16, :, c * S:(c + 1) * S]
                            sp.dma_start(dst, scratch[w2, part, :, c * S:(c + 1) * S]
                                         .rearrange("(h d) t -> d h t", d=HD0)).then_inc(sem(f"stacked{c}"), 16)
            for k in range(GROUPS):
                b, g = k // 4, k % 4
                sp.wait_ge(sem("max_part3"), k + 1)
                sp.dma_start(max_rows[k].rearrange("q x n -> x q n"), max_parts[:, k % 2])\
                    .then_inc(sem("maxima_stored"), 16)
                sp.wait_ge(sem("maxima_stored"), 16 * (k + 1))
                sp.dma_start(QK6[0].rearrange("p (h t) -> p h t", h=H)[108:111, 4 * g:4 * g + 4, b * S:(b + 1) * S],
                             max_rows[k].rearrange("q (h i) n -> q h (i n)", h=4))\
                    .then_inc(sem(f"max_rows_in{k % 2}"), 16)
            sp.dma_start(rw0[:, :, :], io["router_w0"].rearrange("(k p) e -> p k e", p=P)).then_inc(sem("route_in"), 16)
            sp.dma_start(rc[:, :], io["route_consts"]).then_inc(sem("route_in"), 16)
            for slot_n in range(E0 + 1):
                gu, dn = W_B(slot_n)
                if slot_n == 5:
                    sp.wait_ge(sem("a_values"), 32)
                if slot_n == 6:
                    sp.wait_ge(sem("a_proj"), TT)
                src_gu = io["L0_shared_gate_up"] if slot_n == 0 else io["L0_w_gate_up"][slot_n - 1]
                src_dn = io["L0_shared_down"] if slot_n == 0 else io["L0_w_down"][slot_n - 1]
                name = "w_shared0" if slot_n == 0 else "w_routed0"
                sp.dma_start(gu, src_gu.rearrange("(k p) n -> p k n", p=P)).then_inc(sem(name), 16)
                sp.dma_start(dn, src_dn.rearrange("(j p) n -> p j n", p=P)).then_inc(sem(name), 16)
            sp_b(sp)

        @block.gpsimd
        def _(pool):
            nc.gpsimd.memset(eps5[:, :], LN_EPS).then_inc(sem("eps_set"), 1)
            nc.gpsimd.memset(eps6[:, :], RMS_EPS).then_inc(sem("eps_set"), 1)
            nc.gpsimd.memset(V32[:, :, :, :], 0.0).then_inc(sem("v_padded"), 1)
            pool.wait_ge(sem("v_padded"), 1)
            nc.gpsimd.memset(V32[:, :, :, HD0:HD0 + 1], 1.0).then_inc(sem("v_padded"), 1)
            pool.wait_ge(sem("stacked1"), 192)
            nc.gpsimd.memset(zeros[:, :], 0.0).then_inc(sem("zeros_set"), 1)
            pool.wait_ge(sem("zeros_set"), 1)
            pool.dma_start(xs_rows[:, :].rearrange("(j p) n -> p j n", p=P),
                           zeros[:, :].unsqueeze(1).to_broadcast([P, N_TILES0, D])).then_inc(sem("rows_zeroed"), 16)
            pool.wait_ge(sem("rows_zeroed"), 16)
            pool_b(pool)

        def pe_transpose_tokens(pe, src, ready, ready_at, batches=range(B)):
            for c in batches:
                for i in range(QT):
                    pe.wait_ge(sem(ready), ready_at(4 * c + i))
                    for k in range(KD):
                        ins = nc.tensor.transpose(PS[:, 2 * c + k, i * P:(i + 1) * P],
                                                  src[:, 4 * c + i, k * P:(k + 1) * P], ident[:, :])
                ins.then_inc(sem("tokens_turned"), 1)

        @block.tensor
        def _(pe):
            pe.wait_ge(sem("w_qk0"), 32)
            for n in range(8):
                c, w, j = n // 4, n // 2 % 2, n % 2
                if n % 4 == 0:
                    pe.wait_ge(sem(f"xT_in{c}"), 16)
                for k in range(KD):
                    ins = nc.tensor.matmul(PS[:, n, :], W_A[w][:, k, j * P:(j + 1) * P],
                                           XT[:, k, c * S:(c + 1) * S], start=k == 0, stop=k == KD - 1)
                ins.then_inc(sem("proj_done"), 1)
            pe.wait_ge(sem("w_v0"), 16)
            for t in range(TT):
                if t % 2 == 0:
                    pe.wait_ge(sem("q32_ready"), t // 2 + 1)
                for k in range(KD):
                    ins = nc.tensor.matmul(PS[:, t // 2, t % 2 * D:(t % 2 + 1) * D], XT[:, k, t * P:(t + 1) * P],
                                           W_A[2][:, k, :], start=k == 0, stop=k == KD - 1)
                if t % 2:
                    ins.then_inc(sem("v_done"), 1)

            def scores(b, h, i):
                M = b * H * QT + QT * h + i
                wait(pe, sem("a_max"), M - 1)
                w = (i + 1) * P
                q0, k0 = h * T + b * S + i * P, h * T + b * S
                nc.tensor.matmul(PS[:, 6 + i % 2, 0:w], QK6[0][:, bass.ds(q0, P)], QK6[1][:, bass.ds(k0, w)],
                                 start=True, stop=False)
                nc.tensor.matmul(PS[:, 6 + i % 2, i * P:w], identb[:, :], maskb[:, :],
                                 start=False, stop=True).then_inc(sem("a_scores"), 1)

            def turn_maxima(k):
                pe.wait_ge(sem("a_max"), (k + 1) * 4 * QT)
                wait(pe, sem("a_out"), k - 2)
                wait(pe, sem("max_rest"), k)
                nc.tensor.transpose(PS[0:4 * QT, 5, 0:P], negmax0[:, k // 4, k % 4 * 4 * QT:(k % 4 + 1) * 4 * QT],
                                    ident[:, :]).then_inc(sem("a_maxima"), 1)

            def scores_t(b, g, j, x):
                n = 2 * (16 * b + 4 * g + j) + x
                wait(pe, sem("a_exp"), n - 1)
                w = (QT - j) * P
                for c in range(2 * x, 2 * x + 2):
                    at = (4 * g + c) * T + b * S + j * P
                    nc.tensor.matmul(PS[:, c, 0:w], QK6[1][:, at:at + P], QK6[0][:, at:at + w],
                                     start=True, stop=False)
                    ins = nc.tensor.matmul(PS[:, c, 0:P], identb[:, :], masktb[:, :], start=False, stop=True)
                ins.then_inc(sem("a_scores_t"), 1)

            def values(b, g, j):
                u = 16 * b + 4 * g + j
                pe.wait_ge(sem("a_exp"), 2 * u + 2)
                if j == 0:
                    wait(pe, sem("a_ot"), 4 * b + g)
                for c in range(4):
                    ins = nc.tensor.matmul(PS[32 * c:32 * c + 32, 4, j * P:S], V32[:, 4 * b + j, 4 * g + c, :],
                                           PT[:, u % 2, c, 0:S - j * P], start=j == 0, stop=j == QT - 1,
                                           skip_group_check=True)
                ins.then_inc(sem("a_values"), 1)

            def turn_back(b, g):
                G = 4 * b + g
                pe.wait_ge(sem("a_ot"), G + 1)
                wait(pe, sem("a_out"), G)
                pe.wait_ge(sem("max_rest"), min(G + 3, GROUPS))
                for i in range(QT):
                    ins = nc.tensor.transpose(PS[:, 5, i * P:(i + 1) * P], OT[:, i * P:(i + 1) * P], ident[:, :])
                ins.then_inc(sem("a_turned"), 1)

            pe.wait_ge(sem("consts_in"), 64)
            pe.wait_ge(sem("bias_rows_in"), 64)
            pe.wait_ge(sem("stacked0"), 192)
            pe.wait_ge(sem("v_copied"), 4)
            pe.wait_ge(sem("q32_ready"), 8)
            ahead = [(b, h, i) for b in range(B) for h in range(H) for i in range(QT)]

            def first_pass(n):
                for _ in range(min(n, len(ahead))):
                    if ahead[0] == (1, 0, 0):
                        pe.wait_ge(sem("stacked1"), 192)
                    scores(*ahead.pop(0))

            first_pass(4 * QT + 2)
            turn_maxima(0)
            first_pass(4 * QT)
            turn_maxima(1)
            first_pass(2)
            units = [(b, g, j) for b in range(B) for g in range(4) for j in range(QT)]
            pe.wait_ge(sem("max_rows_in0"), 16)
            for x in range(2):
                scores_t(*units[0], x)
            for u, (b, g, j) in enumerate(units):
                G = 4 * b + g
                if j == QT - 1 and G + 1 < GROUPS:
                    pe.wait_ge(sem(f"max_rows_in{(G + 1) % 2}"), 16 * ((G + 1) // 2 + 1))
                for x in range(2):
                    if u + 1 < len(units):
                        scores_t(*units[u + 1], x)
                    first_pass(1)
                if j == QT - 1 and G + 2 < GROUPS:
                    turn_maxima(G + 2)
                first_pass(1)
                values(b, g, j)
                first_pass(1)
                if j == 0 and G > 0:
                    turn_back((G - 1) // 4, (G - 1) % 4)
            turn_back(B - 1, 3)

            pe.wait_ge(sem("a_exp"), 64)
            pe_transpose_tokens(pe, AO, "a_out", lambda t: 4 + t // QT * 4)
            pe.wait_ge(sem("xT_ready"), 2)
            pe.wait_ge(sem("w_o0"), 16)
            for t in range(TT):
                for k in range(KD):
                    ins = nc.tensor.matmul(PS[:, 4 + t // 2, t % 2 * D:(t % 2 + 1) * D], XT[:, k, t * P:(t + 1) * P],
                                           W_A[3][:, k, :], start=k == 0, stop=k == KD - 1)
                ins.then_inc(sem("a_proj"), 1)
            pe_b(pe)

        @block.scalar
        def _(act):
            act.dma_start(bqk0[:, :, :], io["bqk0"]).then_inc(sem("bias_in"), 16)
            act.dma_start(W_A[2], io["L0_attn_wv"].rearrange("(k p) n -> p k n", p=P)).then_inc(sem("w_v0"), 16)
            act.dma_start(ident[:, :], io["ident"]).then_inc(sem("consts_in"), 16)
            act.dma_start(identb[:, :], io["identb"]).then_inc(sem("consts_in"), 16)
            act.dma_start(maskb[:, :], io["maskb"]).then_inc(sem("consts_in"), 16)
            act.dma_start(masktb[:, :], io["masktb"]).then_inc(sem("consts_in"), 16)
            act.dma_start(biasrow[:, 0, :], io["L0_attn_bv"].rearrange("(o n) -> o n", o=1).to_broadcast([P, D]))\
                .then_inc(sem("bv_in"), 16)
            act.dma_start(biasrow[:, 1, :], io["L0_attn_bo"].rearrange("(o n) -> o n", o=1).to_broadcast([P, D]))\
                .then_inc(sem("bo_in"), 16)
            act.dma_start(W_A[3], io["L0_attn_wo"].rearrange("(k p) n -> p k n", p=P)).then_inc(sem("w_o0"), 16)
            act.dma_start(X[:, :, :], io["x"].rearrange("(t p) n -> p t n", p=P)).then_inc(sem("x_in"), 16)

            def part1(n):
                act.wait_ge(sem("q32_ready"), n + 1)
                nc.scalar.activation(parts[:, n, 0, :], q32[:, n, :], ACT.Copy).then_inc(sem("part1_done"), 1)

            part1(0)
            for n in range(8):
                if n < 7:
                    part1(n + 1)
                act.wait_ge(sem("rest_ready"), n + 1)
                nc.scalar.activation(parts[:, n, 1, :], rest[:, n % 2, :], ACT.Copy).then_inc(sem("part2_done"), 1)

            def max_part1(k):
                act.wait_ge(sem("a_maxima"), k + 1)
                wait(act, sem("maxima_stored"), 16 * (k - 1))
                nc.scalar.activation(max_parts[:, k % 2, 0, :], PS[0:4 * QT, 5, 0:P], ACT.Copy)\
                    .then_inc(sem("max_part1"), 1)

            def max_part2(k):
                act.wait_ge(sem("max_rest"), k + 1)
                nc.scalar.activation(max_parts[:, k % 2, 1, :], max_rest, ACT.Copy).then_inc(sem("max_part2"), 1)

            for k in range(2):
                max_part1(k)
                max_part2(k)
            for u in range(4 * GROUPS):
                w = (QT - u % 4) * P
                for x in range(2):
                    act.wait_ge(sem("a_scores_t"), 2 * u + x + 1)
                    wait(act, sem("a_values"), u - 1)
                    nc.scalar.activation(PT[:, u % 2, 2 * x:2 * x + 2, 0:w], PS[:, 2 * x:2 * x + 2, 0:w],
                                         ACT.Exp).then_inc(sem("a_exp"), 1)
                    if u // 4 + 2 < GROUPS and (u % 4, x) == (3, 1):
                        max_part1(u // 4 + 2)
                    if 4 <= u < 4 * (GROUPS - 1) and (u % 4, x) == (0, 1):
                        max_part2(u // 4 + 1)
            act_xT(act, 0)
            act_sqrt(act, 1)
            act_b(act)

        @block.vector
        def _(dve):
            own = Chain(dve, sem("dve_own"))

            def to_q32(n):
                c, w, j = n // 4, n // 2 % 2, n % 2
                dve.wait_ge(sem("proj_done"), n + 1)
                if n == 0:
                    dve.wait_ge(sem("bias_in"), 16)
                nc.vector.tensor_scalar(q32[:, n, :], PS[:, n, :], bqk0[:, w, j:j + 1], 0.25 if w == 0 else 1.0,
                                        ALU.add, ALU.mult).then_inc(sem("q32_ready"), 1)

            to_q32(0)
            to_q32(1)
            for n in range(8):
                dve.wait_ge(sem("part1_done"), n + 1)
                if n >= 2:
                    dve.wait_ge(sem("split_done"), n - 1)
                nc.vector.tensor_tensor(rest[:, n % 2, :], q32[:, n, :], parts[:, n, 0, :], ALU.subtract)\
                    .then_inc(sem("rest_ready"), 1)
                if n + 2 < 8:
                    dve.wait_ge(sem("rest_ready"), n + 1)
                    to_q32(n + 2)
                dve.wait_ge(sem("part2_done"), n + 1)
                nc.vector.tensor_tensor(parts[:, n, 2, :], rest[:, n % 2, :], parts[:, n, 1, :], ALU.subtract)\
                    .then_inc(sem("split_done"), 1)
            dve.wait_ge(sem("bv_in"), 16)
            dve.wait_ge(sem("v_padded"), 2)
            for u in range(4):
                dve.wait_ge(sem("v_done"), u + 1)
                for t in range(2):
                    ins = nc.vector.tensor_tensor(
                        V32[:, 2 * u + t, :, 0:HD0], PS[:, u, t * D:(t + 1) * D].rearrange("p (h d) -> p h d", h=H),
                        biasrow[:, 0, :].rearrange("p (h d) -> p h d", h=H), ALU.add)
                ins.then_inc(sem("v_copied"), 1)
            dve.wait_ge(sem("x_in"), 16)
            dve.wait_ge(sem("bo_in"), 16)
            own.step(nc.vector.tensor_tensor(X[:, :, :], X[:, :, :],
                                             biasrow[:, 1, :].unsqueeze(1).to_broadcast([P, TT, D]), ALU.add))
            x_plus_bo = own.n

            def maxes(b, h, i):
                M = b * H * QT + QT * h + i
                dve.wait_ge(sem("a_scores"), M + 1)
                nc.vector.tensor_reduce(negmax0[:, b, bass.ds(QT * h + i, 1)], PS[:, 6 + i % 2, 0:(i + 1) * P], AX_X,
                                        ALU.max, negate=True).then_inc(sem("a_max"), 1)

            def max_less_part1(k):
                dve.wait_ge(sem("max_part1"), k + 1)
                wait(dve, sem("max_part3"), k)
                nc.vector.tensor_tensor(max_rest, PS[0:4 * QT, 5, 0:P], max_parts[:, k % 2, 0, :], ALU.subtract)\
                    .then_inc(sem("max_rest"), 1)

            def max_part3(k):
                dve.wait_ge(sem("max_part2"), k + 1)
                nc.vector.tensor_tensor(max_parts[:, k % 2, 2, :], max_rest, max_parts[:, k % 2, 1, :], ALU.subtract)\
                    .then_inc(sem("max_part3"), 1)

            def copy_ot(b, g):
                G = 4 * b + g
                dve.wait_ge(sem("a_values"), 4 * G + 4)
                wait(dve, sem("a_turned"), G)
                nc.vector.tensor_copy(OT, PS[:, 4, :]).then_inc(sem("a_ot"), 1)

            def normalise(b, g):
                G = 4 * b + g
                dve.wait_ge(sem("a_turned"), G + 1)
                o = PS[:, 5, :].rearrange("p (i c d) -> p i c d", i=QT, c=4)
                nc.vector.reciprocal(rinv0[:, :].rearrange("p (i c) -> p i c", i=QT), o[:, :, :, HD0])\
                    .then_inc(sem("a_rinv"), 1)
                dve.wait_ge(sem("a_rinv"), G + 1)
                nc.vector.tensor_tensor(
                    AO[:, 4 * b:4 * b + 4, 4 * g * HD0:4 * (g + 1) * HD0].rearrange("p i (c d) -> p i c d", c=4),
                    o[:, :, :, 0:HD0],
                    rinv0[:, :].rearrange("p (i c) -> p i c", i=QT).unsqueeze(3).to_broadcast([P, QT, 4, HD0]),
                    ALU.mult).then_inc(sem("a_out"), 1)

            ahead = [(b, h, i) for b in range(B) for h in range(H) for i in range(QT)]

            def first_pass(n):
                for _ in range(min(n, len(ahead))):
                    maxes(*ahead.pop(0))

            first_pass(4 * QT + 2)
            max_less_part1(0)
            first_pass(2)
            max_part3(0)
            first_pass(4 * QT - 2)
            max_less_part1(1)
            first_pass(2)
            max_part3(1)
            for G in range(GROUPS):
                for j in range(QT):
                    first_pass(2)
                    if G + 2 < GROUPS and j == QT - 1:
                        max_less_part1(G + 2)
                    first_pass(2)
                    if 0 < G < GROUPS - 1 and j == 0:
                        max_part3(G + 1)
                    if j == 0 and G > 0:
                        normalise((G - 1) // 4, (G - 1) % 4)
                copy_ot(G // 4, G % 4)
            normalise(B - 1, 3)
            dve.wait_ge(sem("dve_own"), x_plus_bo)

            def add(c):
                for t in range(QT * c, QT * (c + 1), 2):
                    dve.wait_ge(sem("a_proj"), t + 2)
                    own.step(nc.vector.tensor_tensor(
                        R[:, t:t + 2, :], PS[:, 4 + t // 2, :].rearrange("p (t n) -> p t n", t=2),
                        X[:, t:t + 2, :], ALU.add))

            dve_norm(dve, own, 1, add)
            dve_b(dve, own)



def lay_out(arrays, w):
    import numpy as np
    turned = np.ascontiguousarray
    arrays["router_w0"] = turned(w["L0_ffn_router_w"].T)
    arrays["L0_w_gate_up"] = w["L0_ffn_w_gate_up"]
    arrays["L0_w_down"] = w["L0_ffn_w_down"]
    arrays["L0_shared_gate_up"] = w["L0_ffn_shared_gate_up"]
    arrays["L0_shared_down"] = w["L0_ffn_shared_down"]
    for name in ("Wq", "Wk", "Wkg1", "Wkg2", "Wo"):
        arrays[f"L1_attn_{name}T"] = turned(w["L1_attn_" + name].T)
    arrays["L1_attn_WvgT"] = turned(np.concatenate([w["L1_attn_Wv"], w["L1_attn_Wg"]]).T)
    arrays["L1_attn_bkg2"] = w["L1_attn_bkg2"]
    arrays["L1_attn_bg"] = w["L1_attn_bg"]
    def by_head(a):
        return a.reshape(KD, P, H, P).transpose(2, 1, 0, 3)

    arrays["w_qkv1"] = turned(np.stack([by_head(w["L1_ffn_wq"]), by_head(w["L1_ffn_wk"]), by_head(w["L1_ffn_wv"])],
                                       axis=2).reshape(H, P, 3 * KD * P))
    arrays["w_o1"] = turned(w["L1_ffn_wo"].reshape(H // 2, 2, P, D).transpose(0, 2, 1, 3).reshape(H // 2, P, 2 * D))
    arrays["L1_ffn_ln1_w"], arrays["L1_ffn_ln2_w"] = w["L1_ffn_ln1_w"], w["L1_ffn_ln2_w"]
    arrays["gate_w1"] = turned(w["L1_ffn_gate_w"].T)

    def gate_up(g, u):
        gu = np.concatenate([g, u], axis=-2)
        gu = np.moveaxis(gu, -1, -2).reshape(*gu.shape[:-2], KD, P, gu.shape[-2])
        return np.moveaxis(gu, -2, -3)

    gu = gate_up(w["L1_ffn_eg_w"], w["L1_ffn_eu_w"]).reshape(E1, P, -1)
    dn = w["L1_ffn_ed_w"].transpose(0, 2, 1).reshape(E1, 2, F1 // 2, D)
    dn = np.concatenate([dn, np.zeros((E1, 2, P - F1 // 2, D), dn.dtype)], axis=2)
    dn = dn.transpose(0, 2, 1, 3).reshape(E1, P, 2 * D)
    arrays["w_experts1"] = turned(np.concatenate([gu, dn], axis=2).transpose(1, 0, 2))
    arrays["w_shared_gu1"] = turned(gate_up(w["L1_ffn_sg_w"], w["L1_ffn_su_w"]).reshape(P, -1))
    sd = w["L1_ffn_sd_w"].T
    sd = np.concatenate([sd, np.zeros((3 * P - FS1, D), sd.dtype)]).reshape(3, P, D)
    arrays["w_shared_dn1"] = turned(sd.transpose(1, 0, 2).reshape(P, 3 * D))


def _constants():
    import numpy as np
    bf = mybir.dt.np(BF16)
    start = 2.0 ** (-8.0 / H)
    slopes = np.array([start * start ** i for i in range(H)], dtype=np.float32)
    parts, left = [], slopes.copy()
    for _ in range(3):
        part = left.astype(bf)
        parts.append(part)
        left = left - part.astype(np.float32)
    pos = np.arange(S)
    pos_parts = [(pos // 256 * 256).astype(bf), (pos % 256).astype(bf)]
    q_rows, k_rows = np.zeros((2, H, P - 96, S), bf)
    for i in range(3):
        for j in range(2):
            r = 2 * i + j
            q_rows[:, r, :], k_rows[:, r, :] = parts[i][:, None], pos_parts[j][None, :]
            q_rows[:, 6 + r, :], k_rows[:, 6 + r, :] = pos_parts[j][None, :], -parts[i][:, None]
    route = np.zeros((P, RC_WORDS), np.float32)
    route[:, 0:16] = np.arange(16)
    route[:, 16:24] = P * np.arange(8)
    route[:, 24:24 + N_TILES0] = np.arange(N_TILES0)
    route[:, 40:40 + E0 * TT] = np.arange(E0 * TT) % TT != 0
    route[:, 128:256] = np.arange(P)[:, None] < np.arange(P)[None, :]
    route[:, 256:384] = 1.0
    feature, token = np.arange(P), np.arange(T)
    gla = np.concatenate([feature[:, None] // 8 == np.arange(H)[None, :],
                          feature[:, None] // 8 == np.arange(D)[None, :] // 16,
                          feature[:, None] % CH <= np.arange(CH)[None, :]], axis=1).astype(np.float32)
    k_rows[:, 12:15, :] = 1
    mask = np.where(np.arange(P)[None, :] > np.arange(P)[:, None], -1e30, 0.0).astype(bf)
    return {
        "masktb": np.ascontiguousarray(mask.T),
        "run": (token % CH != 0).astype(np.float32), "gla_consts": gla,
        "route_consts": route,
        "ident": np.eye(P, dtype=np.float32),
        "identb": np.eye(P, dtype=np.float32).astype(bf),
        "maskb": mask,
        "q_bias_rows": q_rows, "k_bias_rows": k_rows,
    }


def kernel(**inputs):
    import numpy as _np
    import concourse.bacc as _bacc
    from concourse import mybir as _mybir
    from concourse.bass_utils import run_bass_kernel_spmd as _run

    w = {k: _np.ascontiguousarray(v) for k, v in inputs.items()}
    arrays = _constants()
    x = w["L0_attn_x"].reshape(T, D)
    arrays["x"] = x
    arrays["xT"] = _np.ascontiguousarray(x.T)
    arrays["bqk0"] = _np.ascontiguousarray(
        _np.stack([w["L0_attn_bq"], w["L0_attn_bk"]]).reshape(2, KD, P).transpose(2, 0, 1))
    for name in ("wq", "wk", "wv", "wo", "bv", "bo"):
        arrays["L0_attn_" + name] = w["L0_attn_" + name]
    lay_out(arrays, w)

    nc = _bacc.Bacc("TRN2", target_bir_lowering=False, num_devices=1)
    io, fed = {}, {}
    for name, a in arrays.items():
        fed[f"in_{name}"] = a
        io[name] = nc.dram_tensor(f"in_{name}", a.shape, _mybir.dt.from_np(a.dtype), kind="ExternalInput").ap()
    out = nc.dram_tensor("out", (T, D), F32, kind="ExternalOutput").ap()
    program(nc, io, out)
    r = _run(nc, [fed], core_ids=[0])
    return r.results[0]["out"].reshape(B, S, D)
```
